# Optimizing a Trainium2 kernel written in Bass

```python
import numpy as np
import jax
import jax.numpy as jnp

def _softmax(x, axis=-1):
    return jax.nn.softmax(x, axis=axis)

def _gelu(x):
    return jax.nn.gelu(x, approximate=True)

def _silu(x):
    return jax.nn.silu(x)

def _sigmoid(x):
    return jax.nn.sigmoid(x)

def _layernorm(x, axis=-1, eps=1e-05):
    m = jnp.mean(x, axis=axis, keepdims=True)
    v = jnp.var(x, axis=axis, keepdims=True)
    return (x - m) / jnp.sqrt(v + eps)

def _scatter_add(tgt, idx, src, axis=0):
    return tgt.at[idx].add(src)

def _segment_sum(src, seg, n):
    return jax.ops.segment_sum(src, seg, n)
kernel_name = 'mk_gps_d1_gnn_r8_805a0c'

def setup_inputs(seed: int=0):
    np.random.seed(seed)
    _w = jnp.asarray

    def _rec_inputs():
        import jax
        import jax.numpy as jnp
        _gk = jax.random.key(seed)
        x = -8.776e-05 + 1 * jax.random.normal(jax.random.fold_in(_gk, 1), (6250, 256), jnp.float32)
        src = jax.random.randint(jax.random.fold_in(_gk, 2), (100000,), 0, 6250, jnp.int32)
        dst = jnp.minimum((6250 * jax.random.uniform(jax.random.fold_in(_gk, 3), (100000,)) ** 2.0).astype(jnp.int32), 49999)
        _o = jnp.argsort(dst, stable=True)
        src = src[_o]
        dst = dst[_o]
        edge_attr_4 = 0.000126197 + 0.999763 * jax.random.normal(jax.random.fold_in(_gk, 11), (100000, 4), jnp.float32)
        edge_attr_8 = jax.random.uniform(jax.random.fold_in(_gk, 12), (100000, 8), jnp.float32, 0.0, 1)
        return (x, src, dst, edge_attr_4, edge_attr_8)
    x, src, dst, edge_attr_4, edge_attr_8 = _rec_inputs()

    def _L0_gnn_setup():
        import jax, jax.numpy as jnp
        import numpy as np
        N_NODES = 2500
        N_EDGES = 40000
        MUL = 64
        NUM_BASIS = 8
        INV_SQRT3 = 0.5773502691896258
        EPS = 1e-05
        key = jax.random.key(seed)
        k = jax.random.split(key, 16)
        return {'node_hiddens': jax.random.normal(k[0], (N_NODES, 4 * MUL), dtype=jnp.float32), 'edge_attr': jax.random.uniform(k[1], (N_EDGES, NUM_BASIS), dtype=jnp.float32), 'edge_sh': jax.random.normal(k[2], (N_EDGES, 4), dtype=jnp.float32), 'w1_s': jax.random.normal(k[3], (MUL, MUL), dtype=jnp.float32), 'w1_v': jax.random.normal(k[4], (MUL, MUL), dtype=jnp.float32), 'wsc_s': jax.random.normal(k[5], (MUL, MUL), dtype=jnp.float32), 'wsc_v': jax.random.normal(k[6], (MUL, MUL), dtype=jnp.float32), 'w2_s': jax.random.normal(k[7], (2 * MUL, MUL), dtype=jnp.float32), 'w2_v': jax.random.normal(k[8], (2 * MUL, MUL), dtype=jnp.float32), 'fc_w1': jax.random.normal(k[9], (NUM_BASIS, 64), dtype=jnp.float32), 'fc_w2': jax.random.normal(k[10], (64, 64), dtype=jnp.float32), 'fc_w3': jax.random.normal(k[11], (64, 4 * MUL), dtype=jnp.float32), 'g_s': jnp.ones((MUL,), dtype=jnp.float32), 'g_v': jnp.ones((MUL,), dtype=jnp.float32), 'edge_index': jax.random.randint(k[12], (2, N_EDGES), 0, N_NODES)}
    _L0_gnn_all = _L0_gnn_setup()
    _L0_gnn_in = {k: v for k, v in _L0_gnn_all.items() if k in ('w1_s', 'w1_v', 'wsc_s', 'wsc_v', 'w2_s', 'w2_v', 'fc_w1', 'fc_w2', 'fc_w3', 'g_s', 'g_v')}
    del _L0_gnn_all

    def _L0_mix_setup():
        import jax, jax.numpy as jnp
        import numpy as np
        NHEAD = 8
        ATT_EPS = 1e-06
        LN_EPS = 1e-05

        def _layernorm(x, g, b):
            mu = jnp.mean(x, axis=-1, keepdims=True)
            var = jnp.mean(jnp.square(x - mu), axis=-1, keepdims=True)
            return (x - mu) * jax.lax.rsqrt(var + LN_EPS) * g + b
        key = jax.random.key(seed)
        ks = jax.random.split(key, 7)
        N, L, C = (4, 2048, 256)
        s = 1.0 / np.sqrt(C)
        return {'x': jax.random.normal(ks[0], (N, L, C), jnp.float32), 'Wq': jax.random.normal(ks[1], (C, C), jnp.float32) * s, 'Wk': jax.random.normal(ks[2], (C, C), jnp.float32) * s, 'Wv': jax.random.normal(ks[3], (C, C), jnp.float32) * s, 'Wm': jax.random.normal(ks[4], (C, C), jnp.float32) * s, 'W1': jax.random.normal(ks[5], (2 * C, 2 * C), jnp.float32) * (1.0 / np.sqrt(2 * C)), 'W2': jax.random.normal(ks[6], (2 * C, C), jnp.float32) * (1.0 / np.sqrt(2 * C)), 'g1': jnp.ones((C,), jnp.float32), 'b1': jnp.zeros((C,), jnp.float32), 'g2': jnp.ones((C,), jnp.float32), 'b2': jnp.zeros((C,), jnp.float32)}
    _L0_mix_all = _L0_mix_setup()
    _L0_mix_in = {k: v for k, v in _L0_mix_all.items() if k in ('Wq', 'Wk', 'Wv', 'Wm', 'W1', 'W2', 'g1', 'b1', 'g2', 'b2')}
    del _L0_mix_all

    def _L0_ffn_setup():
        import math
        import jax, jax.numpy as jnp
        import numpy as np
        CAPACITY_FACTOR = 1.25
        key = jax.random.key(seed)
        ks = jax.random.split(key, 5)
        B, L, D, F, E = (8, 1024, 256, 1024, 8)
        h = jax.random.normal(ks[0], (B, L, D), dtype=jnp.float32)
        gate_w = jax.random.normal(ks[1], (D, E), dtype=jnp.float32) * 0.02
        gate_b = jnp.zeros((E,), dtype=jnp.float32)
        w1 = jax.random.normal(ks[2], (E, D, F), dtype=jnp.float32) * (1.0 / math.sqrt(D))
        b1 = jnp.zeros((E, F), dtype=jnp.float32)
        w2 = jax.random.normal(ks[3], (E, F, D), dtype=jnp.float32) * (1.0 / math.sqrt(F))
        b2 = jnp.zeros((E, D), dtype=jnp.float32)
        return {'h': h, 'gate_w': gate_w, 'gate_b': gate_b, 'w1': w1, 'b1': b1, 'w2': w2, 'b2': b2}
    _L0_ffn_all = _L0_ffn_setup()
    _L0_ffn_in = {k: v for k, v in _L0_ffn_all.items() if k in ('gate_w', 'gate_b', 'w1', 'b1', 'w2', 'b2')}
    del _L0_ffn_all
    return {'x': x, 'src': src, 'dst': dst, 'edge_attr_4': edge_attr_4, 'edge_attr_8': edge_attr_8, 'L0_gnn_w1_s': _L0_gnn_in['w1_s'], 'L0_gnn_w1_v': _L0_gnn_in['w1_v'], 'L0_gnn_wsc_s': _L0_gnn_in['wsc_s'], 'L0_gnn_wsc_v': _L0_gnn_in['wsc_v'], 'L0_gnn_w2_s': _L0_gnn_in['w2_s'], 'L0_gnn_w2_v': _L0_gnn_in['w2_v'], 'L0_gnn_fc_w1': _L0_gnn_in['fc_w1'], 'L0_gnn_fc_w2': _L0_gnn_in['fc_w2'], 'L0_gnn_fc_w3': _L0_gnn_in['fc_w3'], 'L0_gnn_g_s': _L0_gnn_in['g_s'], 'L0_gnn_g_v': _L0_gnn_in['g_v'], 'L0_mix_Wq': _L0_mix_in['Wq'], 'L0_mix_Wk': _L0_mix_in['Wk'], 'L0_mix_Wv': _L0_mix_in['Wv'], 'L0_mix_Wm': _L0_mix_in['Wm'], 'L0_mix_W1': _L0_mix_in['W1'], 'L0_mix_W2': _L0_mix_in['W2'], 'L0_mix_g1': _L0_mix_in['g1'], 'L0_mix_b1': _L0_mix_in['b1'], 'L0_mix_g2': _L0_mix_in['g2'], 'L0_mix_b2': _L0_mix_in['b2'], 'L0_ffn_gate_w': _L0_ffn_in['gate_w'], 'L0_ffn_gate_b': _L0_ffn_in['gate_b'], 'L0_ffn_w1': _L0_ffn_in['w1'], 'L0_ffn_b1': _L0_ffn_in['b1'], 'L0_ffn_w2': _L0_ffn_in['w2'], 'L0_ffn_b2': _L0_ffn_in['b2']}

def reference(x, src, dst, edge_attr_4, edge_attr_8, L0_gnn_w1_s, L0_gnn_w1_v, L0_gnn_wsc_s, L0_gnn_wsc_v, L0_gnn_w2_s, L0_gnn_w2_v, L0_gnn_fc_w1, L0_gnn_fc_w2, L0_gnn_fc_w3, L0_gnn_g_s, L0_gnn_g_v, L0_mix_Wq, L0_mix_Wk, L0_mix_Wv, L0_mix_Wm, L0_mix_W1, L0_mix_W2, L0_mix_g1, L0_mix_b1, L0_mix_g2, L0_mix_b2, L0_ffn_gate_w, L0_ffn_gate_b, L0_ffn_w1, L0_ffn_b1, L0_ffn_w2, L0_ffn_b2):
    import jax
    import jax.numpy as jnp

    def _L0_gnn_ref(node_hiddens, edge_attr, edge_sh, w1_s, w1_v, wsc_s, wsc_v, w2_s, w2_v, fc_w1, fc_w2, fc_w3, g_s, g_v, edge_index):
        import jax, jax.numpy as jnp
        import numpy as np
        N_NODES = 2500
        N_EDGES = 40000
        MUL = 64
        NUM_BASIS = 8
        INV_SQRT3 = 0.5773502691896258
        EPS = 1e-05
        N = node_hiddens.shape[0]
        xs = node_hiddens[:, :MUL]
        xv = node_hiddens[:, MUL:].reshape(N, MUL, 3)
        h = jax.nn.silu(edge_attr @ fc_w1 * (1.0 / np.sqrt(float(NUM_BASIS))))
        h = jax.nn.silu(h @ fc_w2 * (1.0 / np.sqrt(64.0)))
        w = h @ fc_w3 * (1.0 / np.sqrt(64.0))
        wA, wB, wC, wD = jnp.split(w, 4, axis=1)
        inv = 1.0 / np.sqrt(float(MUL))
        sc_s = xs @ wsc_s * inv
        sc_v = jnp.einsum('nud,uv->nvd', xv, wsc_v) * inv
        ys = xs @ w1_s * inv
        yv = jnp.einsum('nud,uv->nvd', xv, w1_v) * inv
        src = edge_index[0]
        dst = edge_index[1]
        es = ys[dst]
        ev = yv[dst]
        sh0 = edge_sh[:, :1]
        sh1 = edge_sh[:, 1:]
        m0a = wA * es * sh0
        m0b = wD * jnp.einsum('eud,ed->eu', ev, sh1) * INV_SQRT3
        m1a = wB[:, :, None] * es[:, :, None] * sh1[:, None, :]
        m1b = wC[:, :, None] * ev * sh0[:, :, None]
        mid_s = jnp.concatenate([m0a, m0b], axis=1)
        mid_v = jnp.concatenate([m1a, m1b], axis=1)
        ns = jax.ops.segment_sum(mid_s, src, num_segments=N)
        nv = jax.ops.segment_sum(mid_v, src, num_segments=N)
        deg = jax.ops.segment_sum(jnp.ones((src.shape[0],), node_hiddens.dtype), src, num_segments=N)
        dn = jax.lax.rsqrt(jnp.maximum(deg, 1.0))
        ns = ns * dn[:, None]
        nv = nv * dn[:, None, None]
        inv2 = 1.0 / np.sqrt(2.0 * MUL)
        os_ = ns @ w2_s * inv2 + sc_s
        ov = jnp.einsum('nud,uv->nvd', nv, w2_v) * inv2 + sc_v
        os_ = os_ * jax.lax.rsqrt(jnp.mean(os_ * os_, axis=1, keepdims=True) + EPS) * g_s
        rms_v = jax.lax.rsqrt(jnp.mean(ov * ov, axis=(1, 2))[:, None, None] + EPS)
        ov = ov * rms_v * g_v[None, :, None]
        return jnp.concatenate([os_, ov.reshape(N, 3 * MUL)], axis=1)

    def _L0_mix_ref(x, Wq, Wk, Wv, Wm, W1, W2, g1, b1, g2, b2):
        import jax, jax.numpy as jnp
        import numpy as np
        NHEAD = 8
        ATT_EPS = 1e-06
        LN_EPS = 1e-05

        def _layernorm(x, g, b):
            mu = jnp.mean(x, axis=-1, keepdims=True)
            var = jnp.mean(jnp.square(x - mu), axis=-1, keepdims=True)
            return (x - mu) * jax.lax.rsqrt(var + LN_EPS) * g + b
        N, L, C = x.shape
        H = NHEAD
        D = C // H
        q = (x @ Wq).reshape(N, L, H, D)
        k = (x @ Wk).reshape(N, L, H, D)
        v = (x @ Wv).reshape(N, L, H, D)
        Q = jax.nn.elu(q) + 1.0
        K = jax.nn.elu(k) + 1.0
        v = v / L
        KV = jnp.einsum('nshd,nshv->nhdv', K, v)
        Z = 1.0 / (jnp.einsum('nlhd,nhd->nlh', Q, K.sum(axis=1)) + ATT_EPS)
        msg = jnp.einsum('nlhd,nhdv,nlh->nlhv', Q, KV, Z) * L
        msg = msg.reshape(N, L, C) @ Wm
        msg = _layernorm(msg, g1, b1)
        h = jnp.concatenate([x, msg], axis=-1) @ W1
        h = jax.nn.relu(h) @ W2
        msg = _layernorm(h, g2, b2)
        return x + msg

    def _L0_ffn_ref(h, gate_w, gate_b, w1, b1, w2, b2):
        import math
        import jax, jax.numpy as jnp
        import numpy as np
        CAPACITY_FACTOR = 1.25
        B, L, D = h.shape
        E = gate_w.shape[1]
        T = B * L
        C = max(1, math.ceil(CAPACITY_FACTOR * T / E))
        x = h.reshape(T, D)
        logits = x @ gate_w + gate_b
        probs = jax.nn.softmax(logits, axis=-1)
        idx = jnp.argmax(probs, axis=-1)
        prb = jnp.take_along_axis(probs, idx[:, None], axis=1)[:, 0]
        one_hot = jax.nn.one_hot(idx, E, dtype=jnp.float32)
        pos = (jnp.cumsum(one_hot, axis=0) * one_hot).sum(-1).astype(jnp.int32) - 1
        kept = pos < C
        pos_safe = jnp.where(kept, pos, C)
        buf = jnp.zeros((E, C, D), dtype=h.dtype).at[idx, pos_safe].set(x, mode='drop')
        hmid = jax.nn.relu(jnp.einsum('ecd,edf->ecf', buf, w1) + b1[:, None, :])
        ybuf = jnp.einsum('ecf,efd->ecd', hmid, w2) + b2[:, None, :]
        pos_g = jnp.minimum(pos, C - 1)
        y_tok = ybuf[idx, pos_g] * (prb * kept)[:, None]
        y = y_tok.reshape(B, L, D)
        y = jnp.nan_to_num(y, nan=0.0, posinf=10000.0, neginf=-10000.0)
        return y
    edge_index = jnp.stack([src, dst])
    xn = _layernorm(x, axis=-1)
    x = x + _L0_gnn_ref(xn, edge_attr_8, edge_attr_4, L0_gnn_w1_s, L0_gnn_w1_v, L0_gnn_wsc_s, L0_gnn_wsc_v, L0_gnn_w2_s, L0_gnn_w2_v, L0_gnn_fc_w1, L0_gnn_fc_w2, L0_gnn_fc_w3, L0_gnn_g_s, L0_gnn_g_v, edge_index) + _L0_mix_ref(xn[None], L0_mix_Wq, L0_mix_Wk, L0_mix_Wv, L0_mix_Wm, L0_mix_W1, L0_mix_W2, L0_mix_g1, L0_mix_b1, L0_mix_g2, L0_mix_b2)[0]
    x = x + _L0_ffn_ref(_layernorm(x, axis=-1)[None], L0_ffn_gate_w, L0_ffn_gate_b, L0_ffn_w1, L0_ffn_b1, L0_ffn_w2, L0_ffn_b2)[0]
    return x

_drawn_inputs = setup_inputs


def setup_inputs(seed=0):
    import zlib

    import numpy as np

    out = dict(_drawn_inputs(seed))
    spreads = {'L0_gnn_g_s': (1.0, 0.2),
     'L0_gnn_g_v': (1.0, 0.2),
     'L0_mix_g1': (1.0, 0.2),
     'L0_mix_b1': (0.0, 0.277),
     'L0_mix_g2': (1.0, 0.2),
     'L0_mix_b2': (0.0, 0.1),
     'L0_ffn_gate_b': (0.0, 0.1),
     'L0_ffn_b1': (0.0, 0.8),
     'L0_ffn_b2': (0.0, 0.8)}
    factors = {}
    for name, (base, spread) in spreads.items():
        noise = np.random.default_rng([zlib.crc32(name.encode()), seed]).standard_normal(out[name].shape)
        drawn = base * np.exp(spread * noise) if base else spread * noise
        out[name] = jnp.asarray(drawn.astype(out[name].dtype))
    for name, factor in factors.items():
        out[name] = (out[name] * factor).astype(out[name].dtype)
    return out
```

```python
from contextlib import ExitStack

import concourse.bass as bass
from concourse import mybir

F32 = mybir.dt.float32
I32 = mybir.dt.int32
U32 = mybir.dt.uint32
ALU = mybir.AluOpType
ACT = mybir.ActivationFunctionType
AX = mybir.AxisListType.X

P = 128
MUL = 64
HEADS = 8
LN_EPS = 1e-5
ATT_EPS = 1e-6
LEAD = 2
G = 16
YSLOTS = 8
OSLOTS = 4
TABLES = 2
CNT = 8 * MUL


class Signal:

    def __init__(self, sem, unit=1, lead=0):
        self.sem, self.unit, self.lead = sem, unit, lead

    def credit(self, eng):
        eng.sem_inc(self.sem, self.lead * self.unit)

    def of(self, n):
        return (n + (self.lead + 1)) * self.unit


def wait(eng, signal, n):
    eng.wait_ge(signal.sem, signal.of(n))


class Kernel:
    pass


def program(nc, t, out):
    N, D = t["x"].shape
    E = t["src"].shape[0]
    NT = (N + P - 1) // P
    LAST = N - (NT - 1) * P
    NPAD = NT * P
    NB = (E + P * G - 1) // (P * G)
    ELAST = (E - (NB - 1) * P * G) // G
    assert NT == NB and NT % 2 == 1 and ELAST * G == E - (NB - 1) * P * G

    with ExitStack() as ctx:
        k = Kernel()
        k.used = []
        k.nc, k.t, k.out, k.ctx = nc, t, out, ctx
        k.N, k.D, k.E, k.NT, k.LAST, k.NPAD, k.NB, k.ELAST = N, D, E, NT, LAST, NPAD, NB, ELAST
        k.NEXP = t["L0_ffn_gate_w"].shape[1]
        k.FF = t["L0_ffn_w1"].shape[2]
        k.CAP = max(1, -(-5 * N // (4 * k.NEXP)))
        k.acc = ctx.enter_context(nc.sbuf_tensor("acc", [P, NT, D], F32))
        k.ident = ctx.enter_context(nc.sbuf_tensor("ident", [P, P], F32))
        k.ones = ctx.enter_context(nc.sbuf_tensor("ones", [P, P], F32))
        k.weight = ctx.enter_context(nc.sbuf_tensor("weight", [P, NT], F32))
        k.back = ctx.enter_context(nc.sbuf_tensor("back", [P, NT], F32))
        k.ytab = dram(k, "ytab", [NPAD, D], F32)
        k.sctab = dram(k, "sctab", [NPAD, D], F32)
        k.qtab = dram(k, "qtab", [NT, P, D], F32)
        k.tables = [dram(k, f"table{j}", [N + P, CNT + 1], F32) for j in range(TABLES)]
        k.srcp = dram(k, "srcp", [NB, P, G], I32)
        k.dstp = dram(k, "dstp", [NB, P, G], I32)
        k.shp = dram(k, "shp", [NB, P, G * 4], F32)
        k.attrp = dram(k, "attrp", [NB, P, G * 8], F32)
        k.buf = dram(k, "buf", [k.NEXP * k.CAP + NPAD, D], F32)
        k.ybuf = dram(k, "ybuf", [k.NEXP * k.CAP, D], F32)
        with ExitStack() as mix:
            k.xnT = mix.enter_context(nc.sbuf_tensor("xnT", [P, 2, NPAD], F32))
            k.KV = mix.enter_context(nc.sbuf_tensor("KV", [P, 2, P], F32))
            k.KS = mix.enter_context(nc.sbuf_tensor("KS", [P, 2, P], F32))
            constants(k)
            stage_nodes(k)
            stage_edges(k)
        stage_gnn(k)
        stage_route(k)
        stage_experts(k)
        stage_combine(k)


def new_sem(k, c, name):
    k.used.append(c.enter_context(k.nc.semaphore(name)))
    return k.used[-1]


def clear_semaphores(k):
    with k.nc.Block() as block:
        @block.gpsimd
        def _(pool):
            for s in k.used:
                pool.sem_clear(s)
    k.used = []


def dram(k, name, shape, dt):
    return k.nc.dram_tensor(name, shape, dt).ap()


def permuted_rows(w):
    for d in range(3):
        yield (d + 1) // 2, MUL * ((d + 1) % 2), w[MUL + d::3]
    yield 0, 0, w[0:MUL]


def vectors_first(row):
    return row[..., MUL:].rearrange("... (u d) -> ... d u", d=3)


def constants(k):
    nc = k.nc
    with ExitStack() as c:
        zeroed = new_sem(k, c, "c_zeroed")
        with nc.Block() as block:
            @block.gpsimd
            def _(pool):
                nc.gpsimd.memset(k.ident[:, :], 0.0)
                nc.gpsimd.memset(k.ones[:, :], 1.0).then_inc(zeroed, 1)
                pool.wait_ge(zeroed, 1)
                nc.gpsimd.affine_select(out=k.ident[:, :], in_=k.ident[:, :], compare_op=ALU.not_equal, fill=1.0,
                                        base=0, pattern=[[-1, P]], channel_multiplier=1)


def stage_nodes(k):
    nc, t, NT, D, N, LAST, NPAD = k.nc, k.t, k.NT, k.D, k.N, k.LAST, k.NPAD
    NB, ELAST = k.NB, k.ELAST
    acc, xnT, ident = k.acc, k.xnT, k.ident
    ZR = N + P
    with ExitStack() as c:
        def sb(name, shape, dt=F32):
            return c.enter_context(nc.sbuf_tensor("n_" + name, shape, dt))

        def bank(name):
            return c.enter_context(nc.psum_tensor("n_" + name, [P, 512], F32))

        def sem(name):
            return new_sem(k, c, "n_" + name)

        stats, mv, mean = sb("stats", [P, NT, 6]), sb("mv", [P, NT, 4]), sb("mean", [P, NT])
        rstd, shift, grow, half = sb("rstd", [P, NT]), sb("shift", [P, NT]), sb("grow", [P, NT]), sb("half", [P, NT])
        vare = sb("vare", [P, NT])
        xp, xt = sb("xp", [P, 2, D]), sb("xt", [P, 2, 2, P])
        wq, wk, wv = sb("wq", [P, 2, D]), sb("wk", [P, 2, D]), sb("wv", [P, 2, D])
        wg = sb("wg", [P, 2, 2, P])
        low, exps = sb("low", [P, 2, D]), sb("exps", [P, 2, D])
        qlow, qexps, qf = sb("qlow", [P, 2, D]), sb("qexps", [P, 2, D]), sb("qf", [P, 2, D])
        kf, vf = sb("kf", [P, 2, D]), sb("vf", [P, 2, 2, P + 1])
        ysc = sb("ysc", [P, 2, 2, D])
        mask = sb("mask", [P, P])
        zer = sb("zer", [P, 2048])
        padsrc, padzero = sb("padsrc", [P, G], I32), sb("padzero", [P, G], I32)
        pT = [bank("pT0"), bank("pT1")]
        pK, pV, pQ, pY, pKV = bank("pK"), bank("pV"), bank("pQ"), bank("pY"), bank("pKV")

        x_in, w_in, w1_in, laid = sem("x_in"), sem("w_in"), sem("w1_in"), sem("laid")
        memsets, x_zeroed, powered, statd, meant = (sem(s) for s in (
            "memsets", "x_zeroed", "powered", "statd", "meant"))
        xp_ready = Signal(sem("xp_ready"), lead=LEAD)
        xT_done = Signal(sem("xT_done"), lead=LEAD)
        xt_ready = Signal(sem("xt_ready"), lead=LEAD)
        xt_kept = Signal(sem("xt_kept"), lead=LEAD)
        prod_k = Signal(sem("prod_k"), lead=LEAD)
        prod_v = Signal(sem("prod_v"), lead=LEAD)
        prod_q = Signal(sem("prod_q"), lead=LEAD)
        prod_y = Signal(sem("prod_y"), lead=LEAD)
        k_low, k_exp, k_feat = (Signal(sem(s), lead=LEAD) for s in ("k_low", "k_exp", "k_feat"))
        q_low, q_exp, q_feat = (Signal(sem(s), lead=LEAD) for s in ("q_low", "q_exp", "q_feat"))
        v_copied = Signal(sem("v_copied"), lead=LEAD)
        y_copied = Signal(sem("y_copied"), lead=LEAD)
        grown = Signal(sem("grown"), lead=LEAD)
        kv_added = Signal(sem("kv_added"), lead=LEAD)
        stores, stored = Signal(sem("stores"), 48), Signal(sem("stored"), lead=LEAD)
        masked, ln_ready = sem("masked"), sem("ln_ready")

        def tiles(eng, tile):
            with eng.Fori(0, NT // 2) as i:
                for j in range(2):
                    tile(i * 2 + j, j)
            tile(NT - 1, 0)

        edges = []
        whole = (NB - 1) * P * G
        for name, to, w in (("src", k.srcp, 1), ("dst", k.dstp, 1), ("edge_attr_4", k.shp, 4), ("edge_attr_8", k.attrp, 8)):
            src = t[name]
            flat = src[0:whole] if w == 1 else src[0:whole, :]
            rest = src[whole:k.E] if w == 1 else src[whole:k.E, :]
            pat = "(b p g) -> (b p) g" if w == 1 else "(b p g) f -> (b p) (g f)"
            edges.append((to[0:NB - 1].rearrange("b p f -> (b p) f"), flat.rearrange(pat, p=P, g=G)))
            pat = "(p g) -> p g" if w == 1 else "(p g) f -> p (g f)"
            edges.append((to[NB - 1, 0:ELAST, :], rest.rearrange(pat, g=G)))
        fills = []
        for tab in k.tables:
            flat = tab.rearrange("r c -> (r c)")
            total = ZR * (CNT + 1)
            chunk = P * 2048
            at = 0
            while at < total:
                n = min(chunk, total - at)
                w = n // P
                fills.append((flat[at:at + w * P].rearrange("(p w) -> p w", p=P), zer[:, 0:w]))
                at += w * P
                if n - w * P:
                    r = n - w * P
                    fills.append((flat[at:at + r].rearrange("(p w) -> p w", p=1), zer[0:1, 0:r]))
                    at += r
        rows = k.NEXP * k.CAP
        bflat = k.buf[0:rows - rows % 8].rearrange("(n r) d -> n (r d)", r=8)
        at = 0
        while at < bflat.shape[0]:
            n = min(P, bflat.shape[0] - at)
            fills.append((bflat[at:at + n], zer[0:n, :]))
            at += n
        if rows % 8:
            fills.append((k.buf[rows - rows % 8:rows], zer[0:rows % 8, 0:D]))
        LAID = len(edges) + len(fills) + 4

        with nc.Block() as block:
            @block.sync
            def _(sp):
                sp.wait_ge(x_zeroed, 1)
                xv = t["x"][0:(NT - 1) * P].rearrange("(t p) d -> p t d", p=P)
                sp.dma_start(acc[:, 0:NT - 1, :], xv).then_inc(x_in, 16)
                sp.dma_start(acc[0:LAST, NT - 1, :], t["x"][(NT - 1) * P:N]).then_inc(x_in, 16)
                for w, to in ((t["L0_mix_Wq"], wq), (t["L0_mix_Wk"], wk), (t["L0_mix_Wv"], wv)):
                    for chunk, p0, rows in permuted_rows(w):
                        sp.dma_start(to[p0:p0 + MUL, chunk, :], rows).then_inc(w_in, 16)
                sp.wait_ge(memsets, 1)
                for m, (s, v) in enumerate(((t["L0_gnn_w1_s"], t["L0_gnn_w1_v"]), (t["L0_gnn_wsc_s"], t["L0_gnn_wsc_v"]))):
                    for chunk in range(2):
                        for h in range(2):
                            w = s if (chunk, h) == (0, 0) else v
                            sp.dma_start(wg[h * MUL:(h + 1) * MUL, chunk, m, h * MUL:(h + 1) * MUL], w).then_inc(w1_in, 16)

                def tile(n, j):
                    wait(sp, y_copied, n)
                    rows = bass.ds(n * P, P)
                    sp.dma_start(k.ytab[rows, :], ysc[:, j, 0, :]).then_inc(stores.sem, 16)
                    sp.dma_start(k.sctab[rows, :], ysc[:, j, 1, :]).then_inc(stores.sem, 16)
                    wait(sp, q_feat, n)
                    sp.dma_start(k.qtab[bass.ds(n, 1), :, :].rearrange("a p d -> p (a d)"), qf[:, j, :]).then_inc(stores.sem, 16)
                    sp.wait_ge(stores.sem, stores.of(n))
                    sp.sem_inc(stored.sem, 1)
                stored.credit(sp)
                tiles(sp, tile)
                sp.wait_ge(laid, 16 * LAID)

            @block.gpsimd
            def _(pool):
                nc.gpsimd.memset(acc[:, NT - 1, :], 0.0).then_inc(x_zeroed, 1)
                nc.gpsimd.memset(half[:, :], -0.5)
                nc.gpsimd.memset(wg[:, :, :, :], 0.0).then_inc(memsets, 1)
                nc.gpsimd.memset(vf[:, :, :, P:P + 1], 1.0)
                nc.gpsimd.memset(padzero[:, :], 0)
                nc.gpsimd.memset(zer[:, :], 0.0)
                nc.gpsimd.iota(padsrc[:, :], pattern=[[0, G]], base=N, channel_multiplier=1).then_inc(memsets, 1)
                pool.wait_ge(memsets, 2)
                for to, of in edges + fills:
                    pool.dma_start(to, of).then_inc(laid, 16)
                tail = P - ELAST
                pool.dma_start(k.srcp[NB - 1, ELAST:P, :], padsrc[ELAST:P, :]).then_inc(laid, 16)
                pool.dma_start(k.dstp[NB - 1, ELAST:P, :], padzero[ELAST:P, :]).then_inc(laid, 16)
                pool.dma_start(k.shp[NB - 1, ELAST:P, :], zer[ELAST:P, 0:G * 4]).then_inc(laid, 16)
                pool.dma_start(k.attrp[NB - 1, ELAST:P, :], zer[ELAST:P, 0:G * 8]).then_inc(laid, 16)
                pool.wait_ge(meant, 3)
                nc.gpsimd.tensor_tensor(rstd[:, :], vare[:, :], half[:, :], ALU.pow).then_inc(powered, 1)

            @block.vector
            def _(dve):
                for s in (xt_ready, k_low, k_feat, q_low, q_feat, grown):
                    s.credit(dve)
                nc.vector.memset(mask[:, :], 0.0).then_inc(masked, 1)
                dve.wait_ge(masked, 1)
                for h in range(4):
                    m = nc.vector.memset(mask[32 * h:32 * h + 32, 32 * h:32 * h + 32], 1.0)
                m.then_inc(masked, 1)
                dve.wait_ge(x_in, 32)
                with dve.Fori(0, NT) as i:
                    nc.vector.bn_stats(stats[:, bass.ds(i, 1), :].rearrange("p a d -> p (a d)"),
                                       acc[:, bass.ds(i, 1), :].rearrange("p a d -> p (a d)")).then_inc(statd, 1)
                dve.wait_ge(statd, NT)
                nc.vector.tensor_tensor(mv[:, :, 0], stats[:, :, 1], stats[:, :, 4], ALU.add)
                nc.vector.tensor_tensor(mv[:, :, 1], stats[:, :, 1], stats[:, :, 4], ALU.subtract)
                nc.vector.tensor_tensor(vare[:, :], stats[:, :, 2], stats[:, :, 5], ALU.add).then_inc(meant, 1)
                dve.wait_ge(meant, 1)
                nc.vector.tensor_scalar(mean[:, :], mv[:, :, 0], 0.5, None, ALU.mult)
                nc.vector.tensor_tensor(mv[:, :, 2], mv[:, :, 1], mv[:, :, 1], ALU.mult)
                nc.vector.tensor_scalar(mv[:, :, 3], vare[:, :], 1.0 / D, LN_EPS, ALU.mult, ALU.add).then_inc(meant, 1)
                dve.wait_ge(meant, 2)
                nc.vector.scalar_tensor_tensor(out=vare[:, :], in0=mv[:, :, 2], scalar=0.25, in1=mv[:, :, 3],
                                               op0=ALU.mult, op1=ALU.add).then_inc(meant, 1)
                dve.wait_ge(powered, 1)
                nc.vector.scalar_tensor_tensor(out=shift[:, :], in0=mean[:, :], scalar=-1.0, in1=rstd[:, :],
                                               op0=ALU.mult, op1=ALU.mult)
                nc.vector.tensor_scalar_add(grow[:, :], rstd[:, :], 1.0).then_inc(ln_ready, 1)
                dve.wait_ge(ln_ready, 1)

                def tile(n, j):
                    wait(dve, xT_done, n)
                    dve.wait_ge(prod_y.sem, prod_y.of(n - 2))
                    dve.wait_ge(xt_kept.sem, xt_kept.of(n - 2))
                    nc.vector.tensor_copy(xt[:, j, :, :], pT[j][:, 0:2 * P]).then_inc(xt_ready.sem, 1)
                    wait(dve, xp_ready, n)
                    a = acc[:, bass.ds(n, 1), :].rearrange("p a d -> p (a d)")
                    nc.vector.tensor_scalar(a, a, grow[:, bass.ds(n, 1)], shift[:, bass.ds(n, 1)], ALU.mult, ALU.add).then_inc(grown.sem, 1)
                    wait(dve, prod_k, n)
                    dve.wait_ge(k_exp.sem, k_exp.of(n - 2))
                    nc.vector.tensor_scalar_min(low[:, j, :], pK[:, 0:D], 0.0).then_inc(k_low.sem, 1)
                    wait(dve, prod_q, n)
                    dve.wait_ge(q_exp.sem, q_exp.of(n - 2))
                    nc.vector.tensor_scalar_min(qlow[:, j, :], pQ[:, 0:D], 0.0).then_inc(q_low.sem, 1)
                    wait(dve, k_exp, n)
                    dve.wait_ge(kv_added.sem, kv_added.of(n - 2))
                    nc.vector.scalar_tensor_tensor(out=kf[:, j, :], in0=pK[:, 0:D], scalar=0.0, in1=exps[:, j, :],
                                                   op0=ALU.max, op1=ALU.add).then_inc(k_feat.sem, 1)
                    wait(dve, q_exp, n)
                    dve.wait_ge(stored.sem, stored.of(n - 2))
                    nc.vector.scalar_tensor_tensor(out=qf[:, j, :], in0=pQ[:, 0:D], scalar=0.0, in1=qexps[:, j, :],
                                                   op0=ALU.max, op1=ALU.add).then_inc(q_feat.sem, 1)
                tiles(dve, tile)
                wait(dve, kv_added, NT - 1)
                dve.wait_ge(masked, 2)
                for ch in range(2):
                    nc.vector.tensor_tensor(k.KV[:, ch, :], pKV[:, ch * (P + 1):ch * (P + 1) + P], mask[:, :], ALU.mult)
                    nc.vector.tensor_scalar(k.KS[:, ch, :], mask[:, :], pKV[:, ch * (P + 1) + P:(ch + 1) * (P + 1)], None, ALU.mult)

            @block.scalar
            def _(act):
                for s in (xp_ready, xt_kept, k_exp, q_exp, v_copied, y_copied):
                    s.credit(act)
                act.wait_ge(ln_ready, 1)

                def norm(n, j):
                    act.wait_ge(xT_done.sem, xT_done.of(n - 2))
                    a = acc[:, bass.ds(n, 1), :].rearrange("p a d -> p (a d)")
                    scale, bias = rstd[:, bass.ds(n, 1)], shift[:, bass.ds(n, 1)]
                    nc.scalar.activation(xp[:, j, 0:MUL], a[:, 0:MUL], ACT.Identity, scale=scale, bias=bias)
                    nc.scalar.activation(xp[:, j, MUL:D].rearrange("p (d u) -> p d u", d=3),
                                         a[:, MUL:D].rearrange("p (u d) -> p d u", d=3),
                                         ACT.Identity, scale=scale, bias=bias).then_inc(xp_ready.sem, 1)

                def rest(n, j):
                    wait(act, xt_ready, n)
                    nc.scalar.copy(xnT[:, :, bass.ds(n * P, P)], xt[:, j, :, :]).then_inc(xt_kept.sem, 1)
                    wait(act, k_low, n)
                    act.wait_ge(k_feat.sem, k_feat.of(n - 2))
                    nc.scalar.activation(exps[:, j, :], low[:, j, :], ACT.Exp).then_inc(k_exp.sem, 1)
                    wait(act, prod_v, n)
                    act.wait_ge(kv_added.sem, kv_added.of(n - 2))
                    nc.scalar.copy(vf[:, j, :, 0:P], pV[:, 0:D].rearrange("p (c v) -> p c v", c=2)).then_inc(v_copied.sem, 1)
                    wait(act, q_low, n)
                    act.wait_ge(q_feat.sem, q_feat.of(n - 2))
                    nc.scalar.activation(qexps[:, j, :], qlow[:, j, :], ACT.Exp).then_inc(q_exp.sem, 1)
                    wait(act, prod_y, n)
                    act.wait_ge(stored.sem, stored.of(n - 2))
                    nc.scalar.activation(ysc[:, j, :, :].rearrange("p m (c v) -> p c m v", c=2),
                                         pY[:, :].rearrange("p (c m v) -> p c m v", c=2, m=2), ACT.Copy, scale=MUL ** -0.5).then_inc(y_copied.sem, 1)
                with act.Fori(0, NT // 2) as i:
                    for j in range(2):
                        norm(i * 2 + j, j)
                    for j in range(2):
                        rest(i * 2 + j, j)
                norm(NT - 1, 0)
                rest(NT - 1, 0)

            @block.tensor
            def _(pe):
                for s in (xT_done, prod_k, prod_v, prod_q, prod_y, kv_added):
                    s.credit(pe)
                pe.wait_ge(memsets, 1)
                pe.wait_ge(w_in, 16 * 12)
                pe.wait_ge(w1_in, 16 * 8)
                pe.wait_ge(memsets, 2)
                nc.tensor.matmul(pKV[:, 0:2 * (P + 1)], zer[:, 0:P], zer[:, 0:2 * (P + 1)], start=True, stop=True)

                def transpose(n, j):
                    wait(pe, xp_ready, n)
                    pe.wait_ge(xt_ready.sem, xt_ready.of(n - 2))
                    for ch in range(2):
                        m = nc.tensor.transpose(pT[j][:, ch * P:(ch + 1) * P], xp[:, j, ch * P:(ch + 1) * P], ident[:, :])
                    m.then_inc(xT_done.sem, 1)

                def products(n, j):
                    wait(pe, xt_ready, n)
                    pe.wait_ge(k_feat.sem, k_feat.of(n - 1))
                    for ch in range(2):
                        m = nc.tensor.matmul(pK[:, 0:D], xt[:, j, ch, :], wk[:, ch, :], start=ch == 0, stop=ch == 1)
                    m.then_inc(prod_k.sem, 1)
                    pe.wait_ge(q_feat.sem, q_feat.of(n - 1))
                    for m_ in range(2):
                        for ch in range(2):
                            m = nc.tensor.matmul(pQ[:, m_ * P:(m_ + 1) * P], wq[:, ch, m_ * P:(m_ + 1) * P], xt[:, j, ch, :],
                                                 start=ch == 0, stop=ch == 1)
                    m.then_inc(prod_q.sem, 1)
                    pe.wait_ge(v_copied.sem, v_copied.of(n - 1))
                    for ch in range(2):
                        m = nc.tensor.matmul(pV[:, 0:D], xt[:, j, ch, :], wv[:, ch, :], start=ch == 0, stop=ch == 1)
                    m.then_inc(prod_v.sem, 1)
                    pe.wait_ge(y_copied.sem, y_copied.of(n - 1))
                    for ch in range(2):
                        m = nc.tensor.matmul(pY[:, ch * D:(ch + 1) * D], xt[:, j, ch, :],
                                             wg[:, ch, :, :].rearrange("p m v -> p (m v)"), start=True, stop=True)
                    m.then_inc(prod_y.sem, 1)

                def add_kv(n, j, rows):
                    wait(pe, k_feat, n)
                    wait(pe, v_copied, n)
                    for ch in range(2):
                        m = nc.tensor.matmul(pKV[:, ch * (P + 1):(ch + 1) * (P + 1)], kf[0:rows, j, ch * P:(ch + 1) * P],
                                             vf[0:rows, j, ch, :], start=False, stop=True, skip_group_check=True)
                    m.then_inc(kv_added.sem, 1)
                with pe.Fori(0, NT // 2) as i:
                    for j in range(2):
                        transpose(i * 2 + j, j)
                    for j in range(2):
                        products(i * 2 + j, j)
                    for j in range(2):
                        add_kv(i * 2 + j, j, P)
                transpose(NT - 1, 0)
                products(NT - 1, 0)
                add_kv(NT - 1, 0, LAST)
        clear_semaphores(k)


def stage_edges(k):
    nc, t, NB, N, D = k.nc, k.t, k.NB, k.N, k.D
    DUOS = G // 2
    TILES = NB * G
    with ExitStack() as c:
        def sb(name, shape, dt=F32):
            return c.enter_context(nc.sbuf_tensor("e_" + name, shape, dt))

        def bank(name):
            return c.enter_context(nc.psum_tensor("e_" + name, [P, 512], F32))

        def sem(name):
            return new_sem(k, c, "e_" + name)

        srcI, dstI = sb("srcI", [P, 2, G], I32), sb("dstI", [P, 2, G], I32)
        sh, attr = sb("sh", [P, 2, G, 4]), sb("attr", [P, 2, G * 8])
        srcf, eq = sb("srcf", [P, 2, G]), sb("eq", [P, 2, G, P])
        cnt, rows = sb("cnt", [P, 2, G]), sb("rows", [P, 2, G], I32)
        flag, away = sb("flag", [P, G]), sb("away", [P, G])
        spare, spare_i = sb("spare", [P, 1]), sb("spare_i", [P, 1], I32)
        later = sb("later", [P, P])
        junk = sb("junk", [P, 4, P])
        fc1, fc2, fc3 = sb("fc1", [P, DUOS, P]), sb("fc2", [P, P]), sb("fc3", [P, 2, D])
        fc3r = sb("fc3r", [P, D])
        attrT, h1, h2 = sb("attrT", [P, P]), sb("h1", [P, DUOS * P]), sb("h2", [P, 2, DUOS * P])
        y = sb("y", [P, YSLOTS, D])
        wac = sb("wac", [P, 2, 2, P])
        te, ev = sb("te", [P, 2, 2, MUL]), sb("ev", [P, 2, 2, 3, MUL])
        ev2 = sb("ev2", [P, 2, 2, MUL])
        ev3 = sb("ev3", [P, 2, 2, MUL])
        msg = sb("msg", [P, 2, 2, 4, 2, MUL])
        total = sb("total", [P, OSLOTS, CNT + 1])
        pA, pH, pW, pO = bank("pA"), [bank("pH0"), bank("pH1")], [bank("pW0"), bank("pW1")], [bank("pO0"), bank("pO1")]

        mix = Mix(k, c)
        consts, w_in, fc_ready = sem("consts"), sem("w_in"), sem("fc_ready")
        paced = sem("paced")
        loaded = [sem("loaded0"), sem("loaded1")]
        src_float = Signal(sem("src_float"))
        attr_turned, attrT_ready = Signal(sem("attr_turned")), Signal(sem("attrT_ready"))
        up = Signal(sem("up"))
        up_silu = Signal(sem("up_silu"))
        src_rows = Signal(sem("src_rows"))
        equal = Signal(sem("equal"), lead=LEAD)
        counted, flagged, rows_ready = Signal(sem("counted"), lead=LEAD), Signal(sem("flagged")), Signal(sem("rows_ready"))
        block_done = Signal(sem("block_done"), lead=LEAD)
        w_done = Signal(sem("w_done"), lead=LEAD)
        wac_ready = Signal(sem("wac_ready"), lead=LEAD)
        y_in = [Signal(sem(f"y_in{s}"), 16) for s in range(YSLOTS)]
        ev_ready, te_ready, ev2_ready, ev3_ready = (Signal(sem(s), lead=LEAD) for s in ("ev_ready", "te_ready", "ev2_ready", "ev3_ready"))
        msg_ready = Signal(sem("msg_ready"), lead=LEAD)
        summed = Signal(sem("summed"), lead=LEAD)
        total_ready = Signal(sem("total_ready"), lead=LEAD)
        added = [Signal(sem(f"added{j}"), 16, lead=LEAD) for j in range(TABLES)]
        zspare = sb("zspare", [P // 2, CNT + 1])
        DVE_STEPS = [(), (0,), (), (), (3,), (4,), (5,), (6, 7)]

        def blocks(eng, prep_first, body):
            prep_first()
            with eng.Fori(0, NB // 2) as i:
                for j in range(2):
                    body(i * 2 + j, j, True)
            body(NB - 1, 0, False)

        def duo_of(b, d):
            return b * DUOS + d

        with nc.Block() as block:
            @block.sync
            def _(sp):
                sp.wait_ge(consts, 1)
                for q in range(DUOS):
                    for h in range(2):
                        r = (2 * q + h) * 8
                        sp.dma_start(fc1[r:r + 8, q, h * MUL:(h + 1) * MUL], t["L0_gnn_fc_w1"]).then_inc(w_in, 16)
                for h in range(2):
                    s = slice(h * MUL, (h + 1) * MUL)
                    sp.dma_start(fc2[s, s], t["L0_gnn_fc_w2"]).then_inc(w_in, 16)
                    sp.dma_start(fc3r[s, :], t["L0_gnn_fc_w3"]).then_inc(w_in, 16)

                mix.load_weights(sp)

                def load(b, j):
                    sp.wait_ge(block_done.sem, block_done.of(b - 2))
                    for to, of in ((srcI, k.srcp), (dstI, k.dstp), (attr, k.attrp)):
                        sp.dma_start(to[:, j, :], of[bass.ds(b, 1)].rearrange("a p f -> p (a f)")).then_inc(loaded[j], 16)
                    sp.dma_start(sh[:, j].rearrange("p g f -> p (g f)"),
                                 k.shp[bass.ds(b, 1)].rearrange("a p f -> p (a f)")).then_inc(loaded[j], 16)
                    mix.load(sp, b)
                with sp.Fori(0, NB // 2) as i:
                    for j in range(2):
                        load(i * 2 + j, j)
                load(NB - 1, 0)

            @block.gpsimd
            def _(pool):
                nc.gpsimd.memset(zspare[:, :], 0.0)
                nc.gpsimd.memset(fc1[:, :, :], 0.0)
                nc.gpsimd.memset(fc2[:, :], 0.0)
                nc.gpsimd.memset(fc3[:, :, :], 0.0).then_inc(consts, 1)
                nc.gpsimd.iota(spare_i[:, :], pattern=[[0, 1]], base=N, channel_multiplier=1)
                nc.gpsimd.memset(later[:, :], 1.0).then_inc(consts, 1)
                pool.wait_ge(consts, 2)
                nc.gpsimd.affine_select(out=later[:, :], in_=later[:, :], compare_op=ALU.is_ge, fill=1024.0,
                                        base=0, pattern=[[-1, P]], channel_multiplier=1).then_inc(consts, 1)

                for j in range(TABLES):
                    for h in range(2):
                        rows_ = slice(N + h * P // 2, N + (h + 1) * P // 2)
                        pool.dma_start(k.tables[j][rows_, :], zspare[:, :]).then_inc(added[j].sem, 16)

                def gather(j, g):
                    pool.indirect_dma_start(y[:, g % YSLOTS, :], None, k.ytab,
                                            bass.IndirectOffsetOnAxis(ap=dstI[:, j, g:g + 1], axis=0)).then_inc(y_in[g % YSLOTS].sem, 16)

                def tiles(b, j, turn, more):
                    wait(pool, rows_ready, b)
                    for d in range(DUOS):
                        wait(pool, msg_ready, duo_of(b, d))
                        pool.sem_inc(paced, 1)
                        for u in range(2):
                            g = 2 * d + u + YSLOTS
                            if g < G:
                                gather(j, g)
                            elif more:
                                if g == G:
                                    pool.wait_ge(loaded[1 - j], (turn + 1) * 64)
                                    pool.sem_inc(paced, 1)
                                gather(1 - j, g - G)
                        for u in range(2):
                            g = 2 * d + u
                            tab = g % TABLES
                            added_before = b * (G // TABLES) + g // TABLES - 1
                            pool.wait_ge(added[tab].sem, added[tab].of(added_before))
                            wait(pool, total_ready, b * G + g)
                            pool.sem_inc(paced, 1)
                            pool.indirect_dma_start(k.tables[tab], bass.IndirectOffsetOnAxis(ap=rows[:, j, g:g + 1], axis=0),
                                                    total[:, g % OSLOTS, :], None, compute_op=ALU.add).then_inc(added[tab].sem, 16)

                pool.wait_ge(loaded[0], 64)
                for g in range(YSLOTS):
                    gather(0, g)
                with pool.Fori(0, NB // 2) as i:
                    for j in range(2):
                        tiles(i * 2 + j, j, i + j, True)
                tiles(NB - 1, 0, 0, False)
                for j in range(TABLES):
                    n = (TILES - 1 - j) // TABLES
                    pool.wait_ge(added[j].sem, added[j].of(n))

            @block.scalar
            def _(act):
                for s in (wac_ready, total_ready):
                    s.credit(act)
                mix.credit_act(act)

                def silu(to, of, scale, n):
                    wait(act, up, n)
                    nc.scalar.activation(to, of, ACT.Silu, scale=scale).then_inc(up_silu.sem, 1)

                def prep(b, j, step):
                    if step == 0:
                        wait(act, attr_turned, b)
                        nc.scalar.copy(attrT[:, :], pA[:, 0:P]).then_inc(attrT_ready.sem, 1)
                    elif step in (1, 2):
                        h = step - 1
                        silu(h1[:, h * 512:(h + 1) * 512], pH[h][:, :], 8 ** -0.5, b * 4 + h)
                    elif step in (3, 4):
                        h = step - 3
                        silu(h2[:, j, h * 512:(h + 1) * 512], pH[h][:, :], 0.125, b * 4 + 2 + h)

                def scaled(b, j, d):
                    n = duo_of(b, d)
                    wait(act, w_done, n)
                    act.wait_ge(msg_ready.sem, msg_ready.of(n - 2))
                    for u in range(2):
                        m = nc.scalar.activation(wac[:, d % 2, u, :], pW[d % 2][:, u * D:u * D + P], ACT.Copy,
                                                 scale=sh[:, j, 2 * d + u, 0:1])
                    m.then_inc(wac_ready.sem, 1)

                def totals(b, j, d):
                    for u in range(2):
                        g = 2 * d + u
                        n = b * G + g
                        slot = g % OSLOTS
                        a = added[g % TABLES]
                        act.wait_ge(a.sem, a.of(b * (G // TABLES) + (g // TABLES) - OSLOTS // TABLES))
                        nc.scalar.copy(total[:, slot, CNT:CNT + 1], cnt[:, j, g:g + 1])
                        wait(act, summed, n)
                        nc.scalar.copy(total[:, slot, 0:CNT], pO[u][:, :]).then_inc(total_ready.sem, 1)

                def body(b, j, more):
                    wait(act, rows_ready, b)
                    for d in range(DUOS):
                        scaled(b, j, d)
                        if more and 1 <= d < 6:
                            prep(b + 1, 1 - j, d - 1)
                        if d:
                            totals(b, j, d - 1)
                        mix.act(act, b, d)
                    totals(b, j, DUOS - 1)
                    mix.act(act, b, DUOS)
                act.wait_ge(fc_ready, 1)
                blocks(act, lambda: [prep(0, 0, s) for s in range(5)], body)

            @block.vector
            def _(dve):
                for s in (block_done, equal, counted, ev_ready, te_ready, ev2_ready, ev3_ready, msg_ready):
                    s.credit(dve)
                dve.wait_ge(w_in, 16 * (2 * DUOS + 4))
                dve.wait_ge(consts, 3)
                for h in range(2):
                    s = slice(h * MUL, (h + 1) * MUL)
                    for to, of, by in ((0, 0, 0.125), (1, 2, 0.125), (2, 1, 0.125), (3, 3, 0.125 * 3 ** -0.5)):
                        m = nc.vector.tensor_scalar(fc3[s, h, to * MUL:(to + 1) * MUL], fc3r[s, of * MUL:(of + 1) * MUL], by, None, ALU.mult)
                nc.vector.tensor_copy(spare[:, :], spare_i[:, :]).then_inc(fc_ready, 1)
                dve.wait_ge(fc_ready, 1)

                def prep(b, j, step, i_turn):
                    if step == 0:
                        dve.wait_ge(loaded[j], (i_turn + 1) * 64)
                        nc.vector.tensor_copy(srcf[:, j, :], srcI[:, j, :]).then_inc(src_float.sem, 1)
                    elif step in (3, 4, 5, 6):
                        q = step - 3
                        n = b * 4 + q
                        wait(dve, src_rows, n)
                        g = slice(4 * q, 4 * q + 4)
                        nc.vector.tensor_tensor(eq[:, j, g, :], pA[:, :].rearrange("p (g i) -> p g i", g=4),
                                                srcf[:, j, g].unsqueeze(2).to_broadcast([P, 4, P]), ALU.is_equal).then_inc(equal.sem, 1)
                        wait(dve, equal, n)
                        dve.wait_ge(counted.sem, counted.of(n - 1))
                        for u in range(4):
                            m = nc.vector.tensor_tensor_reduce(out=junk[:, u, :], in0=eq[:, j, 4 * q + u, :], in1=later[:, :],
                                                               scale=1.0, scalar=0.0, op0=ALU.mult, op1=ALU.add,
                                                               accum_out=cnt[:, j, 4 * q + u:4 * q + u + 1])
                        m.then_inc(counted.sem, 1)
                    elif step == 7:
                        wait(dve, counted, b * 4 + 3)
                        nc.vector.tensor_scalar(flag[:, :], cnt[:, j, :], 1000.0, None, ALU.is_ge)
                        nc.vector.tensor_tensor(away[:, :], spare[:, :].to_broadcast([P, G]), srcf[:, j, :], ALU.subtract).then_inc(flagged.sem, 1)
                        dve.wait_ge(flagged.sem, flagged.of(b * 2))
                        nc.vector.tensor_tensor(away[:, :], away[:, :], flag[:, :], ALU.mult).then_inc(flagged.sem, 1)
                        dve.wait_ge(flagged.sem, flagged.of(b * 2 + 1))
                        nc.vector.tensor_tensor(rows[:, j, :], srcf[:, j, :], away[:, :], ALU.add).then_inc(rows_ready.sem, 1)

                def messages(b, j, d, i_turn):
                    n, par = duo_of(b, d), d % 2
                    s0 = (2 * d) % YSLOTS
                    for u in range(2):
                        dve.wait_ge(y_in[s0 + u].sem, y_in[s0 + u].of(b * (G // YSLOTS) + (2 * d) // YSLOTS))
                    yd = y[:, s0:s0 + 2, :]
                    es = yd[:, :, 0:MUL]
                    evd = yd[:, :, MUL:D].rearrange("p t (d u) -> p t d u", d=3)
                    shd = sh[:, j, 2 * d:2 * d + 2, 1:4].unsqueeze(3).to_broadcast([P, 2, 3, MUL])
                    w = pW[par][:, :].rearrange("p (t w) -> p t w", t=2)
                    m_ = msg[:, par]
                    dve.wait_ge(ev3_ready.sem, ev3_ready.of(n - 2))
                    nc.vector.tensor_tensor(ev[:, par], evd, shd, ALU.mult).then_inc(ev_ready.sem, 1)
                    wait(dve, wac_ready, n)
                    dve.wait_ge(summed.sem, summed.of((n - 2) * 2 + 1))
                    nc.vector.tensor_tensor(te[:, par], w[:, :, P:P + MUL], es, ALU.mult).then_inc(te_ready.sem, 1)
                    wait(dve, ev_ready, n)
                    nc.vector.tensor_tensor(ev2[:, par], ev[:, par, :, 0, :], ev[:, par, :, 1, :], ALU.add).then_inc(ev2_ready.sem, 1)
                    nc.vector.tensor_tensor(m_[:, :, 0, 0, :], wac[:, par, :, 0:MUL], es, ALU.mult)
                    wait(dve, ev2_ready, n)
                    nc.vector.tensor_tensor(ev3[:, par], ev2[:, par], ev[:, par, :, 2, :], ALU.add).then_inc(ev3_ready.sem, 1)
                    nc.vector.tensor_tensor(m_[:, :, 1:4, 1, :], evd, wac[:, par, :, MUL:P].unsqueeze(2).to_broadcast([P, 2, 3, MUL]), ALU.mult)
                    wait(dve, te_ready, n)
                    nc.vector.tensor_tensor(m_[:, :, 1:4, 0, :], te[:, par].unsqueeze(2).to_broadcast([P, 2, 3, MUL]), shd, ALU.mult)
                    wait(dve, ev3_ready, n)
                    nc.vector.tensor_tensor(m_[:, :, 0, 1, :], w[:, :, P + MUL:D], ev3[:, par], ALU.mult).then_inc(msg_ready.sem, 1)

                mix.credit_dve(dve)
                for s in range(8):
                    prep(0, 0, s, 0)
                with dve.Fori(0, NB // 2) as i:
                    for j in range(2):
                        b = i * 2 + j
                        for d in range(DUOS):
                            messages(b, j, d, i)
                            for step in DVE_STEPS[d]:
                                prep(b + 1, 1 - j, step, i + j)
                            mix.dve(dve, b, d)
                        mix.dve(dve, b, DUOS)
                        wait(dve, msg_ready, duo_of(b, DUOS - 1))
                        dve.sem_inc(block_done.sem, 1)
                for d in range(DUOS):
                    messages(NB - 1, 0, d, NB // 2)
                    mix.dve(dve, NB - 1, d)
                mix.dve(dve, NB - 1, DUOS)

            @block.tensor
            def _(pe):
                for s in (w_done, summed):
                    s.credit(pe)
                mix.credit_pe(pe)
                pe.wait_ge(fc_ready, 1)

                def prep(b, j, step, i_turn):
                    if step == 0:
                        pe.wait_ge(loaded[j], (i_turn + 1) * 64)
                        pe.wait_ge(equal.sem, equal.of(b * 4 - 1))
                        nc.tensor.transpose(pA[:, 0:P], attr[:, j, :], k.ident[:, :]).then_inc(attr_turned.sem, 1)
                    elif step in (1, 2):
                        h = step - 1
                        if h == 0:
                            wait(pe, attrT_ready, b)
                        for q in range(4):
                            m = nc.tensor.matmul(pH[h][:, q * P:(q + 1) * P], fc1[:, 4 * h + q, :], attrT[:, :], start=True, stop=True)
                        m.then_inc(up.sem, 1)
                    elif step in (3, 4):
                        h = step - 3
                        wait(pe, up_silu, b * 4 + h)
                        nc.tensor.matmul(pH[h][:, :], fc2[:, :], h1[:, h * 512:(h + 1) * 512], start=True, stop=True).then_inc(up.sem, 1)
                    if step in (2, 3, 4, 5):
                        q = step - 2
                        if q == 0:
                            wait(pe, src_float, b)
                            wait(pe, attrT_ready, b)
                        else:
                            wait(pe, equal, b * 4 + q - 1)
                        for u in range(4):
                            m = nc.tensor.transpose(pA[:, u * P:(u + 1) * P],
                                                    srcf[:, j, 4 * q + u:4 * q + u + 1].to_broadcast([P, P]), k.ident[:, :])
                        m.then_inc(src_rows.sem, 1)

                def weights(b, j, d):
                    n = duo_of(b, d)
                    if d == 0 or d == 4:
                        wait(pe, up_silu, b * 4 + 2 + d // 4)
                    pe.wait_ge(msg_ready.sem, msg_ready.of(n - 2))
                    for u in range(2):
                        m = nc.tensor.matmul(pW[d % 2][:, u * D:(u + 1) * D], h2[:, j, d * P:(d + 1) * P], fc3[:, u, :], start=True, stop=True)
                    m.then_inc(w_done.sem, 1)

                def sums(b, j, d):
                    n = duo_of(b, d)
                    wait(pe, msg_ready, n)
                    for u in range(2):
                        tile = b * G + 2 * d + u
                        pe.wait_ge(total_ready.sem, total_ready.of(tile - 2))
                        nc.tensor.matmul(pO[u][:, :], eq[:, j, 2 * d + u, :],
                                         msg[:, d % 2, u].rearrange("p a b c -> p (a b c)"), start=True, stop=True).then_inc(summed.sem, 1)

                def body(b, j, more):
                    weights(b, j, 0)
                    for d in range(DUOS):
                        if d + 1 < DUOS:
                            weights(b, j, d + 1)
                        if more is not False and d:
                            prep(b + 1, 1 - j, d - 1, more)
                        mix.pe(pe, b, d)
                        sums(b, j, d)

                for s in range(8):
                    prep(0, 0, s, 0)
                with pe.Fori(0, NB // 2) as i:
                    for j in range(2):
                        body(i * 2 + j, j, i + j)
                body(NB - 1, 0, False)
        clear_semaphores(k)


class Mix:

    def __init__(self, k, c):
        self.k, nc, t, D = k, k.nc, k.t, k.D

        def sb(name, shape, dt=F32):
            return c.enter_context(nc.sbuf_tensor("m_" + name, shape, dt))

        def sem(name):
            return new_sem(k, c, "m_" + name)

        self.wm, self.w1, self.w2 = sb("wm", [P, 2, D]), sb("w1", [P, 4, 2 * D]), sb("w2", [P, 4, D])
        self.g1, self.b1 = sb("g1", [P, 2]), sb("b1", [P, 2])
        self.g2, self.b2 = sb("g2", [P, D]), sb("b2", [P, D])
        self.q = sb("q", [P, D])
        self.den, self.rden, self.msgT = sb("den", [P, D]), sb("rden", [P, D]), sb("msgT", [P, 2, P])
        self.st, self.mv = sb("st", [P, 6]), sb("mv", [P, 2])
        self.ve, self.sd, self.rs, self.nb = sb("ve", [P, 1]), sb("sd", [P, 1]), sb("rs", [P, 1]), sb("nb", [P, 1])
        self.mn, self.mT, self.hid = sb("mn", [P, D]), sb("mT", [P, 2, P]), sb("hid", [P, 4, P])
        self.o1, self.o2 = sb("o1", [P, D]), sb("o2", [P, D])
        self.pM = c.enter_context(nc.psum_tensor("m_pM", [P, 512], F32))
        self.w_in, self.q_in = sem("w_in"), Signal(sem("q_in"), 16)
        self.WEIGHTS = 2 + 3 + 2 + 4 + 4 + 2
        s = lambda name, lead=0: Signal(sem(name), lead=lead)
        self.attended = s("attended", LEAD)
        self.den_eps, self.den_inv, self.msg_T = s("den_eps"), s("den_inv"), s("msg_T")
        self.projected, self.stat, self.aggr, self.var_eps = s("projected"), s("stat"), s("aggr"), s("var_eps")
        self.sqrt, self.rstd, self.shift = s("sqrt"), s("rstd"), s("shift")
        self.normed, self.turned, self.turned_ready = s("normed"), s("turned"), s("turned_ready")
        self.hidden, self.hid_ready, self.mlp_out = s("hidden"), s("hid_ready"), s("mlp_out")
        self.out_normed, self.gained, self.acc_msg = s("out_normed", LEAD), s("gained"), s("acc_msg")
        self.acc_done = s("acc_done", LEAD)
        self.aggregates = sem("aggregates")

    def load_weights(self, sp):
        t, D = self.k.t, self.k.D
        n = 0
        for to, of in ((self.wm, t["L0_mix_Wm"]),):
            for ch in range(2):
                sp.dma_start(to[:, ch, :], of[ch * P:(ch + 1) * P, :]).then_inc(self.w_in, 16)
        for chunk, p0, rows in permuted_rows(t["L0_mix_W1"][0:D, :]):
            sp.dma_start(self.w1[p0:p0 + MUL, chunk, :], rows).then_inc(self.w_in, 16)
        for ch in range(2):
            sp.dma_start(self.w1[:, 2 + ch, :], t["L0_mix_W1"][D + ch * P:D + (ch + 1) * P, :]).then_inc(self.w_in, 16)
        for ch in range(4):
            sp.dma_start(self.w2[:, ch, :], t["L0_mix_W2"][ch * P:(ch + 1) * P, :]).then_inc(self.w_in, 16)
        for to, of in ((self.g1, "L0_mix_g1"), (self.b1, "L0_mix_b1")):
            for ch in range(2):
                sp.dma_start(to[:, ch:ch + 1], t[of][ch * P:(ch + 1) * P].rearrange("(p a) -> p a", a=1)).then_inc(self.w_in, 16)
        for to, of in ((self.g2, "L0_mix_g2"), (self.b2, "L0_mix_b2")):
            sp.dma_start(to[:, :], t[of].partition_broadcast(P)).then_inc(self.w_in, 16)

    LOADS = 2 + 4 + 2 + 4 + 4 + 2

    def load(self, sp, n):
        sp.wait_ge(self.attended.sem, self.attended.of(n - 1))
        sp.dma_start(self.q[:, :], self.k.qtab[bass.ds(n, 1)].rearrange("a p d -> p (a d)")).then_inc(self.q_in.sem, 16)

    def credit_pe(self, pe):
        self.attended.credit(pe)
        pe.wait_ge(self.w_in, 16 * self.LOADS)

    def pe(self, pe, n, d):
        nc, k, pM, D = self.k.nc, self.k, self.pM, self.k.D
        if d == 0:
            wait(pe, self.q_in, n)
            pe.wait_ge(self.out_normed.sem, self.out_normed.of(n - 1))
            for w, at in ((k.KS, 0), (k.KV, D)):
                for ch in range(2):
                    m = nc.tensor.matmul(pM[:, at + ch * P:at + (ch + 1) * P], w[:, ch, :], self.q[:, ch * P:(ch + 1) * P],
                                         start=True, stop=True)
            m.then_inc(self.attended.sem, 1)
        elif d == 1:
            wait(pe, self.msg_T, n)
            for ch in range(2):
                m = nc.tensor.matmul(pM[:, 0:D], self.msgT[:, ch, :], self.wm[:, ch, :], start=ch == 0, stop=ch == 1)
            m.then_inc(self.projected.sem, 1)
        elif d == 4:
            wait(pe, self.normed, n)
            for ch in range(2):
                m = nc.tensor.transpose(pM[:, ch * P:(ch + 1) * P], self.mn[:, ch * P:(ch + 1) * P], k.ident[:, :])
            m.then_inc(self.turned.sem, 1)
        elif d == 5:
            wait(pe, self.turned_ready, n)
            for m_ in range(4):
                for ch in range(4):
                    x = k.xnT[:, ch, bass.ds(n * P, P)] if ch < 2 else self.mT[:, ch - 2, :]
                    m = nc.tensor.matmul(pM[:, m_ * P:(m_ + 1) * P], self.w1[:, ch, m_ * P:(m_ + 1) * P], x,
                                         start=ch == 0, stop=ch == 3)
            m.then_inc(self.hidden.sem, 1)
        elif d == 6:
            wait(pe, self.hid_ready, n)
            for ch in range(4):
                m = nc.tensor.matmul(pM[:, 0:D], self.hid[:, ch, :], self.w2[:, ch, :], start=ch == 0, stop=ch == 3)
            m.then_inc(self.mlp_out.sem, 1)

    def statistics(self, dve, n, which):
        nc, o = self.k.nc, n * 2 + which
        nc.vector.bn_stats(self.st[:, :], self.pM[:, 0:self.k.D]).then_inc(self.stat.sem, 1)
        wait(dve, self.stat, o)
        dve.sem_inc(self.aggregates, 1)
        nc.vector.bn_aggr(self.mv[:, :], self.st[:, :]).then_inc(self.aggr.sem, 1)
        wait(dve, self.aggr, o)
        nc.vector.tensor_scalar_add(self.ve[:, :], self.mv[:, 1:2], LN_EPS).then_inc(self.var_eps.sem, 1)

    def inverse(self, dve, n, which):
        nc, o = self.k.nc, n * 2 + which
        wait(dve, self.sqrt, o)
        nc.vector.reciprocal(self.rs[:, :], self.sd[:, :]).then_inc(self.rstd.sem, 1)
        wait(dve, self.rstd, o)
        nc.vector.scalar_tensor_tensor(out=self.nb[:, :], in0=self.mv[:, 0:1], scalar=-1.0, in1=self.rs[:, :],
                                       op0=ALU.mult, op1=ALU.mult).then_inc(self.shift.sem, 1)

    def credit_dve(self, dve):
        self.acc_done.credit(dve)
        dve.wait_ge(self.w_in, 16 * self.LOADS)

    def dve(self, dve, n, d):
        nc, k, pM, D = self.k.nc, self.k, self.pM, self.k.D
        if d == 0:
            wait(dve, self.attended, n)
            nc.vector.tensor_scalar_add(self.den[:, :], pM[:, 0:D], ATT_EPS).then_inc(self.den_eps.sem, 1)
            wait(dve, self.den_eps, n)
            nc.vector.reciprocal(self.rden[:, :], self.den[:, :]).then_inc(self.den_inv.sem, 1)
            wait(dve, self.den_inv, n)
            nc.vector.tensor_tensor(self.msgT[:, :, :].rearrange("p a b -> p (a b)"), pM[:, D:2 * D], self.rden[:, :], ALU.mult).then_inc(self.msg_T.sem, 1)
        elif d == 1:
            wait(dve, self.projected, n)
            self.statistics(dve, n, 0)
        elif d == 2:
            self.inverse(dve, n, 0)
        elif d == 6:
            wait(dve, self.mlp_out, n)
            self.statistics(dve, n, 1)
        elif d == 7:
            self.inverse(dve, n, 1)
        elif d == 8:
            a = k.acc[:, bass.ds(n, 1), :].rearrange("p a d -> p (a d)")
            wait(dve, self.out_normed, n)
            nc.vector.tensor_tensor(a, a, self.b2[:, :], ALU.add).then_inc(self.gained.sem, 1)
            nc.vector.tensor_tensor(self.o2[:, :], self.o1[:, :], self.g2[:, :], ALU.mult).then_inc(self.acc_msg.sem, 1)
            wait(dve, self.gained, n)
            wait(dve, self.acc_msg, n)
            nc.vector.tensor_tensor(a, a, self.o2[:, :], ALU.add).then_inc(self.acc_done.sem, 1)

    def credit_act(self, act):
        self.out_normed.credit(act)

    def act(self, act, n, d):
        nc, pM, D = self.k.nc, self.pM, self.k.D
        if d in (2, 7):
            wait(act, self.var_eps, n * 2 + (d == 7))
            nc.scalar.activation(self.sd[:, :], self.ve[:, :], ACT.Sqrt).then_inc(self.sqrt.sem, 1)
        elif d == 3:
            wait(act, self.shift, n * 2)
            nc.scalar.activation(self.mn[:, :], pM[:, 0:D], ACT.Identity, scale=self.rs[:, :], bias=self.nb[:, :]).then_inc(self.normed.sem, 1)
        elif d == 4:
            wait(act, self.turned, n)
            for ch in range(2):
                m = nc.scalar.activation(self.mT[:, ch, :], pM[:, ch * P:(ch + 1) * P], ACT.Identity,
                                         scale=self.g1[:, ch:ch + 1], bias=self.b1[:, ch:ch + 1])
            m.then_inc(self.turned_ready.sem, 1)
        elif d == 5:
            wait(act, self.hidden, n)
            nc.scalar.activation(self.hid[:, :, :].rearrange("p a b -> p (a b)"), pM[:, :], ACT.Relu).then_inc(self.hid_ready.sem, 1)
        elif d == 8:
            wait(act, self.shift, n * 2 + 1)
            act.wait_ge(self.acc_done.sem, self.acc_done.of(n - 1))
            nc.scalar.activation(self.o1[:, :], pM[:, 0:D], ACT.Identity, scale=self.rs[:, :], bias=self.nb[:, :]).then_inc(self.out_normed.sem, 1)


def stage_gnn(k):
    nc, t, NT, D, N = k.nc, k.t, k.NT, k.D, k.N
    with ExitStack() as c:
        def sb(name, shape, dt=F32):
            return c.enter_context(nc.sbuf_tensor("g_" + name, shape, dt))

        def bank(name):
            return c.enter_context(nc.psum_tensor("g_" + name, [P, 512], F32))

        def sem(name):
            return new_sem(k, c, "g_" + name)

        parts, sc = sb("parts", [P, 2, TABLES, CNT + 1]), sb("sc", [P, 2, D])
        ns, deg, root, dn = sb("ns", [P, 2, CNT + 1]), sb("deg", [P, 2, 1]), sb("root", [P, 2, 1]), sb("dn", [P, 2, 1])
        nsn, nT = sb("nsn", [P, 2, CNT]), sb("nT", [P, 2, 4, P])
        w2r, w2 = sb("w2r", [P, 2, MUL]), sb("w2", [P, 2, MUL])
        gain = sb("gain", [P, D])
        gv = sb("gv", [P, MUL])
        o, o2, junk = sb("o", [P, 2, D]), sb("o2", [P, 2, D]), sb("junk", [P, 2, D])
        ms, mse, rms, inv = sb("ms", [P, 2, 2]), sb("mse", [P, 2, 2]), sb("rms", [P, 2, 2]), sb("inv", [P, 2, 2])
        pT, pG = [bank("pT0"), bank("pT1")], [bank("pG0"), bank("pG1")]
        w_in, loaded, ready = sem("w_in"), [sem("loaded0"), sem("loaded1")], sem("ready")
        s = lambda name: Signal(sem(name), lead=LEAD)
        summed, degree, rooted, scaled_dn, scaled, turned, turned_ready, through = (s(x) for x in (
            "summed", "degree", "rooted", "scaled_dn", "scaled", "turned", "turned_ready", "through"))
        with_sc, squares, eps_in, rms_ready, inv_ready, gained, acc_done = (s(x) for x in (
            "with_sc", "squares", "eps_in", "rms_ready", "inv_ready", "gained", "acc_done"))
        LOADS = TABLES + 1

        def pairs(eng, *steps):
            with eng.Fori(0, NT // 2) as i:
                for step in steps:
                    for j in range(2):
                        step(i * 2 + j, j, i)
            for step in steps:
                step(NT - 1, 0, NT // 2)

        with nc.Block() as block:
            @block.sync
            def _(sp):
                for to, of in ((0, "L0_gnn_w2_s"), (1, "L0_gnn_w2_v")):
                    sp.dma_start(w2r[:, to, :], t[of]).then_inc(w_in, 16)
                sp.dma_start(gain[:, 0:MUL], t["L0_gnn_g_s"].partition_broadcast(P)).then_inc(w_in, 16)
                sp.dma_start(gv[:, :], t["L0_gnn_g_v"].partition_broadcast(P)).then_inc(w_in, 16)

                def load(n, j, turn):
                    sp.wait_ge(with_sc.sem, with_sc.of(n - 2))
                    for tab in range(TABLES):
                        sp.dma_start(parts[:, j, tab, :], k.tables[tab][bass.ds(n * P, P), :]).then_inc(loaded[j], 16)
                    sp.dma_start(sc[:, j, :], k.sctab[bass.ds(n * P, P), :]).then_inc(loaded[j], 16)
                pairs(sp, load)

            @block.vector
            def _(dve):
                for x in (summed, degree, scaled_dn, with_sc, squares, eps_in, inv_ready, gained, acc_done):
                    x.credit(dve)
                dve.wait_ge(w_in, 64)
                nc.vector.tensor_scalar(w2[:, :, :], w2r[:, :, :], (2.0 * MUL) ** -0.5, None, ALU.mult)
                nc.vector.tensor_copy(gain[:, MUL:D].rearrange("p (d u) -> p d u", d=3),
                                      gv[:, :].unsqueeze(1).to_broadcast([P, 3, MUL])).then_inc(ready, 1)
                dve.wait_ge(ready, 1)

                def sum_parts(n, j, turn):
                    dve.wait_ge(loaded[j], (turn + 1) * 16 * LOADS)
                    dve.wait_ge(scaled.sem, scaled.of(n - 2))
                    nc.vector.tensor_tensor(ns[:, j, :], parts[:, j, 0, :], parts[:, j, 1, :], ALU.add).then_inc(summed.sem, 1)
                    wait(dve, summed, n)
                    nc.vector.tensor_scalar_max(deg[:, j, :], ns[:, j, CNT:CNT + 1], 1.0).then_inc(degree.sem, 1)

                def invert(n, j, turn):
                    wait(dve, rooted, n)
                    nc.vector.reciprocal(dn[:, j, :], root[:, j, :]).then_inc(scaled_dn.sem, 1)

                def add_sc(n, j, turn):
                    wait(dve, through, n)
                    dve.wait_ge(gained.sem, gained.of(n - 2))
                    nc.vector.tensor_tensor(o[:, j, :], pG[j][:, 0:D], sc[:, j, :], ALU.add).then_inc(with_sc.sem, 1)
                    wait(dve, with_sc, n)
                    for h, (a, b) in enumerate(((0, MUL), (MUL, D))):
                        m = nc.vector.tensor_tensor_reduce(out=junk[:, j, a:b], in0=o[:, j, a:b], in1=o[:, j, a:b], scale=1.0 / (b - a),
                                                           scalar=0.0, op0=ALU.mult, op1=ALU.add, accum_out=ms[:, j, h:h + 1])
                    m.then_inc(squares.sem, 1)
                    wait(dve, squares, n)
                    nc.vector.tensor_scalar_add(mse[:, j, :], ms[:, j, :], LN_EPS).then_inc(eps_in.sem, 1)

                def add_acc(n, j, turn):
                    wait(dve, rms_ready, n)
                    nc.vector.reciprocal(inv[:, j, :], rms[:, j, :]).then_inc(inv_ready.sem, 1)
                    wait(dve, inv_ready, n)
                    for h, (a, b) in enumerate(((0, MUL), (MUL, D))):
                        m = nc.vector.scalar_tensor_tensor(out=o2[:, j, a:b], in0=o[:, j, a:b], scalar=inv[:, j, h:h + 1],
                                                           in1=gain[:, a:b], op0=ALU.mult, op1=ALU.mult)
                    m.then_inc(gained.sem, 1)
                    wait(dve, gained, n)
                    r = k.acc[:, bass.ds(n, 1), :].rearrange("p a d -> p (a d)")
                    nc.vector.tensor_tensor(r[:, 0:MUL], r[:, 0:MUL], o2[:, j, 0:MUL], ALU.add)
                    v = r[:, MUL:D].rearrange("p (u d) -> p u d", d=3)
                    nc.vector.tensor_tensor(v, v, o2[:, j, MUL:D].rearrange("p (d u) -> p u d", d=3), ALU.add).then_inc(acc_done.sem, 1)
                pairs(dve, sum_parts, invert, add_sc, add_acc)

            @block.scalar
            def _(act):
                for x in (rooted, scaled, turned_ready, rms_ready):
                    x.credit(act)

                def root_deg(n, j, turn):
                    wait(act, degree, n)
                    nc.scalar.activation(root[:, j, :], deg[:, j, :], ACT.Sqrt).then_inc(rooted.sem, 1)

                def scale(n, j, turn):
                    wait(act, scaled_dn, n)
                    act.wait_ge(turned.sem, turned.of(n - 2))
                    nc.scalar.activation(nsn[:, j, :], ns[:, j, 0:CNT], ACT.Copy, scale=dn[:, j, :]).then_inc(scaled.sem, 1)

                def keep(n, j, turn):
                    wait(act, turned, n)
                    act.wait_ge(through.sem, through.of(n - 2))
                    nc.scalar.copy(nT[:, j].rearrange("p a b -> p (a b)"), pT[j][:, :]).then_inc(turned_ready.sem, 1)

                def root_ms(n, j, turn):
                    wait(act, eps_in, n)
                    nc.scalar.activation(rms[:, j, :], mse[:, j, :], ACT.Sqrt).then_inc(rms_ready.sem, 1)
                pairs(act, root_deg, scale, keep, root_ms)

            @block.tensor
            def _(pe):
                for x in (turned, through):
                    x.credit(pe)
                pe.wait_ge(ready, 1)

                def turn_(n, j, turn):
                    wait(pe, scaled, n)
                    pe.wait_ge(turned_ready.sem, turned_ready.of(n - 2))
                    for ch in range(4):
                        m = nc.tensor.transpose(pT[j][:, ch * P:(ch + 1) * P], nsn[:, j, ch * P:(ch + 1) * P], k.ident[:, :])
                    m.then_inc(turned.sem, 1)

                def product(n, j, turn):
                    wait(pe, turned_ready, n)
                    pe.wait_ge(with_sc.sem, with_sc.of(n - 2))
                    for ch in range(4):
                        m = nc.tensor.matmul(pG[j][:, ch * MUL:(ch + 1) * MUL], nT[:, j, ch, :], w2[:, min(ch, 1), :], start=True, stop=True)
                    m.then_inc(through.sem, 1)
                pairs(pe, turn_, product)
        clear_semaphores(k)


def stage_route(k):
    nc, t, NT, D, N = k.nc, k.t, k.NT, k.D, k.N
    X, CAP = k.NEXP, k.CAP
    with ExitStack() as c:
        def sb(name, shape, dt=F32):
            return c.enter_context(nc.sbuf_tensor("r_" + name, shape, dt))

        def bank(name):
            return c.enter_context(nc.psum_tensor("r_" + name, [P, 512], F32))

        def sem(name):
            return new_sem(k, c, "r_" + name)

        stats, mean, diff, vare = sb("stats", [P, NT, 6]), sb("mean", [P, NT]), sb("diff", [P, NT]), sb("vare", [P, NT])
        msum, vs, dsq, half = sb("msum", [P, NT]), sb("vs", [P, NT]), sb("dsq", [P, NT]), sb("half", [P, NT])
        rstd, shift = sb("rstd", [P, NT]), sb("shift", [P, NT])
        tn, ts, tT = sb("tn", [P, NT, D]), sb("ts", [P, 2, D]), sb("tT", [P, 2, 2, P])
        gw, gb = sb("gw", [P, 2, X]), sb("gb", [P, X])
        logits, ex, onehot = sb("logits", [P, NT, X]), sb("ex", [P, NT, X]), sb("onehot", [P, NT, X])
        score, pos, tmp = sb("score", [P, NT, X]), sb("pos", [P, NT, X]), sb("tmp", [P, NT, X])
        cum, tot = sb("cum", [P, NT, X]), sb("tot", [P, NT, X])
        top, total, best, place = sb("top", [P, NT]), sb("total", [P, NT]), sb("best", [P, NT]), sb("place", [P, NT])
        slot, kept, spare, over = sb("slot", [P, NT]), sb("kept", [P, NT]), sb("spare", [P, NT]), sb("over", [P, NT])
        valid, onest = sb("valid", [P, NT]), sb("onest", [P, NT])
        first, start = sb("first", [P, X]), sb("start", [P, X])
        first_i, start_i, spare_i = sb("first_i", [P, X], I32), sb("start_i", [P, X], I32), sb("spare_i", [P, NT], I32)
        rows = sb("rows", [P, NT], I32)
        before = sb("before", [P, P])
        pT, pL = [bank("pT0"), bank("pT1")], [bank("pL0"), bank("pL1")]
        pC, pS = bank("pC"), bank("pS")
        w_in, set_up, masks, statd, dved, powered, ln_ready, expd, chosen, counted = (sem(x) for x in (
            "w_in", "set_up", "masks", "statd", "dved", "powered", "ln_ready", "expd", "chosen", "counted"))
        scattered, centred, rows_ready = sem("scattered"), sem("centred"), sem("rows_ready")
        s = lambda name: Signal(sem(name), lead=LEAD)
        ts_ready, tn_kept, turned, turned_ready, gated, logit = (s(x) for x in (
            "ts_ready", "tn_kept", "turned", "turned_ready", "gated", "logit"))

        def pairs(eng, *steps):
            with eng.Fori(0, NT // 2) as i:
                for step in steps:
                    for j in range(2):
                        step(i * 2 + j, j)
            for step in steps:
                step(NT - 1, 0)

        with nc.Block() as block:
            @block.sync
            def _(sp):
                for ch in range(2):
                    sp.dma_start(gw[:, ch, :], t["L0_ffn_gate_w"][ch * P:(ch + 1) * P, :]).then_inc(w_in, 16)
                sp.dma_start(gb[:, :], t["L0_ffn_gate_b"].partition_broadcast(P)).then_inc(w_in, 16)

            @block.gpsimd
            def _(pool):
                nc.gpsimd.memset(half[:, :], -0.5)
                nc.gpsimd.memset(onest[:, :], 1.0)
                nc.gpsimd.memset(valid[:, :], 1.0)
                nc.gpsimd.memset(before[:, :], 1.0)
                nc.gpsimd.iota(first_i[:, :], pattern=[[-1, X]], base=X, channel_multiplier=0)
                nc.gpsimd.iota(start_i[:, :], pattern=[[CAP, X]], base=0, channel_multiplier=0)
                nc.gpsimd.iota(spare_i[:, :], pattern=[[P, NT]], base=X * CAP, channel_multiplier=1).then_inc(set_up, 1)
                pool.wait_ge(set_up, 1)
                nc.gpsimd.affine_select(out=valid[:, :], in_=valid[:, :], compare_op=ALU.is_ge, fill=0.0,
                                        base=N - 1, pattern=[[-P, NT]], channel_multiplier=-1)
                nc.gpsimd.affine_select(out=before[:, :], in_=before[:, :], compare_op=ALU.is_ge, fill=0.0,
                                        base=-1, pattern=[[1, P]], channel_multiplier=-1).then_inc(masks, 1)
                pool.wait_ge(dved, 3)
                nc.gpsimd.tensor_tensor(rstd[:, :], vare[:, :], half[:, :], ALU.pow).then_inc(powered, 1)
                pool.wait_ge(rows_ready, 1)
                for n in range(NT):
                    pool.indirect_dma_start(k.buf, bass.IndirectOffsetOnAxis(ap=rows[:, n:n + 1], axis=0), tn[:, n, :], None)\
                        .then_inc(scattered, 16)
                pool.wait_ge(scattered, 16 * NT)

            @block.vector
            def _(dve):
                n_ = [0]

                def link(m):
                    n_[0] += 1
                    m.then_inc(dved, 1)
                    dve.wait_ge(dved, n_[0])

                with dve.Fori(0, NT) as i:
                    nc.vector.bn_stats(stats[:, bass.ds(i, 1), :].rearrange("p a d -> p (a d)"),
                                       k.acc[:, bass.ds(i, 1), :].rearrange("p a d -> p (a d)")).then_inc(statd, 1)
                dve.wait_ge(statd, NT)
                nc.vector.tensor_tensor(msum[:, :], stats[:, :, 1], stats[:, :, 4], ALU.add)
                nc.vector.tensor_tensor(diff[:, :], stats[:, :, 1], stats[:, :, 4], ALU.subtract)
                link(nc.vector.tensor_tensor(vare[:, :], stats[:, :, 2], stats[:, :, 5], ALU.add))
                nc.vector.tensor_scalar(mean[:, :], msum[:, :], 0.5, None, ALU.mult)
                nc.vector.tensor_tensor(dsq[:, :], diff[:, :], diff[:, :], ALU.mult)
                link(nc.vector.tensor_scalar(vs[:, :], vare[:, :], 1.0 / D, LN_EPS, ALU.mult, ALU.add))
                link(nc.vector.scalar_tensor_tensor(out=vare[:, :], in0=dsq[:, :], scalar=0.25, in1=vs[:, :], op0=ALU.mult, op1=ALU.add))
                dve.wait_ge(set_up, 1)
                nc.vector.tensor_copy(first[:, :], first_i[:, :])
                nc.vector.tensor_copy(start[:, :], start_i[:, :])
                nc.vector.tensor_copy(spare[:, :], spare_i[:, :])
                for x in (tn_kept, logit):
                    x.credit(dve)
                dve.wait_ge(powered, 1)
                nc.vector.scalar_tensor_tensor(out=shift[:, :], in0=mean[:, :], scalar=-1.0, in1=rstd[:, :],
                                               op0=ALU.mult, op1=ALU.mult).then_inc(ln_ready, 1)
                dve.wait_ge(w_in, 48)

                def keep(n, j):
                    wait(dve, ts_ready, n)
                    nc.vector.tensor_copy(tn[:, bass.ds(n, 1), :].rearrange("p a d -> p (a d)"), ts[:, j, :]).then_inc(tn_kept.sem, 1)

                def bias(n, j):
                    wait(dve, gated, n)
                    nc.vector.tensor_tensor(logits[:, bass.ds(n, 1), :].rearrange("p a d -> p (a d)"), pL[j][:, 0:X], gb[:, :],
                                            ALU.add).then_inc(logit.sem, 1)
                pairs(dve, keep, bias)
                wait(dve, logit, NT - 1)

                def wide(a):
                    return a[:, :].unsqueeze(2).to_broadcast([P, NT, X])

                def over_tiles(a):
                    return a[:, :].unsqueeze(1).to_broadcast([P, NT, X])
                link(nc.vector.tensor_reduce(out=top[:, :], in_=logits[:, :, :], op=ALU.max, axis=AX))
                nc.vector.tensor_tensor(tmp[:, :, :], logits[:, :, :], wide(top), ALU.subtract).then_inc(centred, 1)
                dve.wait_ge(expd, 1)
                nc.vector.tensor_reduce(out=total[:, :], in_=ex[:, :, :], op=ALU.add, axis=AX)
                link(nc.vector.tensor_reduce(out=top[:, :], in_=ex[:, :, :], op=ALU.max, axis=AX))
                nc.vector.reciprocal(best[:, :], total[:, :])
                link(nc.vector.tensor_tensor(onehot[:, :, :], ex[:, :, :], wide(top), ALU.is_equal))
                link(nc.vector.tensor_tensor(score[:, :, :], onehot[:, :, :], over_tiles(first), ALU.mult))
                link(nc.vector.tensor_reduce(out=place[:, :], in_=score[:, :, :], op=ALU.max, axis=AX))
                link(nc.vector.tensor_tensor(onehot[:, :, :], score[:, :, :], wide(place), ALU.is_equal))
                nc.vector.tensor_tensor(best[:, :], best[:, :], top[:, :], ALU.mult)
                dve.wait_ge(masks, 1)
                nc.vector.tensor_tensor(onehot[:, :, :], onehot[:, :, :], wide(valid), ALU.mult).then_inc(chosen, 1)
                dve.wait_ge(counted, 1)
                link(nc.vector.tensor_copy(tot[:, :, :].rearrange("p a b -> p (a b)"), pS[:, 0:NT * X]))
                for e in range(X):
                    m = nc.vector.tensor_tensor_scan(cum[:, :, e], onest[:, :], tot[:, :, e], 0.0, ALU.mult, ALU.add)
                link(m)
                link(nc.vector.tensor_tensor(pos[:, :, :], cum[:, :, :], tot[:, :, :], ALU.subtract))
                link(nc.vector.tensor_tensor(pos[:, :, :].rearrange("p a b -> p (a b)"), pos[:, :, :].rearrange("p a b -> p (a b)"), pC[:, 0:NT * X], ALU.add))
                nc.vector.tensor_tensor(score[:, :, :], pos[:, :, :], over_tiles(start), ALU.add)
                link(nc.vector.tensor_tensor(tmp[:, :, :], pos[:, :, :], onehot[:, :, :], ALU.mult))
                nc.vector.tensor_reduce(out=place[:, :], in_=tmp[:, :, :], op=ALU.add, axis=AX)
                link(nc.vector.tensor_tensor(score[:, :, :], score[:, :, :], onehot[:, :, :], ALU.mult))
                link(nc.vector.tensor_reduce(out=slot[:, :], in_=score[:, :, :], op=ALU.add, axis=AX))
                nc.vector.tensor_scalar(kept[:, :], place[:, :], float(CAP), None, ALU.is_lt)
                nc.vector.tensor_scalar(over[:, :], place[:, :], float(1 - CAP), 0.0, ALU.add, ALU.max)
                link(nc.vector.tensor_tensor(total[:, :], slot[:, :], spare[:, :], ALU.subtract))
                link(nc.vector.tensor_tensor(kept[:, :], kept[:, :], valid[:, :], ALU.mult))
                link(nc.vector.tensor_tensor(total[:, :], total[:, :], kept[:, :], ALU.mult))
                nc.vector.tensor_tensor(k.weight[:, :], best[:, :], kept[:, :], ALU.mult)
                nc.vector.tensor_tensor(k.back[:, :], slot[:, :], over[:, :], ALU.subtract)
                nc.vector.tensor_tensor(rows[:, :], total[:, :], spare[:, :], ALU.add).then_inc(rows_ready, 1)

            @block.scalar
            def _(act):
                for x in (ts_ready, turned_ready):
                    x.credit(act)
                act.wait_ge(ln_ready, 1)

                def norm(n, j):
                    act.wait_ge(tn_kept.sem, tn_kept.of(n - 2))
                    act.wait_ge(turned.sem, turned.of(n - 2))
                    nc.scalar.activation(ts[:, j, :], k.acc[:, bass.ds(n, 1), :].rearrange("p a d -> p (a d)"), ACT.Identity,
                                         scale=rstd[:, bass.ds(n, 1)], bias=shift[:, bass.ds(n, 1)]).then_inc(ts_ready.sem, 1)

                def keep(n, j):
                    wait(act, turned, n)
                    act.wait_ge(gated.sem, gated.of(n - 2))
                    nc.scalar.copy(tT[:, j].rearrange("p a b -> p (a b)"), pT[j][:, 0:D]).then_inc(turned_ready.sem, 1)
                pairs(act, norm, keep)
                act.wait_ge(centred, 1)
                nc.scalar.activation(ex[:, :, :], tmp[:, :, :], ACT.Exp).then_inc(expd, 1)

            @block.tensor
            def _(pe):
                for x in (turned, gated):
                    x.credit(pe)
                pe.wait_ge(w_in, 48)

                def turn(n, j):
                    wait(pe, ts_ready, n)
                    pe.wait_ge(turned_ready.sem, turned_ready.of(n - 2))
                    for ch in range(2):
                        m = nc.tensor.transpose(pT[j][:, ch * P:(ch + 1) * P], ts[:, j, ch * P:(ch + 1) * P], k.ident[:, :])
                    m.then_inc(turned.sem, 1)

                def gate(n, j):
                    wait(pe, turned_ready, n)
                    pe.wait_ge(logit.sem, logit.of(n - 2))
                    for ch in range(2):
                        m = nc.tensor.matmul(pL[j][:, 0:X], tT[:, j, ch, :], gw[:, ch, :], start=ch == 0, stop=ch == 1)
                    m.then_inc(gated.sem, 1)
                pairs(pe, turn, gate)
                pe.wait_ge(chosen, 1)
                oh = onehot[:, :, :].rearrange("p a b -> p (a b)")
                nc.tensor.matmul(pC[:, 0:NT * X], before[:, :], oh, start=True, stop=True)
                nc.tensor.matmul(pS[:, 0:NT * X], k.ones[:, :], oh, start=True, stop=True).then_inc(counted, 1)
        clear_semaphores(k)


def stage_experts(k):
    nc, t, D, FF, CAP = k.nc, k.t, k.D, k.FF, k.CAP
    M = FF // P
    R = (CAP + P - 1) // P
    RL = CAP - (R - 1) * P
    SPLIT = (CAP + 1) // 2
    halves = ((0, SPLIT), (SPLIT, CAP))
    assert R == 8 and SPLIT <= 512
    with ExitStack() as c:
        def sb(name, shape, dt=F32):
            return c.enter_context(nc.sbuf_tensor("x_" + name, shape, dt))

        def bank(name):
            return c.enter_context(nc.psum_tensor("x_" + name, [P, 512], F32))

        def sem(name):
            return new_sem(k, c, "x_" + name)

        w1, w2 = sb("w1", [P, 2, 2, FF]), sb("w2", [P, 2, M, D])
        b1, b2 = sb("b1", [P, 2, M]), sb("b2", [P, 2, D])
        xb, xT = sb("xb", [P, 2, R, D]), sb("xT", [P, 2, 2, R * P])
        hid, yo = sb("hid", [P, M, CAP]), sb("yo", [P, R, D])
        pT, pH, pY = [bank("pT0"), bank("pT1")], [bank("pH0"), bank("pH1")], [bank("pY0"), bank("pY1")]
        loaded, zeroed = [sem("loaded0"), sem("loaded1")], sem("zeroed")
        s = lambda name, unit=1: Signal(sem(name), unit, lead=LEAD)
        turned, turned_ready = s("turned"), s("turned_ready")
        hidden, hid_ready = s("hidden"), s("hid_ready")
        out, row_tile = s("out"), s("row_tile")
        out_ready = s("out_ready")
        stores = sem("stores")
        stored = s("stored")
        LOADS = 2 + 1 + M + 1 + 2
        QT = R // 2

        def experts(eng, *steps):
            with eng.Fori(0, k.NEXP // 2) as i:
                for j in range(2):
                    for step in steps:
                        step(i * 2 + j, j, i)

        with nc.Block() as block:
            @block.sync
            def _(sp):
                sp.wait_ge(zeroed, 1)

                def load(e, j, turn):
                    sp.wait_ge(out_ready.sem, out_ready.of(e - 2))
                    for ch in range(2):
                        sp.dma_start(w1[:, j, ch, :], t["L0_ffn_w1"][bass.ds(e, 1), ch * P:(ch + 1) * P, :].rearrange("a p f -> p (a f)"))\
                            .then_inc(loaded[j], 16)
                    sp.dma_start(w2[:, j, :, :], t["L0_ffn_w2"][bass.ds(e, 1)].rearrange("a (m p) d -> p (a m) d", p=P)).then_inc(loaded[j], 16)
                    for m in range(M):
                        sp.dma_start(b1[:, j, m:m + 1], t["L0_ffn_b1"][bass.ds(e, 1), m * P:(m + 1) * P].rearrange("a p -> p a")).then_inc(loaded[j], 16)
                    sp.dma_start(b2[:, j, :], t["L0_ffn_b2"][bass.ds(e, 1), :].rearrange("a d -> (a d)").partition_broadcast(P)).then_inc(loaded[j], 16)
                    sp.dma_start(xb[:, j, 0:R - 1, :], k.buf[bass.ds(e * CAP, (R - 1) * P), :].rearrange("(r p) d -> p r d", p=P)).then_inc(loaded[j], 16)
                    sp.dma_start(xb[0:RL, j, R - 1, :], k.buf[bass.ds(e * CAP + (R - 1) * P, RL), :]).then_inc(loaded[j], 16)
                experts(sp, load)

            @block.gpsimd
            def _(pool):
                nc.gpsimd.memset(xb[:, :, R - 1, :], 0.0).then_inc(zeroed, 1)
                stored.credit(pool)

                def store(e, j, turn):
                    wait(pool, out_ready, e)
                    pool.dma_start(k.ybuf[bass.ds(e * CAP, (R - 1) * P), :].rearrange("(r p) d -> p r d", p=P), yo[:, 0:R - 1, :]).then_inc(stores, 16)
                    pool.dma_start(k.ybuf[bass.ds(e * CAP + (R - 1) * P, RL), :], yo[0:RL, R - 1, :]).then_inc(stores, 16)
                    pool.wait_ge(stores, (e + 1) * 32)
                    pool.sem_inc(stored.sem, 1)
                experts(pool, store)

            @block.scalar
            def _(act):
                hid_ready.credit(act)

                def hide(e, j, turn):
                    for m in range(M):
                        for h, (a, b) in enumerate(halves):
                            wait(act, hidden, e * 2 * M + 2 * m + h)
                            nc.scalar.activation(hid[:, m, a:b], pH[h][:, 0:b - a], ACT.Relu, bias=b1[:, j, m:m + 1]).then_inc(hid_ready.sem, 1)
                experts(act, hide)

            @block.vector
            def _(dve):
                for x in (turned_ready, row_tile, out_ready):
                    x.credit(dve)

                def turn(e, j, turn_):
                    for q in range(QT):
                        wait(dve, turned, e * QT + q)
                        nc.vector.tensor_copy(xT[:, j, :, 2 * q * P:(2 * q + 2) * P], pT[q % 2][:, :].rearrange("p (c r) -> p c r", c=2)).then_inc(turned_ready.sem, 1)

                def add_b2(e, j, turn_):
                    dve.wait_ge(stored.sem, stored.of(e - 1))
                    for r in range(R):
                        wait(dve, out, e * R + r)
                        nc.vector.tensor_tensor(yo[:, r, :], pY[r % 2][:, 0:D], b2[:, j, :], ALU.add).then_inc(row_tile.sem, 1)
                    wait(dve, row_tile, e * R + R - 1)
                    dve.sem_inc(out_ready.sem, 1)
                turn(0, 0, 0)
                with dve.Fori(0, k.NEXP // 2 - 1) as i:
                    for j in range(2):
                        turn(i * 2 + j + 1, 1 - j, i)
                        add_b2(i * 2 + j, j, i)
                turn(k.NEXP - 1, 1, 0)
                add_b2(k.NEXP - 2, 0, 0)
                add_b2(k.NEXP - 1, 1, 0)

            @block.tensor
            def _(pe):
                for x in (turned, hidden, out):
                    x.credit(pe)

                def turn(e, j, e_turn):
                    pe.wait_ge(loaded[j], (e_turn + 1) * 16 * LOADS)
                    for q in range(QT):
                        pe.wait_ge(turned_ready.sem, turned_ready.of(e * QT + q - 2))
                        for ch in range(2):
                            for r in range(2):
                                m = nc.tensor.transpose(pT[q % 2][:, (2 * ch + r) * P:(2 * ch + r + 1) * P],
                                                        xb[:, j, 2 * q + r, ch * P:(ch + 1) * P], k.ident[:, :])
                        m.then_inc(turned.sem, 1)

                def up(e, j):
                    wait(pe, turned_ready, e * QT + QT - 1)
                    for m_ in range(M):
                        for h, (a, b) in enumerate(halves):
                            pe.wait_ge(hid_ready.sem, hid_ready.of(e * 2 * M + 2 * m_ + h - 2))
                            for ch in range(2):
                                m = nc.tensor.matmul(pH[h][:, 0:b - a], w1[:, j, ch, m_ * P:(m_ + 1) * P], xT[:, j, ch, a:b], start=ch == 0, stop=ch == 1)
                            m.then_inc(hidden.sem, 1)

                def down(e, j):
                    wait(pe, hid_ready, e * 2 * M + 2 * M - 1)
                    for r in range(R):
                        n = P if r < R - 1 else RL
                        pe.wait_ge(row_tile.sem, row_tile.of(e * R + r - 2))
                        for m_ in range(M):
                            m = nc.tensor.matmul(pY[r % 2][0:n, 0:D], hid[:, m_, r * P:r * P + n], w2[:, j, m_, :], start=m_ == 0, stop=m_ == M - 1)
                        m.then_inc(out.sem, 1)
                turn(0, 0, 0)
                with pe.Fori(0, k.NEXP // 2 - 1) as i:
                    for j in range(2):
                        up(i * 2 + j, j)
                        turn(i * 2 + j + 1, 1 - j, i + j)
                        down(i * 2 + j, j)
                up(k.NEXP - 2, 0)
                turn(k.NEXP - 1, 1, k.NEXP // 2 - 1)
                down(k.NEXP - 2, 0)
                up(k.NEXP - 1, 1)
                down(k.NEXP - 1, 1)
        clear_semaphores(k)


def stage_combine(k):
    nc, NT, D, N, LAST = k.nc, k.NT, k.D, k.N, k.LAST
    S = 4
    FMAX = 3.4028234e38
    U8 = mybir.dt.uint8
    with ExitStack() as c:
        def sb(name, shape, dt=F32):
            return c.enter_context(nc.sbuf_tensor("o_" + name, shape, dt))

        def sem(name):
            return new_sem(k, c, "o_" + name)

        g, y = sb("g", [P, 8, D]), sb("y", [P, S, D])
        nan, high, low = sb("nan", [P, S, D], I32), sb("high", [P, S, D], I32), sb("low", [P, S, D], I32)
        zeros, big, small = sb("zeros", [P, D]), sb("big", [P, D]), sb("small", [P, D])
        rows = sb("rows", [P, NT], I32)
        consts, rows_ready = sem("consts"), sem("rows_ready")
        got = [sem(f"got{i}") for i in range(8)]
        s = lambda name: Signal(sem(name), lead=LEAD)
        scaled, flagged, no_nan, no_high, no_low, added = (s(x) for x in ("scaled", "flagged", "no_nan", "no_high", "no_low", "added"))
        stored = sem("stored")
        with nc.Block() as block:
            @block.sync
            def _(sp):
                def rows_of(n):
                    return k.out[n * P:min((n + 1) * P, N), :]
                step = 7
                for a in range(0, NT, step):
                    b = min(a + step, NT)
                    wait(sp, added, b - 1)
                    if b < NT:
                        sp.dma_start(k.out[a * P:b * P, :].rearrange("(t p) d -> p t d", p=P), k.acc[:, a:b, :]).then_inc(stored, 16)
                    else:
                        sp.dma_start(k.out[a * P:(b - 1) * P, :].rearrange("(t p) d -> p t d", p=P), k.acc[:, a:b - 1, :]).then_inc(stored, 16)
                        sp.dma_start(k.out[(b - 1) * P:N, :], k.acc[0:LAST, b - 1, :]).then_inc(stored, 16)
                sp.wait_ge(stored, 16 * (-(-NT // step) + 1))

            @block.gpsimd
            def _(pool):
                nc.gpsimd.memset(zeros[:, :], 0.0)
                nc.gpsimd.memset(big[:, :], 1e4)
                nc.gpsimd.memset(small[:, :], -1e4).then_inc(consts, 1)
                pool.wait_ge(rows_ready, 1)
                for n in range(NT):
                    if n >= 8:
                        wait(pool, scaled, n - 8)
                    pool.indirect_dma_start(g[:, n % 8, :], None, k.ybuf, bass.IndirectOffsetOnAxis(ap=rows[:, n:n + 1], axis=0)).then_inc(got[n % 8], 16)

            @block.scalar
            def _(act):
                scaled.credit(act)
                for n in range(NT):
                    act.wait_ge(got[n % 8], 16 * (n // 8 + 1))
                    if n >= S:
                        wait(act, added, n - S)
                    nc.scalar.activation(y[:, n % S, :], g[:, n % 8, :], ACT.Copy, scale=k.weight[:, n:n + 1]).then_inc(scaled.sem, 1)

            @block.vector
            def _(dve):
                for x in (flagged, no_nan, no_high, no_low, added):
                    x.credit(dve)
                nc.vector.tensor_copy(rows[:, :], k.back[:, :]).then_inc(rows_ready, 1)
                dve.wait_ge(consts, 1)
                for n in range(NT):
                    v = y[:, n % S, :]
                    wait(dve, scaled, n)
                    nc.vector.tensor_tensor(nan[:, n % S, :], v, v, ALU.not_equal)
                    nc.vector.tensor_scalar(high[:, n % S, :], v, FMAX, None, ALU.is_gt)
                    nc.vector.tensor_scalar(low[:, n % S, :], v, -FMAX, None, ALU.is_lt).then_inc(flagged.sem, 1)
                    wait(dve, flagged, n)
                    nc.vector.copy_predicated(v, nan[:, n % S, :], zeros[:, :]).then_inc(no_nan.sem, 1)
                    wait(dve, no_nan, n)
                    nc.vector.copy_predicated(v, high[:, n % S, :], big[:, :]).then_inc(no_high.sem, 1)
                    wait(dve, no_high, n)
                    nc.vector.copy_predicated(v, low[:, n % S, :], small[:, :]).then_inc(no_low.sem, 1)
                    wait(dve, no_low, n)
                    nc.vector.tensor_tensor(k.acc[:, n, :], k.acc[:, n, :], v, ALU.add).then_inc(added.sem, 1)


_INS = ['x', 'src', 'dst', 'edge_attr_4', 'edge_attr_8', 'L0_gnn_w1_s', 'L0_gnn_w1_v', 'L0_gnn_wsc_s', 'L0_gnn_wsc_v',
        'L0_gnn_w2_s', 'L0_gnn_w2_v', 'L0_gnn_fc_w1', 'L0_gnn_fc_w2', 'L0_gnn_fc_w3', 'L0_gnn_g_s', 'L0_gnn_g_v',
        'L0_mix_Wq', 'L0_mix_Wk', 'L0_mix_Wv', 'L0_mix_Wm', 'L0_mix_W1', 'L0_mix_W2', 'L0_mix_g1', 'L0_mix_b1',
        'L0_mix_g2', 'L0_mix_b2', 'L0_ffn_gate_w', 'L0_ffn_gate_b', 'L0_ffn_w1', 'L0_ffn_b1', 'L0_ffn_w2', 'L0_ffn_b2']


def kernel(**inputs):
    import numpy as _np
    import concourse.bacc as _bacc
    from concourse import mybir as _mybir
    from concourse.bass_utils import run_bass_kernel_spmd as _run

    nc = _bacc.Bacc("TRN2", target_bir_lowering=False, num_devices=1)
    arrays, aps = {}, {}
    for name in _INS:
        a = _np.ascontiguousarray(inputs[name])
        arrays[f"in_{name}"] = a
        aps[name] = nc.dram_tensor(f"in_{name}", a.shape, _mybir.dt.from_np(a.dtype), kind="ExternalInput").ap()
    out = nc.dram_tensor("out_0", inputs["x"].shape, _mybir.dt.float32, kind="ExternalOutput").ap()
    program(nc, aps, out)
    r = _run(nc, [arrays], core_ids=[0])
    return r.results[0]["out_0"]
```

```python
from contextlib import ExitStack

import concourse.bass as bass
from concourse import mybir

F32 = mybir.dt.float32
I32 = mybir.dt.int32
U32 = mybir.dt.uint32
ALU = mybir.AluOpType
ACT = mybir.ActivationFunctionType
AX = mybir.AxisListType.X

P = 128
MUL = 64
HEADS = 8
LN_EPS = 1e-5
ATT_EPS = 1e-6
LEAD = 4
G = 16
YSLOTS = 8
OSLOTS = 8
TABLES = 2
CNT = 8 * MUL


class Signal:

    def __init__(self, sem, unit=1, lead=0):
        self.sem, self.unit, self.lead = sem, unit, lead

    def credit(self, eng):
        eng.sem_inc(self.sem, self.lead * self.unit)

    def of(self, n):
        return (n + (self.lead + 1)) * self.unit


def wait(eng, signal, n):
    eng.wait_ge(signal.sem, signal.of(n))


class Kernel:
    pass


def program(nc, t, out):
    N, D = t["x"].shape
    E = t["src"].shape[0]
    NT = (N + P - 1) // P
    LAST = N - (NT - 1) * P
    NPAD = NT * P
    NB = (E + P * G - 1) // (P * G)
    ELAST = (E - (NB - 1) * P * G) // G
    assert NT == NB and NT % 2 == 1 and ELAST * G == E - (NB - 1) * P * G

    with ExitStack() as ctx:
        k = Kernel()
        k.used = []
        k.nc, k.t, k.out, k.ctx = nc, t, out, ctx
        k.N, k.D, k.E, k.NT, k.LAST, k.NPAD, k.NB, k.ELAST = N, D, E, NT, LAST, NPAD, NB, ELAST
        k.NEXP = t["L0_ffn_gate_w"].shape[1]
        k.FF = t["L0_ffn_w1"].shape[2]
        k.CAP = max(1, -(-5 * N // (4 * k.NEXP)))
        k.acc = ctx.enter_context(nc.sbuf_tensor("acc", [P, NT, D], F32))
        k.ident = ctx.enter_context(nc.sbuf_tensor("ident", [P, P], F32))
        k.ones = ctx.enter_context(nc.sbuf_tensor("ones", [P, P], F32))
        k.stats = ctx.enter_context(nc.sbuf_tensor("stats", [P, NT, 6], F32))
        k.weight = ctx.enter_context(nc.sbuf_tensor("weight", [P, NT], F32))
        k.back = ctx.enter_context(nc.sbuf_tensor("back", [P, NT], F32))
        k.ytab = dram(k, "ytab", [NPAD, D], F32)
        k.sctab = dram(k, "sctab", [NPAD, D], F32)
        k.xtab = dram(k, "xtab", [NT, P, D], F32)
        k.qtab = dram(k, "qtab", [NT, P, D], F32)
        k.tables = [dram(k, f"table{j}", [N + P, CNT + 1], F32) for j in range(TABLES)]
        k.srcp = dram(k, "srcp", [NB, P, G], I32)
        k.dstp = dram(k, "dstp", [NB, P, G], I32)
        k.shp = dram(k, "shp", [NB, P, G * 4], F32)
        k.attrp = dram(k, "attrp", [NB, P, G * 8], F32)
        k.buf = dram(k, "buf", [k.NEXP * k.CAP + NPAD, D], F32)
        k.ybuf = dram(k, "ybuf", [k.NEXP * k.CAP, D], F32)
        with ExitStack() as mix:
            k.KV = mix.enter_context(nc.sbuf_tensor("KV", [P, 2, P], F32))
            k.KS = mix.enter_context(nc.sbuf_tensor("KS", [P, 2, P], F32))
            constants(k)
            stage_nodes(k)
            stage_edges(k)
        stage_gnn(k)
        stage_route(k)
        stage_experts(k)
        stage_combine(k)


def new_sem(k, c, name):
    k.used.append(c.enter_context(k.nc.semaphore(name)))
    return k.used[-1]


def clear_semaphores(k):
    with k.nc.Block() as block:
        @block.gpsimd
        def _(pool):
            for s in k.used:
                pool.sem_clear(s)
    k.used = []


def dram(k, name, shape, dt):
    return k.nc.dram_tensor(name, shape, dt).ap()


def permuted_rows(w):
    for d in range(3):
        yield (d + 1) // 2, MUL * ((d + 1) % 2), w[MUL + d::3]
    yield 0, 0, w[0:MUL]


def vectors_first(row):
    return row[..., MUL:].rearrange("... (u d) -> ... d u", d=3)


def constants(k):
    nc = k.nc
    with ExitStack() as c:
        zeroed = new_sem(k, c, "c_zeroed")
        with nc.Block() as block:
            @block.gpsimd
            def _(pool):
                nc.gpsimd.memset(k.ident[:, :], 0.0)
                nc.gpsimd.memset(k.ones[:, :], 1.0).then_inc(zeroed, 1)
                pool.wait_ge(zeroed, 1)
                nc.gpsimd.affine_select(out=k.ident[:, :], in_=k.ident[:, :], compare_op=ALU.not_equal, fill=1.0,
                                        base=0, pattern=[[-1, P]], channel_multiplier=1)


def stage_nodes(k):
    nc, t, NT, D, N, LAST, NPAD = k.nc, k.t, k.NT, k.D, k.N, k.LAST, k.NPAD
    NB, ELAST = k.NB, k.ELAST
    acc, ident = k.acc, k.ident
    ZR = N + P
    with ExitStack() as c:
        def sb(name, shape, dt=F32):
            return c.enter_context(nc.sbuf_tensor("n_" + name, shape, dt))

        def bank(name):
            return c.enter_context(nc.psum_tensor("n_" + name, [P, 512], F32))

        def sem(name):
            return new_sem(k, c, "n_" + name)

        stats, mv, mean = sb("stats", [P, NT, 6]), sb("mv", [P, NT, 4]), sb("mean", [P, NT])
        rstd, shift, grow, half = sb("rstd", [P, NT]), sb("shift", [P, NT]), sb("grow", [P, NT]), sb("half", [P, NT])
        vare = sb("vare", [P, NT])
        xp, xt = sb("xp", [P, 2, D]), sb("xt", [P, 2, 2, P])
        wq, wk, wv = sb("wq", [P, 2, D]), sb("wk", [P, 2, D]), sb("wv", [P, 2, D])
        wg = sb("wg", [P, 2, 2, P])
        low, exps = sb("low", [P, 2, D]), sb("exps", [P, 2, D])
        qlow, qexps, qf = sb("qlow", [P, 2, D]), sb("qexps", [P, 2, D]), sb("qf", [P, 2, D])
        kf, vf = sb("kf", [P, 2, D]), sb("vf", [P, 2, 2, P + 1])
        ysc = sb("ysc", [P, 2, 2, D])
        mask = sb("mask", [P, P])
        zer = sb("zer", [P, 2048])
        padsrc, padzero = sb("padsrc", [P, G], I32), sb("padzero", [P, G], I32)
        pT = [bank("pT0"), bank("pT1")]
        pK, pV, pQ, pY, pKV = bank("pK"), bank("pV"), bank("pQ"), bank("pY"), bank("pKV")

        x_in, w_in, w1_in, laid = sem("x_in"), sem("w_in"), sem("w1_in"), sem("laid")
        memsets, x_zeroed, powered, statd, meant = (sem(s) for s in (
            "memsets", "x_zeroed", "powered", "statd", "meant"))
        xp_ready = Signal(sem("xp_ready"), lead=LEAD)
        xT_done = Signal(sem("xT_done"), lead=LEAD)
        xt_ready = Signal(sem("xt_ready"), lead=LEAD)
        prod_k = Signal(sem("prod_k"), lead=LEAD)
        prod_v = Signal(sem("prod_v"), lead=LEAD)
        prod_q = Signal(sem("prod_q"), lead=LEAD)
        prod_y = Signal(sem("prod_y"), lead=LEAD)
        k_low, k_exp, k_feat = (Signal(sem(s), lead=LEAD) for s in ("k_low", "k_exp", "k_feat"))
        q_low, q_exp, q_feat = (Signal(sem(s), lead=LEAD) for s in ("q_low", "q_exp", "q_feat"))
        v_copied = Signal(sem("v_copied"), lead=LEAD)
        y_copied = Signal(sem("y_copied"), lead=LEAD)
        grown = Signal(sem("grown"), lead=LEAD)
        kv_added = Signal(sem("kv_added"), lead=LEAD)
        stores, stored = Signal(sem("stores"), 64), Signal(sem("stored"), lead=LEAD)
        masked, ln_ready = sem("masked"), sem("ln_ready")

        def tiles(eng, tile):
            with eng.Fori(0, NT // 2) as i:
                for j in range(2):
                    tile(i * 2 + j, j)
            tile(NT - 1, 0)

        edges = []
        whole = (NB - 1) * P * G
        for name, to, w in (("src", k.srcp, 1), ("dst", k.dstp, 1), ("edge_attr_4", k.shp, 4), ("edge_attr_8", k.attrp, 8)):
            src = t[name]
            flat = src[0:whole] if w == 1 else src[0:whole, :]
            rest = src[whole:k.E] if w == 1 else src[whole:k.E, :]
            pat = "(b p g) -> (b p) g" if w == 1 else "(b p g) f -> (b p) (g f)"
            edges.append((to[0:NB - 1].rearrange("b p f -> (b p) f"), flat.rearrange(pat, p=P, g=G)))
            pat = "(p g) -> p g" if w == 1 else "(p g) f -> p (g f)"
            edges.append((to[NB - 1, 0:ELAST, :], rest.rearrange(pat, g=G)))
        fills = []
        for tab in k.tables:
            flat = tab.rearrange("r c -> (r c)")
            total = ZR * (CNT + 1)
            chunk = P * 2048
            at = 0
            while at < total:
                n = min(chunk, total - at)
                w = n // P
                fills.append((flat[at:at + w * P].rearrange("(p w) -> p w", p=P), zer[:, 0:w]))
                at += w * P
                if n - w * P:
                    r = n - w * P
                    fills.append((flat[at:at + r].rearrange("(p w) -> p w", p=1), zer[0:1, 0:r]))
                    at += r
        rows = k.NEXP * k.CAP
        bflat = k.buf[0:rows - rows % 8].rearrange("(n r) d -> n (r d)", r=8)
        at = 0
        while at < bflat.shape[0]:
            n = min(P, bflat.shape[0] - at)
            fills.append((bflat[at:at + n], zer[0:n, :]))
            at += n
        if rows % 8:
            fills.append((k.buf[rows - rows % 8:rows], zer[0:rows % 8, 0:D]))
        LAID = len(edges) + len(fills) + 4

        with nc.Block() as block:
            @block.sync
            def _(sp):
                sp.wait_ge(x_zeroed, 1)
                xv = t["x"][0:(NT - 1) * P].rearrange("(t p) d -> p t d", p=P)
                sp.dma_start(acc[:, 0:NT - 1, :], xv).then_inc(x_in, 16)
                sp.dma_start(acc[0:LAST, NT - 1, :], t["x"][(NT - 1) * P:N]).then_inc(x_in, 16)
                for w, to in ((t["L0_mix_Wq"], wq), (t["L0_mix_Wk"], wk), (t["L0_mix_Wv"], wv)):
                    for chunk, p0, rows in permuted_rows(w):
                        sp.dma_start(to[p0:p0 + MUL, chunk, :], rows).then_inc(w_in, 16)
                sp.wait_ge(memsets, 1)
                for m, (s, v) in enumerate(((t["L0_gnn_w1_s"], t["L0_gnn_w1_v"]), (t["L0_gnn_wsc_s"], t["L0_gnn_wsc_v"]))):
                    for chunk in range(2):
                        for h in range(2):
                            w = s if (chunk, h) == (0, 0) else v
                            sp.dma_start(wg[h * MUL:(h + 1) * MUL, chunk, m, h * MUL:(h + 1) * MUL], w).then_inc(w1_in, 16)

                def tile(n, j):
                    wait(sp, xt_ready, n)
                    sp.dma_start(k.xtab[bass.ds(n, 1), :, :].rearrange("a p d -> p (a d)"),
                                 xt[:, j, :, :].rearrange("p a b -> p (a b)")).then_inc(stores.sem, 16)
                    wait(sp, y_copied, n)
                    rows = bass.ds(n * P, P)
                    sp.dma_start(k.ytab[rows, :], ysc[:, j, 0, :]).then_inc(stores.sem, 16)
                    sp.dma_start(k.sctab[rows, :], ysc[:, j, 1, :]).then_inc(stores.sem, 16)
                    wait(sp, q_feat, n)
                    sp.dma_start(k.qtab[bass.ds(n, 1), :, :].rearrange("a p d -> p (a d)"), qf[:, j, :]).then_inc(stores.sem, 16)
                    sp.wait_ge(stores.sem, stores.of(n))
                    sp.sem_inc(stored.sem, 1)
                stored.credit(sp)
                tiles(sp, tile)
                sp.wait_ge(laid, 16 * LAID)

            @block.gpsimd
            def _(pool):
                nc.gpsimd.memset(acc[:, NT - 1, :], 0.0).then_inc(x_zeroed, 1)
                nc.gpsimd.memset(half[:, :], -0.5)
                nc.gpsimd.memset(wg[:, :, :, :], 0.0).then_inc(memsets, 1)
                nc.gpsimd.memset(vf[:, :, :, P:P + 1], 1.0)
                nc.gpsimd.memset(padzero[:, :], 0)
                nc.gpsimd.memset(zer[:, :], 0.0)
                nc.gpsimd.iota(padsrc[:, :], pattern=[[0, G]], base=N, channel_multiplier=1).then_inc(memsets, 1)
                pool.wait_ge(memsets, 2)
                for to, of in edges + fills:
                    pool.dma_start(to, of).then_inc(laid, 16)
                tail = P - ELAST
                pool.dma_start(k.srcp[NB - 1, ELAST:P, :], padsrc[ELAST:P, :]).then_inc(laid, 16)
                pool.dma_start(k.dstp[NB - 1, ELAST:P, :], padzero[ELAST:P, :]).then_inc(laid, 16)
                pool.dma_start(k.shp[NB - 1, ELAST:P, :], zer[ELAST:P, 0:G * 4]).then_inc(laid, 16)
                pool.dma_start(k.attrp[NB - 1, ELAST:P, :], zer[ELAST:P, 0:G * 8]).then_inc(laid, 16)
                pool.wait_ge(meant, 3)
                nc.gpsimd.tensor_tensor(rstd[:, :], vare[:, :], half[:, :], ALU.pow).then_inc(powered, 1)

            @block.vector
            def _(dve):
                for s in (xt_ready, k_low, k_feat, q_low, q_feat, grown):
                    s.credit(dve)
                nc.vector.memset(mask[:, :], 0.0).then_inc(masked, 1)
                dve.wait_ge(masked, 1)
                for h in range(4):
                    m = nc.vector.memset(mask[32 * h:32 * h + 32, 32 * h:32 * h + 32], 1.0)
                m.then_inc(masked, 1)
                dve.wait_ge(x_in, 32)
                with dve.Fori(0, NT) as i:
                    nc.vector.bn_stats(stats[:, bass.ds(i, 1), :].rearrange("p a d -> p (a d)"),
                                       acc[:, bass.ds(i, 1), :].rearrange("p a d -> p (a d)")).then_inc(statd, 1)
                dve.wait_ge(statd, NT)
                nc.vector.tensor_tensor(mv[:, :, 0], stats[:, :, 1], stats[:, :, 4], ALU.add)
                nc.vector.tensor_tensor(mv[:, :, 1], stats[:, :, 1], stats[:, :, 4], ALU.subtract)
                nc.vector.tensor_tensor(vare[:, :], stats[:, :, 2], stats[:, :, 5], ALU.add).then_inc(meant, 1)
                dve.wait_ge(meant, 1)
                nc.vector.tensor_scalar(mean[:, :], mv[:, :, 0], 0.5, None, ALU.mult)
                nc.vector.tensor_tensor(mv[:, :, 2], mv[:, :, 1], mv[:, :, 1], ALU.mult)
                nc.vector.tensor_scalar(mv[:, :, 3], vare[:, :], 1.0 / D, LN_EPS, ALU.mult, ALU.add).then_inc(meant, 1)
                dve.wait_ge(meant, 2)
                nc.vector.scalar_tensor_tensor(out=vare[:, :], in0=mv[:, :, 2], scalar=0.25, in1=mv[:, :, 3],
                                               op0=ALU.mult, op1=ALU.add).then_inc(meant, 1)
                dve.wait_ge(powered, 1)
                nc.vector.scalar_tensor_tensor(out=shift[:, :], in0=mean[:, :], scalar=-1.0, in1=rstd[:, :],
                                               op0=ALU.mult, op1=ALU.mult)
                nc.vector.tensor_scalar_add(grow[:, :], rstd[:, :], 1.0).then_inc(ln_ready, 1)
                dve.wait_ge(ln_ready, 1)

                def tile(n, j):
                    wait(dve, xT_done, n)
                    dve.wait_ge(prod_y.sem, prod_y.of(n - 2))
                    dve.wait_ge(stored.sem, stored.of(n - 2))
                    nc.vector.tensor_copy(xt[:, j, :, :], pT[j][:, 0:2 * P]).then_inc(xt_ready.sem, 1)
                    wait(dve, xp_ready, n)
                    a = acc[:, bass.ds(n, 1), :].rearrange("p a d -> p (a d)")
                    nc.vector.tensor_scalar(a, a, grow[:, bass.ds(n, 1)], shift[:, bass.ds(n, 1)], ALU.mult, ALU.add).then_inc(grown.sem, 1)
                    wait(dve, prod_k, n)
                    dve.wait_ge(k_exp.sem, k_exp.of(n - 2))
                    nc.vector.tensor_scalar_min(low[:, j, :], pK[:, 0:D], 0.0).then_inc(k_low.sem, 1)
                    wait(dve, prod_q, n)
                    dve.wait_ge(q_exp.sem, q_exp.of(n - 2))
                    nc.vector.tensor_scalar_min(qlow[:, j, :], pQ[:, 0:D], 0.0).then_inc(q_low.sem, 1)
                    wait(dve, k_exp, n)
                    dve.wait_ge(kv_added.sem, kv_added.of(n - 2))
                    nc.vector.scalar_tensor_tensor(out=kf[:, j, :], in0=pK[:, 0:D], scalar=0.0, in1=exps[:, j, :],
                                                   op0=ALU.max, op1=ALU.add).then_inc(k_feat.sem, 1)
                    wait(dve, q_exp, n)
                    dve.wait_ge(stored.sem, stored.of(n - 2))
                    nc.vector.scalar_tensor_tensor(out=qf[:, j, :], in0=pQ[:, 0:D], scalar=0.0, in1=qexps[:, j, :],
                                                   op0=ALU.max, op1=ALU.add).then_inc(q_feat.sem, 1)
                tiles(dve, tile)
                wait(dve, kv_added, NT - 1)
                dve.wait_ge(masked, 2)
                for ch in range(2):
                    nc.vector.tensor_tensor(k.KV[:, ch, :], pKV[:, ch * (P + 1):ch * (P + 1) + P], mask[:, :], ALU.mult)
                    nc.vector.tensor_scalar(k.KS[:, ch, :], mask[:, :], pKV[:, ch * (P + 1) + P:(ch + 1) * (P + 1)], None, ALU.mult)

            @block.scalar
            def _(act):
                for s in (xp_ready, k_exp, q_exp, v_copied, y_copied):
                    s.credit(act)
                act.wait_ge(ln_ready, 1)

                def norm(n, j):
                    act.wait_ge(xT_done.sem, xT_done.of(n - 2))
                    a = acc[:, bass.ds(n, 1), :].rearrange("p a d -> p (a d)")
                    scale, bias = rstd[:, bass.ds(n, 1)], shift[:, bass.ds(n, 1)]
                    nc.scalar.activation(xp[:, j, 0:MUL], a[:, 0:MUL], ACT.Identity, scale=scale, bias=bias)
                    nc.scalar.activation(xp[:, j, MUL:D].rearrange("p (d u) -> p d u", d=3),
                                         a[:, MUL:D].rearrange("p (u d) -> p d u", d=3),
                                         ACT.Identity, scale=scale, bias=bias).then_inc(xp_ready.sem, 1)

                def rest(n, j):
                    wait(act, k_low, n)
                    act.wait_ge(k_feat.sem, k_feat.of(n - 2))
                    nc.scalar.activation(exps[:, j, :], low[:, j, :], ACT.Exp).then_inc(k_exp.sem, 1)
                    wait(act, prod_v, n)
                    act.wait_ge(kv_added.sem, kv_added.of(n - 2))
                    nc.scalar.copy(vf[:, j, :, 0:P], pV[:, 0:D].rearrange("p (c v) -> p c v", c=2)).then_inc(v_copied.sem, 1)
                    wait(act, q_low, n)
                    act.wait_ge(q_feat.sem, q_feat.of(n - 2))
                    nc.scalar.activation(qexps[:, j, :], qlow[:, j, :], ACT.Exp).then_inc(q_exp.sem, 1)
                    wait(act, prod_y, n)
                    act.wait_ge(stored.sem, stored.of(n - 2))
                    nc.scalar.activation(ysc[:, j, :, :].rearrange("p m (c v) -> p c m v", c=2),
                                         pY[:, :].rearrange("p (c m v) -> p c m v", c=2, m=2), ACT.Copy, scale=MUL ** -0.5).then_inc(y_copied.sem, 1)
                with act.Fori(0, NT // 2) as i:
                    for j in range(2):
                        norm(i * 2 + j, j)
                    for j in range(2):
                        rest(i * 2 + j, j)
                norm(NT - 1, 0)
                rest(NT - 1, 0)

            @block.tensor
            def _(pe):
                for s in (xT_done, prod_k, prod_v, prod_q, prod_y, kv_added):
                    s.credit(pe)
                pe.wait_ge(memsets, 1)
                pe.wait_ge(w_in, 16 * 12)
                pe.wait_ge(w1_in, 16 * 8)
                pe.wait_ge(memsets, 2)
                nc.tensor.matmul(pKV[:, 0:2 * (P + 1)], zer[:, 0:P], zer[:, 0:2 * (P + 1)], start=True, stop=True)

                def transpose(n, j):
                    wait(pe, xp_ready, n)
                    pe.wait_ge(xt_ready.sem, xt_ready.of(n - 2))
                    for ch in range(2):
                        m = nc.tensor.transpose(pT[j][:, ch * P:(ch + 1) * P], xp[:, j, ch * P:(ch + 1) * P], ident[:, :])
                    m.then_inc(xT_done.sem, 1)

                def products(n, j):
                    wait(pe, xt_ready, n)
                    pe.wait_ge(k_feat.sem, k_feat.of(n - 1))
                    for ch in range(2):
                        m = nc.tensor.matmul(pK[:, 0:D], xt[:, j, ch, :], wk[:, ch, :], start=ch == 0, stop=ch == 1)
                    m.then_inc(prod_k.sem, 1)
                    pe.wait_ge(q_feat.sem, q_feat.of(n - 1))
                    for m_ in range(2):
                        for ch in range(2):
                            m = nc.tensor.matmul(pQ[:, m_ * P:(m_ + 1) * P], wq[:, ch, m_ * P:(m_ + 1) * P], xt[:, j, ch, :],
                                                 start=ch == 0, stop=ch == 1)
                    m.then_inc(prod_q.sem, 1)
                    pe.wait_ge(v_copied.sem, v_copied.of(n - 1))
                    for ch in range(2):
                        m = nc.tensor.matmul(pV[:, 0:D], xt[:, j, ch, :], wv[:, ch, :], start=ch == 0, stop=ch == 1)
                    m.then_inc(prod_v.sem, 1)
                    pe.wait_ge(y_copied.sem, y_copied.of(n - 1))
                    for ch in range(2):
                        m = nc.tensor.matmul(pY[:, ch * D:(ch + 1) * D], xt[:, j, ch, :],
                                             wg[:, ch, :, :].rearrange("p m v -> p (m v)"), start=True, stop=True)
                    m.then_inc(prod_y.sem, 1)

                def add_kv(n, j, rows):
                    wait(pe, k_feat, n)
                    wait(pe, v_copied, n)
                    for ch in range(2):
                        m = nc.tensor.matmul(pKV[:, ch * (P + 1):(ch + 1) * (P + 1)], kf[0:rows, j, ch * P:(ch + 1) * P],
                                             vf[0:rows, j, ch, :], start=False, stop=True, skip_group_check=True)
                    m.then_inc(kv_added.sem, 1)
                with pe.Fori(0, NT // 2) as i:
                    for j in range(2):
                        transpose(i * 2 + j, j)
                    for j in range(2):
                        products(i * 2 + j, j)
                    for j in range(2):
                        add_kv(i * 2 + j, j, P)
                transpose(NT - 1, 0)
                products(NT - 1, 0)
                add_kv(NT - 1, 0, LAST)
        clear_semaphores(k)


def stage_edges(k):
    nc, t, NB, N, D = k.nc, k.t, k.NB, k.N, k.D
    DUOS = G // 2
    TILES = NB * G
    AHEAD = 2
    BUFS = 4
    with ExitStack() as c:
        def sb(name, shape, dt=F32):
            return c.enter_context(nc.sbuf_tensor("e_" + name, shape, dt))

        def bank(name):
            return c.enter_context(nc.psum_tensor("e_" + name, [P, 512], F32))

        def sem(name):
            return new_sem(k, c, "e_" + name)

        srcI, dstI = sb("srcI", [P, 2, G], I32), sb("dstI", [P, 2, G], I32)
        sh, attr = sb("sh", [P, 2, G, 4]), sb("attr", [P, 2, G * 8])
        srcf, eq = sb("srcf", [P, 2, G]), sb("eq", [P, 2, G, P])
        cnt, rows = sb("cnt", [P, 2, G]), sb("rows", [P, 2, G], I32)
        flag, away = sb("flag", [P, G]), sb("away", [P, G])
        spare, spare_i = sb("spare", [P, 1]), sb("spare_i", [P, 1], I32)
        later = sb("later", [P, P])
        junk = sb("junk", [P, 4, P])
        fc1, fc2, fc3 = sb("fc1", [P, DUOS, P]), sb("fc2", [P, P]), sb("fc3", [P, 2, D])
        fc3r = sb("fc3r", [P, D])
        attrT, h1, h2 = sb("attrT", [P, P]), sb("h1", [P, DUOS * P]), sb("h2", [P, 2, DUOS * P])
        y = sb("y", [P, YSLOTS, D])
        wac = sb("wac", [P, BUFS, 2, P])
        wbd = sb("wbd", [P, BUFS, 2, P])
        te, ev = sb("te", [P, 2, 2, MUL]), sb("ev", [P, 2, 2, 3, MUL])
        ev2 = sb("ev2", [P, 2, 2, MUL])
        ev3 = sb("ev3", [P, 2, 2, MUL])
        msg = sb("msg", [P, BUFS, 2, 4, 2, MUL])
        total = sb("total", [P, OSLOTS, CNT + 1])
        pA, pH, pW, pO = bank("pA"), bank("pH"), [bank("pW0"), bank("pW1")], [bank("pO0"), bank("pO1")]

        mix = Mix(k, c)
        consts, w_in, fc_ready = sem("consts"), sem("w_in"), sem("fc_ready")
        paced = sem("paced")
        loaded = [sem("loaded0"), sem("loaded1")]
        src_float = Signal(sem("src_float"))
        attr_turned, attrT_ready = Signal(sem("attr_turned")), Signal(sem("attrT_ready"))
        up = Signal(sem("up"))
        up_silu = Signal(sem("up_silu"), lead=LEAD)
        src_rows = Signal(sem("src_rows"))
        equal = Signal(sem("equal"), lead=LEAD)
        counted, flagged, rows_ready = Signal(sem("counted"), lead=LEAD), Signal(sem("flagged")), Signal(sem("rows_ready"))
        block_done = Signal(sem("block_done"), lead=LEAD)
        w_done = Signal(sem("w_done"), lead=LEAD)
        wac_ready = Signal(sem("wac_ready"), lead=LEAD)
        y_in = [Signal(sem(f"y_in{s}"), 16) for s in range(YSLOTS)]
        ev_ready, te_ready, ev2_ready, ev3_ready = (Signal(sem(s), lead=LEAD) for s in ("ev_ready", "te_ready", "ev2_ready", "ev3_ready"))
        msg_ready = Signal(sem("msg_ready"), lead=LEAD)
        summed = Signal(sem("summed"), lead=LEAD)
        total_ready = Signal(sem("total_ready"), lead=LEAD)
        added = [Signal(sem(f"added{j}"), 16, lead=2) for j in range(TABLES)]
        zspare = sb("zspare", [P // 2, MUL])
        DVE_STEPS = [(), (0,), (), (), (3,), (4,), (5,), (6, 7)]

        def over_blocks(eng, body):
            body(0, 0, 0, 0, True)
            with eng.Fori(0, (NB - 3) // 2) as i:
                for j in range(2):
                    body(i * 2 + (j + 1), (j + 1) % 2, i + j, i + 1, False)
            body(NB - 2, 1, (NB - 3) // 2, (NB - 1) // 2, False)
            body(NB - 1, 0, (NB - 1) // 2, None, False)

        def duo_before(b, j, d):
            return (b, j, d - 1) if d else (b - 1, 1 - j, DUOS - 1)

        def duo_ahead(b, j, d):
            return (b, j, d + AHEAD) if d + AHEAD < DUOS else (b + 1, 1 - j, d + AHEAD - DUOS)

        def duo_of(b, d):
            return b * DUOS + d

        with nc.Block() as block:
            @block.sync
            def _(sp):
                sp.wait_ge(consts, 1)
                for q in range(DUOS):
                    for h in range(2):
                        r = (2 * q + h) * 8
                        sp.dma_start(fc1[r:r + 8, q, h * MUL:(h + 1) * MUL], t["L0_gnn_fc_w1"]).then_inc(w_in, 16)
                for h in range(2):
                    s = slice(h * MUL, (h + 1) * MUL)
                    sp.dma_start(fc2[s, s], t["L0_gnn_fc_w2"]).then_inc(w_in, 16)
                    sp.dma_start(fc3r[s, :], t["L0_gnn_fc_w3"]).then_inc(w_in, 16)

                mix.load_weights(sp)

                def load(b, j):
                    sp.wait_ge(block_done.sem, block_done.of(b - 2))
                    for to, of in ((srcI, k.srcp), (dstI, k.dstp), (attr, k.attrp)):
                        sp.dma_start(to[:, j, :], of[bass.ds(b, 1)].rearrange("a p f -> p (a f)")).then_inc(loaded[j], 16)
                    sp.dma_start(sh[:, j].rearrange("p g f -> p (g f)"),
                                 k.shp[bass.ds(b, 1)].rearrange("a p f -> p (a f)")).then_inc(loaded[j], 16)
                    mix.load(sp, b, j)
                with sp.Fori(0, NB // 2) as i:
                    for j in range(2):
                        load(i * 2 + j, j)
                load(NB - 1, 0)

            @block.gpsimd
            def _(pool):
                nc.gpsimd.memset(zspare[:, :], 0.0)
                nc.gpsimd.memset(fc1[:, :, :], 0.0)
                nc.gpsimd.memset(fc2[:, :], 0.0)
                nc.gpsimd.memset(fc3[:, :, :], 0.0).then_inc(consts, 1)
                nc.gpsimd.iota(spare_i[:, :], pattern=[[0, 1]], base=N, channel_multiplier=1)
                nc.gpsimd.memset(later[:, :], 1.0).then_inc(consts, 1)
                pool.wait_ge(consts, 2)
                nc.gpsimd.affine_select(out=later[:, :], in_=later[:, :], compare_op=ALU.is_ge, fill=1024.0,
                                        base=0, pattern=[[-1, P]], channel_multiplier=1).then_inc(consts, 1)

                for j in range(TABLES):
                    for h in range(2):
                        rows_ = slice(N + h * P // 2, N + (h + 1) * P // 2)
                        pool.dma_start(k.tables[j][rows_, 0:MUL], zspare[:, :]).then_inc(added[j].sem, 16)

                def gather(j, g):
                    pool.indirect_dma_start(y[:, g % YSLOTS, :], None, k.ytab,
                                            bass.IndirectOffsetOnAxis(ap=dstI[:, j, g:g + 1], axis=0)).then_inc(y_in[g % YSLOTS].sem, 16)

                def scatter(b, j, d):
                    for u in range(2):
                        g = 2 * d + u
                        tab = g % TABLES
                        before = b * (G // TABLES) + (g // TABLES - 1)
                        pool.wait_ge(added[tab].sem, added[tab].of(before))
                        wait(pool, total_ready, b * G + g)
                        pool.sem_inc(paced, 1)
                        pool.indirect_dma_start(k.tables[tab], bass.IndirectOffsetOnAxis(ap=rows[:, j, g:g + 1], axis=0),
                                                total[:, g % OSLOTS, :], None, compute_op=ALU.add).then_inc(added[tab].sem, 16)

                def body(b, j, own, turn, first):
                    for d in range(DUOS):
                        wait(pool, msg_ready, duo_of(b, d))
                        pool.sem_inc(paced, 1)
                        for u in range(2):
                            g = 2 * d + u + YSLOTS
                            if g < G:
                                gather(j, g)
                            elif turn is not None:
                                if g == G:
                                    pool.wait_ge(loaded[1 - j], turn * 64 + 64)
                                    pool.sem_inc(paced, 1)
                                gather(1 - j, g - G)
                        if not (first and d == 0):
                            scatter(*duo_before(b, j, d))

                pool.wait_ge(loaded[0], 64)
                for g in range(YSLOTS):
                    gather(0, g)
                over_blocks(pool, body)
                scatter(NB - 1, 0, DUOS - 1)
                for j in range(TABLES):
                    n = (TILES - 1 - j) // TABLES
                    pool.wait_ge(added[j].sem, added[j].of(n))

            @block.scalar
            def _(act):
                for s in (wac_ready, total_ready, up_silu):
                    s.credit(act)
                mix.credit_act(act)

                def silu(to, of, scale, n):
                    wait(act, up, n)
                    nc.scalar.activation(to, of, ACT.Silu, scale=scale).then_inc(up_silu.sem, 1)

                def prep(b, j, step):
                    if step == 0:
                        wait(act, attr_turned, b)
                        nc.scalar.copy(attrT[:, :], pA[:, 0:P]).then_inc(attrT_ready.sem, 1)
                    elif step in (1, 2):
                        h = step - 1
                        silu(h1[:, h * 512:(h + 1) * 512], pH[:, :], 8 ** -0.5, b * 4 + h)
                    elif step in (3, 4):
                        h = step - 3
                        silu(h2[:, j, h * 512:(h + 1) * 512], pH[:, :], 0.125, b * 4 + 2 + h)

                def scaled(b, j, d):
                    n = duo_of(b, d)
                    wait(act, w_done, n)
                    act.wait_ge(msg_ready.sem, msg_ready.of(n - BUFS))
                    for u in range(2):
                        nc.scalar.activation(wac[:, d % BUFS, u, :], pW[d % 2][:, u * D:u * D + P], ACT.Copy,
                                             scale=sh[:, j, 2 * d + u, 0:1])
                    nc.scalar.copy(wbd[:, d % BUFS], pW[d % 2][:, :].rearrange("p (t w) -> p t w", t=2)[:, :, P:D]).then_inc(wac_ready.sem, 1)

                def totals(b, j, d):
                    if d == 0:
                        wait(act, rows_ready, b)
                    for u in range(2):
                        g = 2 * d + u
                        n = b * G + g
                        slot = g % OSLOTS
                        a = added[g % TABLES]
                        if not (isinstance(b, int) and b == 0 and g < OSLOTS):
                            act.wait_ge(a.sem, a.of(b * (G // TABLES) + (g // TABLES - OSLOTS // TABLES)))
                        nc.scalar.copy(total[:, slot, CNT:CNT + 1], cnt[:, j, g:g + 1])
                        wait(act, summed, n)
                        nc.scalar.copy(total[:, slot, 0:CNT], pO[u][:, :]).then_inc(total_ready.sem, 1)

                def body(b, j, own, turn, first):
                    for d in range(DUOS):
                        if turn is not None or d + AHEAD < DUOS:
                            scaled(*duo_ahead(b, j, d))
                        if not (first and d < 3):
                            mix.act_early(act, b, j, d)
                        if turn is not None and 1 <= d < 6:
                            prep(b + 1, 1 - j, d - 1)
                        if not (first and d == 0):
                            totals(*duo_before(b, j, d))
                        mix.act_late(act, b, j, d)
                act.wait_ge(fc_ready, 1)
                for s in range(5):
                    prep(0, 0, s)
                for d in range(AHEAD):
                    scaled(0, 0, d)
                over_blocks(act, body)
                totals(NB - 1, 0, DUOS - 1)
                for d in range(3):
                    mix.act_early(act, NB, 1, d)

            @block.vector
            def _(dve):
                for s in (block_done, equal, counted, ev_ready, te_ready, ev2_ready, ev3_ready, msg_ready):
                    s.credit(dve)
                dve.wait_ge(w_in, 16 * (2 * DUOS + 4))
                dve.wait_ge(consts, 3)
                for h in range(2):
                    s = slice(h * MUL, (h + 1) * MUL)
                    for to, of, by in ((0, 0, 0.125), (1, 2, 0.125), (2, 1, 0.125), (3, 3, 0.125 * 3 ** -0.5)):
                        m = nc.vector.tensor_scalar(fc3[s, h, to * MUL:(to + 1) * MUL], fc3r[s, of * MUL:(of + 1) * MUL], by, None, ALU.mult)
                nc.vector.tensor_copy(spare[:, :], spare_i[:, :]).then_inc(fc_ready, 1)
                dve.wait_ge(fc_ready, 1)

                def prep(b, j, step, turn):
                    if step == 0:
                        dve.wait_ge(loaded[j], turn * 64 + 64)
                        nc.vector.tensor_copy(srcf[:, j, :], srcI[:, j, :]).then_inc(src_float.sem, 1)
                    elif step in (3, 4, 5, 6):
                        q = step - 3
                        n = b * 4 + q
                        wait(dve, src_rows, n)
                        g = slice(4 * q, 4 * q + 4)
                        nc.vector.tensor_tensor(eq[:, j, g, :], pA[:, :].rearrange("p (g i) -> p g i", g=4),
                                                srcf[:, j, g].unsqueeze(2).to_broadcast([P, 4, P]), ALU.is_equal).then_inc(equal.sem, 1)
                        wait(dve, equal, n)
                        dve.wait_ge(counted.sem, counted.of(n - 1))
                        for u in range(4):
                            m = nc.vector.tensor_tensor_reduce(out=junk[:, u, :], in0=eq[:, j, 4 * q + u, :], in1=later[:, :],
                                                               scale=1.0, scalar=0.0, op0=ALU.mult, op1=ALU.add,
                                                               accum_out=cnt[:, j, 4 * q + u:4 * q + u + 1])
                        m.then_inc(counted.sem, 1)
                    elif step == 7:
                        wait(dve, counted, b * 4 + 3)
                        nc.vector.tensor_scalar(flag[:, :], cnt[:, j, :], 1000.0, None, ALU.is_ge)
                        nc.vector.tensor_tensor(away[:, :], spare[:, :].to_broadcast([P, G]), srcf[:, j, :], ALU.subtract).then_inc(flagged.sem, 1)
                        dve.wait_ge(flagged.sem, flagged.of(b * 2))
                        nc.vector.tensor_tensor(away[:, :], away[:, :], flag[:, :], ALU.mult).then_inc(flagged.sem, 1)
                        dve.wait_ge(flagged.sem, flagged.of(b * 2 + 1))
                        nc.vector.tensor_tensor(rows[:, j, :], srcf[:, j, :], away[:, :], ALU.add).then_inc(rows_ready.sem, 1)

                def messages(b, j, d):
                    n, par = duo_of(b, d), d % 2
                    s0 = (2 * d) % YSLOTS
                    for u in range(2):
                        dve.wait_ge(y_in[s0 + u].sem, y_in[s0 + u].of(b * (G // YSLOTS) + (2 * d) // YSLOTS))
                    yd = y[:, s0:s0 + 2, :]
                    es = yd[:, :, 0:MUL]
                    evd = yd[:, :, MUL:D].rearrange("p t (d u) -> p t d u", d=3)
                    shd = sh[:, j, 2 * d:2 * d + 2, 1:4].unsqueeze(3).to_broadcast([P, 2, 3, MUL])
                    ac, bd, m_ = wac[:, d % BUFS], wbd[:, d % BUFS], msg[:, d % BUFS]
                    dve.wait_ge(ev3_ready.sem, ev3_ready.of(n - 2))
                    nc.vector.tensor_tensor(ev[:, par], evd, shd, ALU.mult).then_inc(ev_ready.sem, 1)
                    wait(dve, wac_ready, n)
                    if not (isinstance(b, int) and b == 0 and d < BUFS):
                        dve.wait_ge(summed.sem, summed.of((n - BUFS) * 2 + 1))
                    nc.vector.tensor_tensor(te[:, par], bd[:, :, 0:MUL], es, ALU.mult).then_inc(te_ready.sem, 1)
                    wait(dve, ev_ready, n)
                    nc.vector.tensor_tensor(ev2[:, par], ev[:, par, :, 0, :], ev[:, par, :, 1, :], ALU.add).then_inc(ev2_ready.sem, 1)
                    nc.vector.tensor_tensor(m_[:, :, 0, 0, :], ac[:, :, 0:MUL], es, ALU.mult)
                    wait(dve, ev2_ready, n)
                    nc.vector.tensor_tensor(ev3[:, par], ev2[:, par], ev[:, par, :, 2, :], ALU.add).then_inc(ev3_ready.sem, 1)
                    nc.vector.tensor_tensor(m_[:, :, 1:4, 1, :], evd, ac[:, :, MUL:P].unsqueeze(2).to_broadcast([P, 2, 3, MUL]), ALU.mult)
                    wait(dve, te_ready, n)
                    nc.vector.tensor_tensor(m_[:, :, 1:4, 0, :], te[:, par].unsqueeze(2).to_broadcast([P, 2, 3, MUL]), shd, ALU.mult)
                    wait(dve, ev3_ready, n)
                    nc.vector.tensor_tensor(m_[:, :, 0, 1, :], bd[:, :, MUL:P], ev3[:, par], ALU.mult).then_inc(msg_ready.sem, 1)

                mix.credit_dve(dve)
                for s in range(8):
                    prep(0, 0, s, 0)
                def body(b, j, own, turn, first):
                    for d in range(DUOS):
                        messages(b, j, d)
                        if turn is not None:
                            for step in DVE_STEPS[d]:
                                prep(b + 1, 1 - j, step, turn)
                        mix.dve(dve, b, j, d, first)
                    wait(dve, msg_ready, duo_of(b, DUOS - 1))
                    dve.sem_inc(block_done.sem, 1)
                over_blocks(dve, body)
                for d in range(4):
                    mix.dve_behind(dve, NB, 1, d)

            @block.tensor
            def _(pe):
                for s in (w_done, summed):
                    s.credit(pe)
                mix.credit_pe(pe)
                pe.wait_ge(fc_ready, 1)

                def prep(b, j, step, turn):
                    if step == 0:
                        pe.wait_ge(loaded[j], turn * 64 + 64)
                        pe.wait_ge(equal.sem, equal.of(b * 4 - 1))
                        nc.tensor.transpose(pA[:, 0:P], attr[:, j, :], k.ident[:, :]).then_inc(attr_turned.sem, 1)
                    elif step in (1, 2):
                        h = step - 1
                        if h == 0:
                            wait(pe, attrT_ready, b)
                        pe.wait_ge(up_silu.sem, up_silu.of(b * 4 + h - 1))
                        for q in range(4):
                            m = nc.tensor.matmul(pH[:, q * P:(q + 1) * P], fc1[:, 4 * h + q, :], attrT[:, :], start=True, stop=True)
                        m.then_inc(up.sem, 1)
                    elif step in (3, 4):
                        h = step - 3
                        wait(pe, up_silu, b * 4 + h + 1)
                        nc.tensor.matmul(pH[:, :], fc2[:, :], h1[:, h * 512:(h + 1) * 512], start=True, stop=True).then_inc(up.sem, 1)
                    if step in (2, 3, 4, 5):
                        q = step - 2
                        if q == 0:
                            wait(pe, src_float, b)
                            wait(pe, attrT_ready, b)
                        else:
                            wait(pe, equal, b * 4 + q - 1)
                        for u in range(4):
                            m = nc.tensor.transpose(pA[:, u * P:(u + 1) * P],
                                                    srcf[:, j, 4 * q + u:4 * q + u + 1].to_broadcast([P, P]), k.ident[:, :])
                        m.then_inc(src_rows.sem, 1)

                def weights(b, j, d):
                    n = duo_of(b, d)
                    if d == 0 or d == 4:
                        wait(pe, up_silu, b * 4 + 2 + d // 4)
                    pe.wait_ge(wac_ready.sem, wac_ready.of(n - 2))
                    for u in range(2):
                        m = nc.tensor.matmul(pW[d % 2][:, u * D:(u + 1) * D], h2[:, j, d * P:(d + 1) * P], fc3[:, u, :], start=True, stop=True)
                    m.then_inc(w_done.sem, 1)

                def sums(b, j, d):
                    n = duo_of(b, d)
                    wait(pe, msg_ready, n)
                    for u in range(2):
                        tile = b * G + 2 * d + u
                        pe.wait_ge(total_ready.sem, total_ready.of(tile - 2))
                        nc.tensor.matmul(pO[u][:, :], eq[:, j, 2 * d + u, :],
                                         msg[:, d % BUFS, u].rearrange("p a b c -> p (a b c)"), start=True, stop=True).then_inc(summed.sem, 1)

                def body(b, j, own, turn, first):
                    for d in range(DUOS):
                        if turn is not None or d + AHEAD < DUOS:
                            weights(*duo_ahead(b, j, d))
                        if turn is not None and d:
                            prep(b + 1, 1 - j, d - 1, turn)
                        if not (first and d == 0):
                            sums(*duo_before(b, j, d))
                        mix.pe(pe, b, j, d, own)

                for s in range(8):
                    prep(0, 0, s, 0)
                for d in range(AHEAD):
                    weights(0, 0, d)
                over_blocks(pe, body)
                sums(NB - 1, 0, DUOS - 1)
        clear_semaphores(k)


class Mix:

    def __init__(self, k, c):
        self.k, nc, t, D = k, k.nc, k.t, k.D

        def sb(name, shape, dt=F32):
            return c.enter_context(nc.sbuf_tensor("m_" + name, shape, dt))

        def sem(name):
            return new_sem(k, c, "m_" + name)

        self.wm, self.w1, self.w2 = sb("wm", [P, 2, D]), sb("w1", [P, 4, 2 * D]), sb("w2", [P, 4, D])
        self.g1, self.b1 = sb("g1", [P, 2]), sb("b1", [P, 2])
        self.g2, self.b2 = sb("g2", [P, D]), sb("b2", [P, D])
        self.q, self.x = sb("q", [P, D]), sb("x", [P, 2, 2, P])
        self.den, self.rden, self.msgT = sb("den", [P, D]), sb("rden", [P, D]), sb("msgT", [P, 2, P])
        self.st, self.mv = sb("st", [P, 6]), sb("mv", [P, 2])
        self.ve, self.sd, self.rs, self.nb = sb("ve", [P, 1]), sb("sd", [P, 1]), sb("rs", [P, 1]), sb("nb", [P, 1])
        self.mn, self.mT, self.hid = sb("mn", [P, D]), sb("mT", [P, 2, P]), sb("hid", [P, 4, P])
        self.o1, self.o2 = sb("o1", [P, D]), self.den
        self.pM = [c.enter_context(nc.psum_tensor(f"m_pM{i}", [P, 512], F32)) for i in range(2)]
        self.w_in, self.q_in = sem("w_in"), Signal(sem("q_in"), 16)
        self.x_in = [sem("x_in0"), sem("x_in1")]
        self.WEIGHTS = 2 + 3 + 2 + 4 + 4 + 2
        s = lambda name, lead=0: Signal(sem(name), lead=lead)
        self.attended = s("attended", LEAD)
        self.den_eps, self.den_inv, self.msg_T = s("den_eps"), s("den_inv"), s("msg_T")
        self.projected, self.stat, self.aggr, self.var_eps = s("projected"), s("stat"), s("aggr"), s("var_eps")
        self.sqrt, self.rstd, self.shift = s("sqrt"), s("rstd"), s("shift")
        self.normed, self.turned, self.turned_ready = s("normed"), s("turned"), s("turned_ready")
        self.hidden, self.hid_ready, self.mlp_out = s("hidden", LEAD), s("hid_ready", LEAD), s("mlp_out")
        self.out_normed, self.gained, self.acc_msg = s("out_normed", LEAD), s("gained"), s("acc_msg")
        self.acc_done = s("acc_done", LEAD)
        self.aggregates = sem("aggregates")

    def load_weights(self, sp):
        t, D = self.k.t, self.k.D
        n = 0
        for to, of in ((self.wm, t["L0_mix_Wm"]),):
            for ch in range(2):
                sp.dma_start(to[:, ch, :], of[ch * P:(ch + 1) * P, :]).then_inc(self.w_in, 16)
        for chunk, p0, rows in permuted_rows(t["L0_mix_W1"][0:D, :]):
            sp.dma_start(self.w1[p0:p0 + MUL, chunk, :], rows).then_inc(self.w_in, 16)
        for ch in range(2):
            sp.dma_start(self.w1[:, 2 + ch, :], t["L0_mix_W1"][D + ch * P:D + (ch + 1) * P, :]).then_inc(self.w_in, 16)
        for ch in range(4):
            sp.dma_start(self.w2[:, ch, :], t["L0_mix_W2"][ch * P:(ch + 1) * P, :]).then_inc(self.w_in, 16)
        for to, of in ((self.g1, "L0_mix_g1"), (self.b1, "L0_mix_b1")):
            for ch in range(2):
                sp.dma_start(to[:, ch:ch + 1], t[of][ch * P:(ch + 1) * P].rearrange("(p a) -> p a", a=1)).then_inc(self.w_in, 16)
        for to, of in ((self.g2, "L0_mix_g2"), (self.b2, "L0_mix_b2")):
            sp.dma_start(to[:, :], t[of].partition_broadcast(P)).then_inc(self.w_in, 16)

    LOADS = 2 + 4 + 2 + 4 + 4 + 2

    def load(self, sp, n, j):
        sp.wait_ge(self.attended.sem, self.attended.of(n - 1))
        sp.dma_start(self.q[:, :], self.k.qtab[bass.ds(n, 1)].rearrange("a p d -> p (a d)")).then_inc(self.q_in.sem, 16)
        sp.wait_ge(self.hidden.sem, self.hidden.of(n * 2 - 3))
        sp.dma_start(self.x[:, j, :, :].rearrange("p a b -> p (a b)"),
                     self.k.xtab[bass.ds(n, 1)].rearrange("a p d -> p (a d)")).then_inc(self.x_in[j], 16)

    def credit_pe(self, pe):
        self.attended.credit(pe)
        self.hidden.credit(pe)
        pe.wait_ge(self.w_in, 16 * self.LOADS)

    def bank(self, j, product):
        return self.pM[(j + product) % 2]

    def pe(self, pe, n, j, d, x_turn):
        nc, k, D = self.k.nc, self.k, self.k.D
        if d == 0:
            pM = self.bank(j, 0)
            wait(pe, self.q_in, n)
            pe.wait_ge(self.hid_ready.sem, self.hid_ready.of(n * 2 - 1))
            for w, at in ((k.KS, 0), (k.KV, D)):
                for ch in range(2):
                    m = nc.tensor.matmul(pM[:, at + ch * P:at + (ch + 1) * P], w[:, ch, :], self.q[:, ch * P:(ch + 1) * P],
                                         start=True, stop=True)
            m.then_inc(self.attended.sem, 1)
        elif d == 2:
            pM = self.bank(j, 1)
            pe.wait_ge(self.out_normed.sem, self.out_normed.of(n - 1))
            wait(pe, self.msg_T, n)
            for ch in range(2):
                m = nc.tensor.matmul(pM[:, 0:D], self.msgT[:, ch, :], self.wm[:, ch, :], start=ch == 0, stop=ch == 1)
            m.then_inc(self.projected.sem, 1)
        elif d == 4:
            pM = self.bank(j, 2)
            wait(pe, self.normed, n)
            for ch in range(2):
                m = nc.tensor.transpose(pM[:, ch * P:(ch + 1) * P], self.mn[:, ch * P:(ch + 1) * P], k.ident[:, :])
            m.then_inc(self.turned.sem, 1)
        elif d in (5, 6):
            pM = self.bank(j, 3)
            wait(pe, self.turned_ready, n)
            if d == 5:
                pe.wait_ge(self.x_in[j], x_turn * 16 + 16)
            else:
                wait(pe, self.hid_ready, n * 2)
            for m_ in (2 * d - 10, 2 * d - 9):
                for ch in range(4):
                    x = self.x[:, j, ch, :] if ch < 2 else self.mT[:, ch - 2, :]
                    m = nc.tensor.matmul(pM[:, m_ * P:(m_ + 1) * P], self.w1[:, ch, m_ * P:(m_ + 1) * P], x,
                                         start=ch == 0, stop=ch == 3)
            m.then_inc(self.hidden.sem, 1)
        elif d == 7:
            pM = self.bank(j, 4)
            wait(pe, self.hid_ready, n * 2 + 1)
            for ch in range(4):
                m = nc.tensor.matmul(pM[:, 0:D], self.hid[:, ch, :], self.w2[:, ch, :], start=ch == 0, stop=ch == 3)
            m.then_inc(self.mlp_out.sem, 1)

    def statistics(self, dve, pM, n, which):
        nc, o = self.k.nc, n * 2 + which
        nc.vector.bn_stats(self.st[:, :], pM[:, 0:self.k.D]).then_inc(self.stat.sem, 1)
        wait(dve, self.stat, o)
        dve.sem_inc(self.aggregates, 1)
        nc.vector.bn_aggr(self.mv[:, :], self.st[:, :]).then_inc(self.aggr.sem, 1)
        wait(dve, self.aggr, o)
        nc.vector.tensor_scalar_add(self.ve[:, :], self.mv[:, 1:2], LN_EPS).then_inc(self.var_eps.sem, 1)

    def inverse(self, dve, n, which):
        nc, o = self.k.nc, n * 2 + which
        wait(dve, self.sqrt, o)
        nc.vector.reciprocal(self.rs[:, :], self.sd[:, :]).then_inc(self.rstd.sem, 1)
        wait(dve, self.rstd, o)
        nc.vector.scalar_tensor_tensor(out=self.nb[:, :], in0=self.mv[:, 0:1], scalar=-1.0, in1=self.rs[:, :],
                                       op0=ALU.mult, op1=ALU.mult).then_inc(self.shift.sem, 1)

    def credit_dve(self, dve):
        self.acc_done.credit(dve)
        dve.wait_ge(self.w_in, 16 * self.LOADS)

    def dve(self, dve, n, j, d, first):
        nc, k, D = self.k.nc, self.k, self.k.D
        if not first:
            self.dve_behind(dve, n, j, d)
        if d == 1:
            pM = self.bank(j, 0)
            wait(dve, self.attended, n)
            dve.wait_ge(self.acc_done.sem, self.acc_done.of(n - 2))
            nc.vector.tensor_scalar_add(self.den[:, :], pM[:, 0:D], ATT_EPS).then_inc(self.den_eps.sem, 1)
            wait(dve, self.den_eps, n)
            nc.vector.reciprocal(self.rden[:, :], self.den[:, :]).then_inc(self.den_inv.sem, 1)
            wait(dve, self.den_inv, n)
            nc.vector.tensor_tensor(self.msgT[:, :, :].rearrange("p a b -> p (a b)"), pM[:, D:2 * D], self.rden[:, :], ALU.mult).then_inc(self.msg_T.sem, 1)
        elif d == 2:
            wait(dve, self.projected, n)
            self.statistics(dve, self.bank(j, 1), n, 0)
        elif d == 3:
            self.inverse(dve, n, 0)

    def dve_behind(self, dve, n, j, d):
        nc, k = self.k.nc, self.k
        if d == 0:
            wait(dve, self.mlp_out, n - 1)
            self.statistics(dve, self.bank(1 - j, 4), n - 1, 1)
        elif d == 1:
            self.inverse(dve, n - 1, 1)
        elif d == 3:
            a = k.acc[:, bass.ds(n - 1, 1), :].rearrange("p a d -> p (a d)")
            wait(dve, self.out_normed, n - 1)
            nc.vector.tensor_tensor(a, a, self.b2[:, :], ALU.add).then_inc(self.gained.sem, 1)
            nc.vector.tensor_tensor(self.o2[:, :], self.o1[:, :], self.g2[:, :], ALU.mult).then_inc(self.acc_msg.sem, 1)
            wait(dve, self.gained, n - 1)
            wait(dve, self.acc_msg, n - 1)
            nc.vector.tensor_tensor(a, a, self.o2[:, :], ALU.add).then_inc(self.acc_done.sem, 1)

    def credit_act(self, act):
        self.out_normed.credit(act)
        self.hid_ready.credit(act)

    def act_early(self, act, n, j, d):
        nc, D = self.k.nc, self.k.D
        if d in (1, 3):
            wait(act, self.var_eps, n * 2 if d == 3 else n * 2 - 1)
            nc.scalar.activation(self.sd[:, :], self.ve[:, :], ACT.Sqrt).then_inc(self.sqrt.sem, 1)
        elif d == 2:
            wait(act, self.shift, n * 2 - 1)
            act.wait_ge(self.acc_done.sem, self.acc_done.of(n - 2))
            nc.scalar.activation(self.o1[:, :], self.bank(1 - j, 4)[:, 0:D], ACT.Identity, scale=self.rs[:, :], bias=self.nb[:, :]).then_inc(self.out_normed.sem, 1)
        elif d == 4:
            wait(act, self.shift, n * 2)
            nc.scalar.activation(self.mn[:, :], self.bank(j, 1)[:, 0:D], ACT.Identity, scale=self.rs[:, :], bias=self.nb[:, :]).then_inc(self.normed.sem, 1)
        elif d in (6, 7):
            self.relu(act, n, j, d - 6)

    def relu(self, act, n, j, half):
        wait(act, self.hidden, n * 2 + half)
        self.k.nc.scalar.activation(self.hid[:, 2 * half:2 * half + 2, :].rearrange("p a b -> p (a b)"),
                                    self.bank(j, 3)[:, 256 * half:256 * half + 256], ACT.Relu).then_inc(self.hid_ready.sem, 1)

    def act_late(self, act, n, j, d):
        nc = self.k.nc
        if d == 4:
            wait(act, self.turned, n)
            for ch in range(2):
                m = nc.scalar.activation(self.mT[:, ch, :], self.bank(j, 2)[:, ch * P:(ch + 1) * P], ACT.Identity,
                                         scale=self.g1[:, ch:ch + 1], bias=self.b1[:, ch:ch + 1])
            m.then_inc(self.turned_ready.sem, 1)


def stage_gnn(k):
    nc, t, NT, D, N = k.nc, k.t, k.NT, k.D, k.N
    T = 7
    NG = NT // T
    assert NG * T == NT and NG % 2 == 1 and T % 2 == 1 and NT * P <= N + P
    with ExitStack() as c:
        def sb(name, shape, dt=F32):
            return c.enter_context(nc.sbuf_tensor("g_" + name, shape, dt))

        def bank(name):
            return c.enter_context(nc.psum_tensor("g_" + name, [P, 512], F32))

        def sem(name):
            return new_sem(k, c, "g_" + name)

        parts, sc = sb("parts", [P, 2, TABLES, T, CNT + 1]), sb("sc", [P, 2, T, D])
        count, deg, root, dn = sb("count", [P, T]), sb("deg", [P, T]), sb("root", [P, T]), sb("dn", [P, T])
        nT = sb("nT", [P, 2, 4, P])
        w2r, w2 = sb("w2r", [P, 2, MUL]), sb("w2", [P, 2, MUL])
        gain = sb("gain", [P, D])
        gv = sb("gv", [P, MUL])
        o, o2, junk = sb("o", [P, 2, T, D]), sb("o2", [P, T, D]), sb("junk", [P, T, D])
        ms, mse, rms, inv = sb("ms", [P, 2, T]), sb("mse", [P, 2, T]), sb("rms", [P, 2, T]), sb("inv", [P, 2, T])
        pT, pG = [bank("pT0"), bank("pT1")], [bank("pG0"), bank("pG1")]
        w_in, loaded, ready = sem("w_in"), [sem("loaded0"), sem("loaded1")], sem("ready")
        sc_in = [sem("sc_in0"), sem("sc_in1")]
        s = lambda name: Signal(sem(name), lead=T + 1)
        summed, turned, turned_ready, through, with_sc = (s(x) for x in (
            "summed", "turned", "turned_ready", "through", "with_sc"))
        s = lambda name: Signal(sem(name), lead=LEAD)
        counted, degree, rooted, dn_ready, squares, eps_in, rms_ready, inv_ready, gained, added, stats_done = (s(x) for x in (
            "counted", "degree", "rooted", "dn_ready", "squares", "eps_in", "rms_ready", "inv_ready", "gained", "added", "stats_done"))

        def groups(eng, body):
            with eng.Fori(0, NG // 2) as i:
                for j in range(2):
                    body(i * 2 + j, j, i)
            body(NG - 1, 0, NG // 2)

        with nc.Block() as block:
            @block.sync
            def _(sp):
                def load(q, j, turn):
                    sp.wait_ge(turned.sem, turned.of(q * T - (T + 1)))
                    for tab in range(TABLES):
                        sp.dma_start(parts[:, j, tab], k.tables[tab][bass.ds(q * (T * P), T * P), :]
                                     .rearrange("(t p) c -> p t c", p=P)).then_inc(loaded[j], 16)
                    sp.wait_ge(squares.sem, squares.of(q - 2))
                    sp.dma_start(sc[:, j], k.sctab[bass.ds(q * (T * P), T * P), :].rearrange("(t p) c -> p t c", p=P)).then_inc(sc_in[j], 16)
                for to, of in ((0, "L0_gnn_w2_s"), (1, "L0_gnn_w2_v")):
                    sp.dma_start(w2r[:, to, :], t[of]).then_inc(w_in, 16)
                sp.dma_start(gain[:, 0:MUL], t["L0_gnn_g_s"].partition_broadcast(P)).then_inc(w_in, 16)
                sp.dma_start(gv[:, :], t["L0_gnn_g_v"].partition_broadcast(P)).then_inc(w_in, 16)
                groups(sp, load)

            @block.gpsimd
            def _(pool):
                for x in (summed, added):
                    x.credit(pool)

                def sum_parts(q, j, turn):
                    pool.wait_ge(loaded[j], (turn + 1) * 16 * TABLES)
                    for u in range(T):
                        a = parts[:, j, 0, u, 0:CNT]
                        nc.gpsimd.tensor_tensor(a, a, parts[:, j, 1, u, 0:CNT], ALU.add).then_inc(summed.sem, 1)

                def add_acc(q):
                    wait(pool, gained, q)
                    r = k.acc[:, bass.ds(q * T, T), :]
                    nc.gpsimd.tensor_tensor(r[:, :, 0:MUL], r[:, :, 0:MUL], o2[:, :, 0:MUL], ALU.add)
                    for d in range(3):
                        v = r[:, :, MUL + d::3]
                        m = nc.gpsimd.tensor_tensor(v, v, o2[:, :, (d + 1) * MUL:(d + 2) * MUL], ALU.add)
                    m.then_inc(added.sem, 1)
                sum_parts(0, 0, 0)
                with pool.Fori(0, NG // 2) as i:
                    for j in range(2):
                        sum_parts(i * 2 + (j + 1), 1 - j, i + j)
                        add_acc(i * 2 + j)
                add_acc(NG - 1)

            @block.vector
            def _(dve):
                for x in (counted, degree, dn_ready, with_sc, squares, eps_in, inv_ready, gained):
                    x.credit(dve)
                dve.wait_ge(w_in, 64)
                nc.vector.tensor_scalar(w2[:, :, :], w2r[:, :, :], (2.0 * MUL) ** -0.5, None, ALU.mult)
                nc.vector.tensor_copy(gain[:, MUL:D].rearrange("p (d u) -> p d u", d=3),
                                      gv[:, :].unsqueeze(1).to_broadcast([P, 3, MUL])).then_inc(ready, 1)
                dve.wait_ge(ready, 1)

                def degrees(q, j, turn):
                    dve.wait_ge(loaded[j], (turn + 1) * 16 * TABLES)
                    nc.vector.tensor_tensor(count[:, :], parts[:, j, 0, :, CNT], parts[:, j, 1, :, CNT], ALU.add).then_inc(counted.sem, 1)
                    wait(dve, counted, q)
                    nc.vector.tensor_scalar_max(deg[:, :], count[:, :], 1.0).then_inc(degree.sem, 1)

                def products(q, j, turn):
                    wait(dve, rooted, q)
                    nc.vector.reciprocal(dn[:, :], root[:, :]).then_inc(dn_ready.sem, 1)
                    wait(dve, dn_ready, q)
                    dve.wait_ge(sc_in[j], (turn + 1) * 16)
                    for u in range(T + 1):
                        if u < T:
                            wait(dve, through, q * T + u)
                            nc.vector.scalar_tensor_tensor(out=o[:, j, u, :], in0=pG[(u + j) % 2][:, 0:D], scalar=dn[:, u:u + 1], in1=sc[:, j, u, :],
                                                           op0=ALU.mult, op1=ALU.add).then_inc(with_sc.sem, 1)
                        if u > 0:
                            v = u - 1
                            wait(dve, with_sc, q * T + v)
                            for h, (a, b) in enumerate(((0, MUL), (MUL, D))):
                                m = nc.vector.tensor_tensor_reduce(out=junk[:, v, a:b], in0=o[:, j, v, a:b], in1=o[:, j, v, a:b], scale=1.0 / (b - a),
                                                                   scalar=0.0, op0=ALU.mult, op1=ALU.add, accum_out=ms[:, h, v:v + 1])
                    m.then_inc(squares.sem, 1)
                    wait(dve, squares, q)
                    nc.vector.tensor_scalar_add(mse[:, :, :], ms[:, :, :], LN_EPS).then_inc(eps_in.sem, 1)

                def gains(q, j):
                    wait(dve, rms_ready, q)
                    nc.vector.reciprocal(inv[:, :, :], rms[:, :, :]).then_inc(inv_ready.sem, 1)
                    wait(dve, inv_ready, q)
                    dve.wait_ge(added.sem, added.of(q - 1))
                    for u in range(T):
                        for h, (a, b) in enumerate(((0, MUL), (MUL, D))):
                            m = nc.vector.scalar_tensor_tensor(out=o2[:, u, a:b], in0=o[:, j, u, a:b], scalar=inv[:, h, u:u + 1],
                                                               in1=gain[:, a:b], op0=ALU.mult, op1=ALU.mult)
                    m.then_inc(gained.sem, 1)

                def statistics(q):
                    wait(dve, added, q)
                    for u in range(T):
                        n = q * T + u
                        nc.vector.bn_stats(k.stats[:, bass.ds(n, 1), :].rearrange("p a d -> p (a d)"),
                                           k.acc[:, bass.ds(n, 1), :].rearrange("p a d -> p (a d)"))
                degrees(0, 0, 0)
                products(0, 0, 0)
                with dve.Fori(0, NG // 2) as i:
                    for j in range(2):
                        q = i * 2 + j
                        degrees(i * 2 + (j + 1), 1 - j, i + j)
                        gains(q, j)
                        products(i * 2 + (j + 1), 1 - j, i + j)
                        statistics(q)
                gains(NG - 1, 0)
                statistics(NG - 1)

            @block.scalar
            def _(act):
                for x in (rooted, turned_ready, rms_ready):
                    x.credit(act)

                def body(q, j, turn):
                    wait(act, degree, q)
                    nc.scalar.activation(root[:, :], deg[:, :], ACT.Sqrt).then_inc(rooted.sem, 1)
                    for u in range(T):
                        n, p = q * T + u, (u + j) % 2
                        wait(act, turned, n)
                        act.wait_ge(through.sem, through.of(n - 2))
                        nc.scalar.copy(nT[:, p].rearrange("p a b -> p (a b)"), pT[p][:, :]).then_inc(turned_ready.sem, 1)
                    wait(act, eps_in, q)
                    nc.scalar.activation(rms[:, :, :], mse[:, :, :], ACT.Sqrt).then_inc(rms_ready.sem, 1)
                groups(act, body)

            @block.tensor
            def _(pe):
                for x in (turned, through):
                    x.credit(pe)
                pe.wait_ge(ready, 1)

                def turn_(q, j, u):
                    n, p = q * T + u, (u + j) % 2
                    wait(pe, summed, n)
                    pe.wait_ge(turned_ready.sem, turned_ready.of(n - 2))
                    for ch in range(4):
                        m = nc.tensor.transpose(pT[p][:, ch * P:(ch + 1) * P], parts[:, j, 0, u, ch * P:(ch + 1) * P], k.ident[:, :])
                    m.then_inc(turned.sem, 1)

                def product(q, j, u):
                    n, p = q * T + u, (u + j) % 2
                    wait(pe, turned_ready, n)
                    pe.wait_ge(with_sc.sem, with_sc.of(n - 2))
                    for ch in range(4):
                        m = nc.tensor.matmul(pG[p][:, ch * MUL:(ch + 1) * MUL], nT[:, p, ch, :], w2[:, min(ch, 1), :], start=True, stop=True)
                    m.then_inc(through.sem, 1)

                def body(q, j, turn):
                    for u in range(T + 1):
                        if u < T:
                            turn_(q, j, u)
                        if u > 0:
                            product(q, j, u - 1)
                groups(pe, body)
        clear_semaphores(k)


def stage_route(k):
    nc, t, NT, D, N = k.nc, k.t, k.NT, k.D, k.N
    X, CAP = k.NEXP, k.CAP
    with ExitStack() as c:
        def sb(name, shape, dt=F32):
            return c.enter_context(nc.sbuf_tensor("r_" + name, shape, dt))

        def bank(name):
            return c.enter_context(nc.psum_tensor("r_" + name, [P, 512], F32))

        def sem(name):
            return new_sem(k, c, "r_" + name)

        stats = k.stats
        mean, diff, vare = sb("mean", [P, NT]), sb("diff", [P, NT]), sb("vare", [P, NT])
        msum, vs, dsq, half = sb("msum", [P, NT]), sb("vs", [P, NT]), sb("dsq", [P, NT]), sb("half", [P, NT])
        rstd, shift = sb("rstd", [P, NT]), sb("shift", [P, NT])
        tn, ts, tT = sb("tn", [P, NT, D]), sb("ts", [P, 2, D]), sb("tT", [P, 2, 2, P])
        gw, gb = sb("gw", [P, 2, X]), sb("gb", [P, X])
        logits, ex, onehot = sb("logits", [P, NT, X]), sb("ex", [P, NT, X]), sb("onehot", [P, NT, X])
        score, pos, tmp = sb("score", [P, NT, X]), sb("pos", [P, NT, X]), sb("tmp", [P, NT, X])
        cum, tot = sb("cum", [P, NT, X]), sb("tot", [P, NT, X])
        top, total, best, place = sb("top", [P, NT]), sb("total", [P, NT]), sb("best", [P, NT]), sb("place", [P, NT])
        slot, kept, spare, over = sb("slot", [P, NT]), sb("kept", [P, NT]), sb("spare", [P, NT]), sb("over", [P, NT])
        valid, onest = sb("valid", [P, NT]), sb("onest", [P, NT])
        first, start = sb("first", [P, X]), sb("start", [P, X])
        first_i, start_i, spare_i = sb("first_i", [P, X], I32), sb("start_i", [P, X], I32), sb("spare_i", [P, NT], I32)
        rows = sb("rows", [P, NT], I32)
        before = sb("before", [P, P])
        pT, pL = [bank("pT0"), bank("pT1")], [bank("pL0"), bank("pL1")]
        pC, pS = bank("pC"), bank("pS")
        w_in, set_up, masks, dved, powered, ln_ready, expd, chosen, counted = (sem(x) for x in (
            "w_in", "set_up", "masks", "dved", "powered", "ln_ready", "expd", "chosen", "counted"))
        scattered, centred, rows_ready = sem("scattered"), sem("centred"), sem("rows_ready")
        s = lambda name: Signal(sem(name), lead=LEAD)
        ts_ready, tn_kept, turned, turned_ready, gated, logit = (s(x) for x in (
            "ts_ready", "tn_kept", "turned", "turned_ready", "gated", "logit"))

        def pairs(eng, *steps):
            with eng.Fori(0, NT // 2) as i:
                for step in steps:
                    for j in range(2):
                        step(i * 2 + j, j)
            for step in steps:
                step(NT - 1, 0)

        with nc.Block() as block:
            @block.sync
            def _(sp):
                for ch in range(2):
                    sp.dma_start(gw[:, ch, :], t["L0_ffn_gate_w"][ch * P:(ch + 1) * P, :]).then_inc(w_in, 16)
                sp.dma_start(gb[:, :], t["L0_ffn_gate_b"].partition_broadcast(P)).then_inc(w_in, 16)

            @block.gpsimd
            def _(pool):
                nc.gpsimd.memset(half[:, :], -0.5)
                nc.gpsimd.memset(onest[:, :], 1.0)
                nc.gpsimd.memset(valid[:, :], 1.0)
                nc.gpsimd.memset(before[:, :], 1.0)
                nc.gpsimd.iota(first_i[:, :], pattern=[[-1, X]], base=X, channel_multiplier=0)
                nc.gpsimd.iota(start_i[:, :], pattern=[[CAP, X]], base=0, channel_multiplier=0)
                nc.gpsimd.iota(spare_i[:, :], pattern=[[P, NT]], base=X * CAP, channel_multiplier=1).then_inc(set_up, 1)
                pool.wait_ge(set_up, 1)
                nc.gpsimd.affine_select(out=valid[:, :], in_=valid[:, :], compare_op=ALU.is_ge, fill=0.0,
                                        base=N - 1, pattern=[[-P, NT]], channel_multiplier=-1)
                nc.gpsimd.affine_select(out=before[:, :], in_=before[:, :], compare_op=ALU.is_ge, fill=0.0,
                                        base=-1, pattern=[[1, P]], channel_multiplier=-1).then_inc(masks, 1)
                pool.wait_ge(dved, 3)
                nc.gpsimd.tensor_tensor(rstd[:, :], vare[:, :], half[:, :], ALU.pow).then_inc(powered, 1)
                pool.wait_ge(rows_ready, 1)
                for n in range(NT):
                    pool.indirect_dma_start(k.buf, bass.IndirectOffsetOnAxis(ap=rows[:, n:n + 1], axis=0), tn[:, n, :], None)\
                        .then_inc(scattered, 16)
                pool.wait_ge(scattered, 16 * NT)

            @block.vector
            def _(dve):
                n_ = [0]

                def link(m):
                    n_[0] += 1
                    m.then_inc(dved, 1)
                    dve.wait_ge(dved, n_[0])

                nc.vector.tensor_tensor(msum[:, :], stats[:, :, 1], stats[:, :, 4], ALU.add)
                nc.vector.tensor_tensor(diff[:, :], stats[:, :, 1], stats[:, :, 4], ALU.subtract)
                link(nc.vector.tensor_tensor(vare[:, :], stats[:, :, 2], stats[:, :, 5], ALU.add))
                nc.vector.tensor_scalar(mean[:, :], msum[:, :], 0.5, None, ALU.mult)
                nc.vector.tensor_tensor(dsq[:, :], diff[:, :], diff[:, :], ALU.mult)
                link(nc.vector.tensor_scalar(vs[:, :], vare[:, :], 1.0 / D, LN_EPS, ALU.mult, ALU.add))
                link(nc.vector.scalar_tensor_tensor(out=vare[:, :], in0=dsq[:, :], scalar=0.25, in1=vs[:, :], op0=ALU.mult, op1=ALU.add))
                dve.wait_ge(set_up, 1)
                nc.vector.tensor_copy(first[:, :], first_i[:, :])
                nc.vector.tensor_copy(start[:, :], start_i[:, :])
                nc.vector.tensor_copy(spare[:, :], spare_i[:, :])
                for x in (tn_kept, logit):
                    x.credit(dve)
                dve.wait_ge(powered, 1)
                nc.vector.scalar_tensor_tensor(out=shift[:, :], in0=mean[:, :], scalar=-1.0, in1=rstd[:, :],
                                               op0=ALU.mult, op1=ALU.mult).then_inc(ln_ready, 1)
                dve.wait_ge(w_in, 48)

                def keep(n, j):
                    wait(dve, ts_ready, n)
                    nc.vector.tensor_copy(tn[:, bass.ds(n, 1), :].rearrange("p a d -> p (a d)"), ts[:, j, :]).then_inc(tn_kept.sem, 1)

                def bias(n, j):
                    wait(dve, gated, n)
                    nc.vector.tensor_tensor(logits[:, bass.ds(n, 1), :].rearrange("p a d -> p (a d)"), pL[j][:, 0:X], gb[:, :],
                                            ALU.add).then_inc(logit.sem, 1)
                pairs(dve, keep, bias)
                wait(dve, logit, NT - 1)

                def wide(a):
                    return a[:, :].unsqueeze(2).to_broadcast([P, NT, X])

                def over_tiles(a):
                    return a[:, :].unsqueeze(1).to_broadcast([P, NT, X])
                link(nc.vector.tensor_reduce(out=top[:, :], in_=logits[:, :, :], op=ALU.max, axis=AX))
                nc.vector.tensor_tensor(tmp[:, :, :], logits[:, :, :], wide(top), ALU.subtract).then_inc(centred, 1)
                dve.wait_ge(expd, 1)
                nc.vector.tensor_reduce(out=total[:, :], in_=ex[:, :, :], op=ALU.add, axis=AX)
                link(nc.vector.tensor_reduce(out=top[:, :], in_=ex[:, :, :], op=ALU.max, axis=AX))
                nc.vector.reciprocal(best[:, :], total[:, :])
                link(nc.vector.tensor_tensor(onehot[:, :, :], ex[:, :, :], wide(top), ALU.is_equal))
                link(nc.vector.tensor_tensor(score[:, :, :], onehot[:, :, :], over_tiles(first), ALU.mult))
                link(nc.vector.tensor_reduce(out=place[:, :], in_=score[:, :, :], op=ALU.max, axis=AX))
                link(nc.vector.tensor_tensor(onehot[:, :, :], score[:, :, :], wide(place), ALU.is_equal))
                nc.vector.tensor_tensor(best[:, :], best[:, :], top[:, :], ALU.mult)
                dve.wait_ge(masks, 1)
                nc.vector.tensor_tensor(onehot[:, :, :], onehot[:, :, :], wide(valid), ALU.mult).then_inc(chosen, 1)
                dve.wait_ge(counted, 1)
                link(nc.vector.tensor_copy(tot[:, :, :].rearrange("p a b -> p (a b)"), pS[:, 0:NT * X]))
                for e in range(X):
                    m = nc.vector.tensor_tensor_scan(cum[:, :, e], onest[:, :], tot[:, :, e], 0.0, ALU.mult, ALU.add)
                link(m)
                link(nc.vector.tensor_tensor(pos[:, :, :], cum[:, :, :], tot[:, :, :], ALU.subtract))
                link(nc.vector.tensor_tensor(pos[:, :, :].rearrange("p a b -> p (a b)"), pos[:, :, :].rearrange("p a b -> p (a b)"), pC[:, 0:NT * X], ALU.add))
                nc.vector.tensor_tensor(score[:, :, :], pos[:, :, :], over_tiles(start), ALU.add)
                link(nc.vector.tensor_tensor(tmp[:, :, :], pos[:, :, :], onehot[:, :, :], ALU.mult))
                nc.vector.tensor_reduce(out=place[:, :], in_=tmp[:, :, :], op=ALU.add, axis=AX)
                link(nc.vector.tensor_tensor(score[:, :, :], score[:, :, :], onehot[:, :, :], ALU.mult))
                link(nc.vector.tensor_reduce(out=slot[:, :], in_=score[:, :, :], op=ALU.add, axis=AX))
                nc.vector.tensor_scalar(kept[:, :], place[:, :], float(CAP), None, ALU.is_lt)
                nc.vector.tensor_scalar(over[:, :], place[:, :], float(1 - CAP), 0.0, ALU.add, ALU.max)
                link(nc.vector.tensor_tensor(total[:, :], slot[:, :], spare[:, :], ALU.subtract))
                link(nc.vector.tensor_tensor(kept[:, :], kept[:, :], valid[:, :], ALU.mult))
                link(nc.vector.tensor_tensor(total[:, :], total[:, :], kept[:, :], ALU.mult))
                nc.vector.tensor_tensor(k.weight[:, :], best[:, :], kept[:, :], ALU.mult)
                nc.vector.tensor_tensor(k.back[:, :], slot[:, :], over[:, :], ALU.subtract)
                nc.vector.tensor_tensor(rows[:, :], total[:, :], spare[:, :], ALU.add).then_inc(rows_ready, 1)

            @block.scalar
            def _(act):
                for x in (ts_ready, turned_ready):
                    x.credit(act)
                act.wait_ge(ln_ready, 1)

                def norm(n, j):
                    act.wait_ge(tn_kept.sem, tn_kept.of(n - 2))
                    act.wait_ge(turned.sem, turned.of(n - 2))
                    nc.scalar.activation(ts[:, j, :], k.acc[:, bass.ds(n, 1), :].rearrange("p a d -> p (a d)"), ACT.Identity,
                                         scale=rstd[:, bass.ds(n, 1)], bias=shift[:, bass.ds(n, 1)]).then_inc(ts_ready.sem, 1)

                def keep(n, j):
                    wait(act, turned, n)
                    act.wait_ge(gated.sem, gated.of(n - 2))
                    nc.scalar.copy(tT[:, j].rearrange("p a b -> p (a b)"), pT[j][:, 0:D]).then_inc(turned_ready.sem, 1)
                pairs(act, norm, keep)
                act.wait_ge(centred, 1)
                nc.scalar.activation(ex[:, :, :], tmp[:, :, :], ACT.Exp).then_inc(expd, 1)

            @block.tensor
            def _(pe):
                for x in (turned, gated):
                    x.credit(pe)
                pe.wait_ge(w_in, 48)

                def turn(n, j):
                    wait(pe, ts_ready, n)
                    pe.wait_ge(turned_ready.sem, turned_ready.of(n - 2))
                    for ch in range(2):
                        m = nc.tensor.transpose(pT[j][:, ch * P:(ch + 1) * P], ts[:, j, ch * P:(ch + 1) * P], k.ident[:, :])
                    m.then_inc(turned.sem, 1)

                def gate(n, j):
                    wait(pe, turned_ready, n)
                    pe.wait_ge(logit.sem, logit.of(n - 2))
                    for ch in range(2):
                        m = nc.tensor.matmul(pL[j][:, 0:X], tT[:, j, ch, :], gw[:, ch, :], start=ch == 0, stop=ch == 1)
                    m.then_inc(gated.sem, 1)
                pairs(pe, turn, gate)
                pe.wait_ge(chosen, 1)
                oh = onehot[:, :, :].rearrange("p a b -> p (a b)")
                nc.tensor.matmul(pC[:, 0:NT * X], before[:, :], oh, start=True, stop=True)
                nc.tensor.matmul(pS[:, 0:NT * X], k.ones[:, :], oh, start=True, stop=True).then_inc(counted, 1)
        clear_semaphores(k)


def stage_experts(k):
    nc, t, D, FF, CAP = k.nc, k.t, k.D, k.FF, k.CAP
    M = FF // P
    R = (CAP + P - 1) // P
    RL = CAP - (R - 1) * P
    SPLIT = (CAP + 1) // 2
    halves = ((0, SPLIT), (SPLIT, CAP))
    assert R == 8 and SPLIT <= 512
    with ExitStack() as c:
        def sb(name, shape, dt=F32):
            return c.enter_context(nc.sbuf_tensor("x_" + name, shape, dt))

        def bank(name):
            return c.enter_context(nc.psum_tensor("x_" + name, [P, 512], F32))

        def sem(name):
            return new_sem(k, c, "x_" + name)

        w1, w2 = sb("w1", [P, 2, 2, FF]), sb("w2", [P, 2, M, D])
        b1, b2 = sb("b1", [P, 2, M]), sb("b2", [P, 2, D])
        xb, xT = sb("xb", [P, 2, R, D]), sb("xT", [P, 2, 2, R * P])
        hid, yo = sb("hid", [P, M, CAP]), sb("yo", [P, R, D])
        pT, pH, pY = [bank("pT0"), bank("pT1")], [bank("pH0"), bank("pH1")], [bank("pY0"), bank("pY1")]
        loaded, zeroed = [sem("loaded0"), sem("loaded1")], sem("zeroed")
        s = lambda name, unit=1: Signal(sem(name), unit, lead=LEAD)
        turned, turned_ready = s("turned"), s("turned_ready")
        hidden, hid_ready = s("hidden"), s("hid_ready")
        out, row_tile = s("out"), s("row_tile")
        out_ready = s("out_ready")
        stores = sem("stores")
        stored = s("stored")
        LOADS = 2 + 1 + M + 1 + 2
        QT = R // 2

        def experts(eng, *steps):
            with eng.Fori(0, k.NEXP // 2) as i:
                for j in range(2):
                    for step in steps:
                        step(i * 2 + j, j, i)

        with nc.Block() as block:
            @block.sync
            def _(sp):
                sp.wait_ge(zeroed, 1)

                def load(e, j, turn):
                    sp.wait_ge(out_ready.sem, out_ready.of(e - 2))
                    for ch in range(2):
                        sp.dma_start(w1[:, j, ch, :], t["L0_ffn_w1"][bass.ds(e, 1), ch * P:(ch + 1) * P, :].rearrange("a p f -> p (a f)"))\
                            .then_inc(loaded[j], 16)
                    sp.dma_start(w2[:, j, :, :], t["L0_ffn_w2"][bass.ds(e, 1)].rearrange("a (m p) d -> p (a m) d", p=P)).then_inc(loaded[j], 16)
                    for m in range(M):
                        sp.dma_start(b1[:, j, m:m + 1], t["L0_ffn_b1"][bass.ds(e, 1), m * P:(m + 1) * P].rearrange("a p -> p a")).then_inc(loaded[j], 16)
                    sp.dma_start(b2[:, j, :], t["L0_ffn_b2"][bass.ds(e, 1), :].rearrange("a d -> (a d)").partition_broadcast(P)).then_inc(loaded[j], 16)
                    sp.dma_start(xb[:, j, 0:R - 1, :], k.buf[bass.ds(e * CAP, (R - 1) * P), :].rearrange("(r p) d -> p r d", p=P)).then_inc(loaded[j], 16)
                    sp.dma_start(xb[0:RL, j, R - 1, :], k.buf[bass.ds(e * CAP + (R - 1) * P, RL), :]).then_inc(loaded[j], 16)
                experts(sp, load)

            @block.gpsimd
            def _(pool):
                nc.gpsimd.memset(xb[:, :, R - 1, :], 0.0).then_inc(zeroed, 1)
                stored.credit(pool)

                def store(e, j, turn):
                    wait(pool, out_ready, e)
                    pool.dma_start(k.ybuf[bass.ds(e * CAP, (R - 1) * P), :].rearrange("(r p) d -> p r d", p=P), yo[:, 0:R - 1, :]).then_inc(stores, 16)
                    pool.dma_start(k.ybuf[bass.ds(e * CAP + (R - 1) * P, RL), :], yo[0:RL, R - 1, :]).then_inc(stores, 16)
                    pool.wait_ge(stores, (e + 1) * 32)
                    pool.sem_inc(stored.sem, 1)
                experts(pool, store)

            @block.scalar
            def _(act):
                hid_ready.credit(act)

                def hide(e, j, turn):
                    for m in range(M):
                        for h, (a, b) in enumerate(halves):
                            wait(act, hidden, e * 2 * M + 2 * m + h)
                            nc.scalar.activation(hid[:, m, a:b], pH[h][:, 0:b - a], ACT.Relu, bias=b1[:, j, m:m + 1]).then_inc(hid_ready.sem, 1)
                experts(act, hide)

            @block.vector
            def _(dve):
                for x in (turned_ready, row_tile, out_ready):
                    x.credit(dve)

                def turn(e, j, turn_):
                    for q in range(QT):
                        wait(dve, turned, e * QT + q)
                        nc.vector.tensor_copy(xT[:, j, :, 2 * q * P:(2 * q + 2) * P], pT[q % 2][:, :].rearrange("p (c r) -> p c r", c=2)).then_inc(turned_ready.sem, 1)

                def add_b2(e, j, turn_):
                    dve.wait_ge(stored.sem, stored.of(e - 1))
                    for r in range(R):
                        wait(dve, out, e * R + r)
                        nc.vector.tensor_tensor(yo[:, r, :], pY[r % 2][:, 0:D], b2[:, j, :], ALU.add).then_inc(row_tile.sem, 1)
                    wait(dve, row_tile, e * R + R - 1)
                    dve.sem_inc(out_ready.sem, 1)
                turn(0, 0, 0)
                with dve.Fori(0, k.NEXP // 2 - 1) as i:
                    for j in range(2):
                        turn(i * 2 + j + 1, 1 - j, i)
                        add_b2(i * 2 + j, j, i)
                turn(k.NEXP - 1, 1, 0)
                add_b2(k.NEXP - 2, 0, 0)
                add_b2(k.NEXP - 1, 1, 0)

            @block.tensor
            def _(pe):
                for x in (turned, hidden, out):
                    x.credit(pe)

                def turn(e, j, e_turn):
                    pe.wait_ge(loaded[j], (e_turn + 1) * 16 * LOADS)
                    for q in range(QT):
                        pe.wait_ge(turned_ready.sem, turned_ready.of(e * QT + q - 2))
                        for ch in range(2):
                            for r in range(2):
                                m = nc.tensor.transpose(pT[q % 2][:, (2 * ch + r) * P:(2 * ch + r + 1) * P],
                                                        xb[:, j, 2 * q + r, ch * P:(ch + 1) * P], k.ident[:, :])
                        m.then_inc(turned.sem, 1)

                def up(e, j):
                    wait(pe, turned_ready, e * QT + QT - 1)
                    for m_ in range(M):
                        for h, (a, b) in enumerate(halves):
                            pe.wait_ge(hid_ready.sem, hid_ready.of(e * 2 * M + 2 * m_ + h - 2))
                            for ch in range(2):
                                m = nc.tensor.matmul(pH[h][:, 0:b - a], w1[:, j, ch, m_ * P:(m_ + 1) * P], xT[:, j, ch, a:b], start=ch == 0, stop=ch == 1)
                            m.then_inc(hidden.sem, 1)

                def down(e, j):
                    wait(pe, hid_ready, e * 2 * M + 2 * M - 1)
                    for r in range(R):
                        n = P if r < R - 1 else RL
                        pe.wait_ge(row_tile.sem, row_tile.of(e * R + r - 2))
                        for m_ in range(M):
                            m = nc.tensor.matmul(pY[r % 2][0:n, 0:D], hid[:, m_, r * P:r * P + n], w2[:, j, m_, :], start=m_ == 0, stop=m_ == M - 1)
                        m.then_inc(out.sem, 1)
                turn(0, 0, 0)
                with pe.Fori(0, k.NEXP // 2 - 1) as i:
                    for j in range(2):
                        up(i * 2 + j, j)
                        turn(i * 2 + j + 1, 1 - j, i + j)
                        down(i * 2 + j, j)
                up(k.NEXP - 2, 0)
                turn(k.NEXP - 1, 1, k.NEXP // 2 - 1)
                down(k.NEXP - 2, 0)
                up(k.NEXP - 1, 1)
                down(k.NEXP - 1, 1)
        clear_semaphores(k)


def stage_combine(k):
    nc, NT, D, N, LAST = k.nc, k.NT, k.D, k.N, k.LAST
    T = 7
    NG = NT // T
    BY_POOL = 4
    with ExitStack() as c:
        def sb(name, shape, dt=F32):
            return c.enter_context(nc.sbuf_tensor("o_" + name, shape, dt))

        def sem(name):
            return new_sem(k, c, "o_" + name)

        y = sb("y", [P, NT, D])
        nan, inf, clamped = sb("nan", [P, T * D], I32), sb("inf", [P, T * D], I32), sb("clamped", [P, T * D])
        zeros = sb("zeros", [P, T * D])
        rows = sb("rows", [P, NT], I32)
        consts, rows_ready = sem("consts"), sem("rows_ready")
        got = [sem(f"got{q}") for q in range(NG)]
        s = lambda name: Signal(sem(name))
        scaled, flagged, no_inf, no_nan, added_pool, added_dve = (s(x) for x in (
            "scaled", "flagged", "no_inf", "no_nan", "added_pool", "added_dve"))
        stored = sem("stored")

        def group(a, q):
            return a[:, q * T:(q + 1) * T, :].rearrange("p t d -> p (t d)")

        with nc.Block() as block:
            @block.sync
            def _(sp):
                for q in range(NG):
                    if q < BY_POOL:
                        wait(sp, added_pool, q)
                    else:
                        wait(sp, added_dve, q - BY_POOL)
                    a, b = q * T, min((q + 1) * T, NT - 1)
                    sp.dma_start(k.out[a * P:b * P, :].rearrange("(t p) d -> p t d", p=P), k.acc[:, a:b, :]).then_inc(stored, 16)
                sp.dma_start(k.out[(NT - 1) * P:N, :], k.acc[0:LAST, NT - 1, :]).then_inc(stored, 16)
                sp.wait_ge(stored, 16 * (NG + 1))

            @block.gpsimd
            def _(pool):
                pool.wait_ge(rows_ready, 1)
                for n in range(NT):
                    pool.indirect_dma_start(y[:, n, :], None, k.ybuf, bass.IndirectOffsetOnAxis(ap=rows[:, n:n + 1], axis=0)).then_inc(got[n // T], 16)
                for q in range(BY_POOL):
                    wait(pool, no_nan, q)
                    a = group(k.acc, q)
                    nc.gpsimd.tensor_tensor(a, a, group(y, q), ALU.add).then_inc(added_pool.sem, 1)

            @block.scalar
            def _(act):
                for q in range(NG):
                    act.wait_ge(got[q], 16 * T)
                    for n in range(q * T, (q + 1) * T):
                        m = nc.scalar.activation(y[:, n, :], y[:, n, :], ACT.Copy, scale=k.weight[:, n:n + 1])
                    m.then_inc(scaled.sem, 1)

            @block.vector
            def _(dve):
                nc.vector.tensor_copy(rows[:, :], k.back[:, :]).then_inc(rows_ready, 1)
                nc.vector.memset(zeros[:, :], 0.0).then_inc(consts, 1)
                dve.wait_ge(consts, 1)
                for q in range(NG):
                    v = group(y, q)
                    wait(dve, scaled, q)
                    if q:
                        wait(dve, no_nan, q - 1)
                    nc.vector.tensor_tensor(nan[:, :], v, v, ALU.not_equal)
                    nc.vector.tensor_scalar(inf[:, :], v, 0.0, 0.0, ALU.mult, ALU.not_equal)
                    nc.vector.tensor_scalar(clamped[:, :], v, 1e4, -1e4, ALU.min, ALU.max).then_inc(flagged.sem, 1)
                    wait(dve, flagged, q)
                    nc.vector.copy_predicated(v, inf[:, :], clamped[:, :]).then_inc(no_inf.sem, 1)
                    wait(dve, no_inf, q)
                    nc.vector.copy_predicated(v, nan[:, :], zeros[:, :]).then_inc(no_nan.sem, 1)
                    if q >= BY_POOL:
                        wait(dve, no_nan, q)
                        a = group(k.acc, q)
                        nc.vector.tensor_tensor(a, a, v, ALU.add).then_inc(added_dve.sem, 1)


_INS = ['x', 'src', 'dst', 'edge_attr_4', 'edge_attr_8', 'L0_gnn_w1_s', 'L0_gnn_w1_v', 'L0_gnn_wsc_s', 'L0_gnn_wsc_v',
        'L0_gnn_w2_s', 'L0_gnn_w2_v', 'L0_gnn_fc_w1', 'L0_gnn_fc_w2', 'L0_gnn_fc_w3', 'L0_gnn_g_s', 'L0_gnn_g_v',
        'L0_mix_Wq', 'L0_mix_Wk', 'L0_mix_Wv', 'L0_mix_Wm', 'L0_mix_W1', 'L0_mix_W2', 'L0_mix_g1', 'L0_mix_b1',
        'L0_mix_g2', 'L0_mix_b2', 'L0_ffn_gate_w', 'L0_ffn_gate_b', 'L0_ffn_w1', 'L0_ffn_b1', 'L0_ffn_w2', 'L0_ffn_b2']


def kernel(**inputs):
    import numpy as _np
    import concourse.bacc as _bacc
    from concourse import mybir as _mybir
    from concourse.bass_utils import run_bass_kernel_spmd as _run

    nc = _bacc.Bacc("TRN2", target_bir_lowering=False, num_devices=1)
    arrays, aps = {}, {}
    for name in _INS:
        a = _np.ascontiguousarray(inputs[name])
        arrays[f"in_{name}"] = a
        aps[name] = nc.dram_tensor(f"in_{name}", a.shape, _mybir.dt.from_np(a.dtype), kind="ExternalInput").ap()
    out = nc.dram_tensor("out_0", inputs["x"].shape, _mybir.dt.float32, kind="ExternalOutput").ap()
    program(nc, aps, out)
    r = _run(nc, [arrays], core_ids=[0])
    return r.results[0]["out_0"]
```

```python
from contextlib import ExitStack

import concourse.bass as bass
from concourse import mybir

F32 = mybir.dt.float32
I32 = mybir.dt.int32
U32 = mybir.dt.uint32
ALU = mybir.AluOpType
ACT = mybir.ActivationFunctionType
AX = mybir.AxisListType.X

P = 128
MUL = 64
HEADS = 8
LN_EPS = 1e-5
ATT_EPS = 1e-6
LEAD = 4
G = 16
YSLOTS = 8
OSLOTS = 8
TABLES = 2
CNT = 8 * MUL


class Signal:

    def __init__(self, sem, unit=1, lead=0):
        self.sem, self.unit, self.lead = sem, unit, lead

    def credit(self, eng):
        eng.sem_inc(self.sem, self.lead * self.unit)

    def of(self, n):
        return (n + (self.lead + 1)) * self.unit


def wait(eng, signal, n):
    eng.wait_ge(signal.sem, signal.of(n))


class Kernel:
    pass


def program(nc, t, out):
    N, D = t["x"].shape
    E = t["src"].shape[0]
    NT = (N + P - 1) // P
    LAST = N - (NT - 1) * P
    NPAD = NT * P
    NB = (E + P * G - 1) // (P * G)
    ELAST = (E - (NB - 1) * P * G) // G
    assert NT == NB and NT % 2 == 1 and ELAST * G == E - (NB - 1) * P * G

    with ExitStack() as ctx:
        k = Kernel()
        k.used = []
        k.nc, k.t, k.out = nc, t, out
        k.N, k.D, k.E, k.NT, k.LAST, k.NB, k.ELAST = N, D, E, NT, LAST, NB, ELAST
        k.NEXP = t["L0_ffn_gate_w"].shape[1]
        k.FF = t["L0_ffn_w1"].shape[2]
        k.CAP = max(1, -(-5 * N // (4 * k.NEXP)))
        k.acc = ctx.enter_context(nc.sbuf_tensor("acc", [P, NT, D], F32))
        k.ident = ctx.enter_context(nc.sbuf_tensor("ident", [P, P], F32))
        k.ones = ctx.enter_context(nc.sbuf_tensor("ones", [P, P], F32))
        k.stats = ctx.enter_context(nc.sbuf_tensor("stats", [P, NT, 6], F32))
        k.weight = ctx.enter_context(nc.sbuf_tensor("weight", [P, NT], F32))
        k.back = ctx.enter_context(nc.sbuf_tensor("back", [P, NT], F32))
        k.ytab = dram(k, "ytab", [NPAD, D], F32)
        k.sctab = dram(k, "sctab", [NPAD, D], F32)
        k.xtab = dram(k, "xtab", [NT, P, D], F32)
        k.qtab = dram(k, "qtab", [NT, P, D], F32)
        k.tables = [dram(k, f"table{j}", [N + P, CNT + 1], F32) for j in range(TABLES)]
        k.srcp = dram(k, "srcp", [NB, P, G], I32)
        k.dstp = dram(k, "dstp", [NB, P, G], I32)
        k.shp = dram(k, "shp", [NB, P, G * 4], F32)
        k.attrp = dram(k, "attrp", [NB, P, G * 8], F32)
        k.buf = dram(k, "buf", [k.NEXP * k.CAP + NPAD, D], F32)
        k.ybuf = dram(k, "ybuf", [k.NEXP * k.CAP, D], F32)
        with ExitStack() as mix:
            k.KV = mix.enter_context(nc.sbuf_tensor("KV", [P, 2, P], F32))
            k.KS = mix.enter_context(nc.sbuf_tensor("KS", [P, 2, P], F32))
            edge_weights(k, mix)
            constants(k)
            stage_nodes(k)
            stage_edges(k)
        stage_gnn(k)
        with ExitStack() as experts:
            expert_weights(k, experts)
            stage_route(k)
            stage_experts(k)
        stage_combine(k)


def new_sem(k, c, name):
    k.used.append(c.enter_context(k.nc.semaphore(name)))
    return k.used[-1]


def clear_semaphores(k):
    with k.nc.Block() as block:
        @block.gpsimd
        def _(pool):
            for s in k.used:
                pool.sem_clear(s)
    k.used = []


def dram(k, name, shape, dt):
    return k.nc.dram_tensor(name, shape, dt).ap()


def permuted_rows(w):
    for d in range(3):
        yield (d + 1) // 2, MUL * ((d + 1) % 2), w[MUL + d::3]
    yield 0, 0, w[0:MUL]


def edge_weights(k, c):
    D, DUOS = k.D, G // 2

    def sb(name, shape):
        return c.enter_context(k.nc.sbuf_tensor(name, shape, F32))
    k.fc1, k.fc2, k.fc3r = sb("fc1", [P, DUOS, P]), sb("fc2", [P, P]), sb("fc3r", [P, D])
    k.wm, k.w1, k.w2 = sb("wm", [P, 2, D]), sb("w1", [P, 4, 2 * D]), sb("w2", [P, 4, D])
    k.g1, k.b1, k.g2, k.b2 = sb("g1", [P, 2]), sb("b1", [P, 2]), sb("g2", [P, D]), sb("b2", [P, D])


def load_edge_weights(k, eng, done):
    t, D, DUOS = k.t, k.D, G // 2
    loads = []
    for q in range(DUOS):
        for h in range(2):
            r = (2 * q + h) * 8
            loads.append((k.fc1[r:r + 8, q, h * MUL:(h + 1) * MUL], t["L0_gnn_fc_w1"]))
    for h in range(2):
        s = slice(h * MUL, (h + 1) * MUL)
        loads.append((k.fc2[s, s], t["L0_gnn_fc_w2"]))
        loads.append((k.fc3r[s, :], t["L0_gnn_fc_w3"]))
    for ch in range(2):
        loads.append((k.wm[:, ch, :], t["L0_mix_Wm"][ch * P:(ch + 1) * P, :]))
    for chunk, p0, rows in permuted_rows(t["L0_mix_W1"][0:D, :]):
        loads.append((k.w1[p0:p0 + MUL, chunk, :], rows))
    for ch in range(2):
        loads.append((k.w1[:, 2 + ch, :], t["L0_mix_W1"][D + ch * P:D + (ch + 1) * P, :]))
    for ch in range(4):
        loads.append((k.w2[:, ch, :], t["L0_mix_W2"][ch * P:(ch + 1) * P, :]))
    for to, of in ((k.g1, "L0_mix_g1"), (k.b1, "L0_mix_b1")):
        for ch in range(2):
            loads.append((to[:, ch:ch + 1], t[of][ch * P:(ch + 1) * P].rearrange("(p a) -> p a", a=1)))
    for to, of in ((k.g2, "L0_mix_g2"), (k.b2, "L0_mix_b2")):
        loads.append((to[:, :], t[of].partition_broadcast(P)))
    for to, of in loads:
        eng.dma_start(to, of).then_inc(done, 16)
    return len(loads)


def expert_weights(k, c):
    M = k.FF // P

    def sb(name, shape):
        return c.enter_context(k.nc.sbuf_tensor("x_" + name, shape, F32))
    k.xw1, k.xw2 = sb("w1", [P, 2, 2, k.FF]), sb("w2", [P, 2, M, k.D])
    k.xb1, k.xb2 = sb("b1", [P, 2, M]), sb("b2", [P, 2, k.D])


def load_expert_weights(k, sp, e, j, done):
    t, M = k.t, k.FF // P
    one = bass.ds(e, 1)
    loads = []
    for ch in range(2):
        loads.append((k.xw1[:, j, ch, :], t["L0_ffn_w1"][one, ch * P:(ch + 1) * P, :].rearrange("a p f -> p (a f)")))
    loads.append((k.xw2[:, j, :, :], t["L0_ffn_w2"][one].rearrange("a (m p) d -> p (a m) d", p=P)))
    for m in range(M):
        loads.append((k.xb1[:, j, m:m + 1], t["L0_ffn_b1"][one, m * P:(m + 1) * P].rearrange("a p -> p a")))
    loads.append((k.xb2[:, j, :], t["L0_ffn_b2"][one, :].rearrange("a d -> (a d)").partition_broadcast(P)))
    for to, of in loads:
        sp.dma_start(to, of).then_inc(done, 16)
    return len(loads)


def refine_rstd(nc, dve, rstd, var, tmp, done, n):
    nc.vector.scalar_tensor_tensor(out=tmp[:, :], in0=rstd[:, :], scalar=-0.5, in1=rstd[:, :], op0=ALU.mult, op1=ALU.mult).then_inc(done, 1)
    dve.wait_ge(done, n + 1)
    nc.vector.tensor_tensor(tmp[:, :], tmp[:, :], var[:, :], ALU.mult).then_inc(done, 1)
    dve.wait_ge(done, n + 2)
    nc.vector.scalar_tensor_tensor(out=rstd[:, :], in0=tmp[:, :], scalar=1.5, in1=rstd[:, :], op0=ALU.add, op1=ALU.mult).then_inc(done, 1)
    dve.wait_ge(done, n + 3)


def constants(k):
    nc = k.nc
    with ExitStack() as c:
        zeroed = new_sem(k, c, "c_zeroed")
        with nc.Block() as block:
            @block.gpsimd
            def _(pool):
                nc.gpsimd.memset(k.ident[:, :], 0.0)
                nc.gpsimd.memset(k.ones[:, :], 1.0).then_inc(zeroed, 1)
                pool.wait_ge(zeroed, 1)
                nc.gpsimd.affine_select(out=k.ident[:, :], in_=k.ident[:, :], compare_op=ALU.not_equal, fill=1.0,
                                        base=0, pattern=[[-1, P]], channel_multiplier=1)


def stage_nodes(k):
    nc, t, NT, D, N, LAST = k.nc, k.t, k.NT, k.D, k.N, k.LAST
    NB, ELAST = k.NB, k.ELAST
    acc, ident = k.acc, k.ident
    ZR = N + P
    FILL = 1024
    with ExitStack() as c:
        def sb(name, shape, dt=F32):
            return c.enter_context(nc.sbuf_tensor("n_" + name, shape, dt))

        def bank(name):
            return c.enter_context(nc.psum_tensor("n_" + name, [P, 512], F32))

        def sem(name):
            return new_sem(k, c, "n_" + name)

        stats, mv, mean = sb("stats", [P, NT, 6]), sb("mv", [P, NT, 4]), sb("mean", [P, NT])
        rstd, shift, grow = sb("rstd", [P, NT]), sb("shift", [P, NT]), sb("grow", [P, NT])
        vare, root = sb("vare", [P, NT]), sb("root", [P, NT])
        xp, xt = sb("xp", [P, 2, D]), sb("xt", [P, 2, 2, P])
        wq, wk, wv = sb("wq", [P, 2, D]), sb("wk", [P, 2, D]), sb("wv", [P, 2, D])
        wg = sb("wg", [P, 2, 2, P])
        low, exps = sb("low", [P, 2, D]), sb("exps", [P, 2, D])
        qlow, qexps, qf = sb("qlow", [P, 2, D]), sb("qexps", [P, 2, D]), sb("qf", [P, 2, D])
        kf, vf = sb("kf", [P, 2, D]), sb("vf", [P, 2, 2, P + 1])
        ysc = sb("ysc", [P, 2, 2, D])
        mask = sb("mask", [P, P])
        zer = sb("zer", [P, FILL])
        padsrc, padzero = sb("padsrc", [P, G], I32), sb("padzero", [P, G], I32)
        pT = [bank("pT0"), bank("pT1")]
        pK, pV, pQ, pY, pKV = bank("pK"), bank("pV"), bank("pQ"), bank("pY"), bank("pKV")

        XT = 7
        x_in = [sem(f"x_in{i}") for i in range(NT // XT)]
        w_in, w1_in, laid, ahead_in = sem("w_in"), sem("w1_in"), sem("laid"), sem("ahead_in")
        memsets, x_zeroed, rooted, statd, meant = (sem(s) for s in (
            "memsets", "x_zeroed", "rooted", "statd", "meant"))
        xp_ready = Signal(sem("xp_ready"), lead=LEAD)
        xT_done = Signal(sem("xT_done"), lead=LEAD)
        xt_ready = Signal(sem("xt_ready"), lead=LEAD)
        prod_k = Signal(sem("prod_k"), lead=LEAD)
        prod_v = Signal(sem("prod_v"), lead=LEAD)
        prod_q = Signal(sem("prod_q"), lead=LEAD)
        prod_y = Signal(sem("prod_y"), lead=LEAD)
        k_low, k_exp, k_feat = (Signal(sem(s), lead=LEAD) for s in ("k_low", "k_exp", "k_feat"))
        q_low, q_exp, q_feat = (Signal(sem(s), lead=LEAD) for s in ("q_low", "q_exp", "q_feat"))
        v_copied = Signal(sem("v_copied"), lead=LEAD)
        y_copied = Signal(sem("y_copied"), lead=LEAD)
        kv_added = Signal(sem("kv_added"), lead=LEAD)
        xt_stored = [Signal(sem(f"xt_stored{j}"), 16, lead=1) for j in range(2)]
        stored = [Signal(sem(f"stored{j}"), 48, lead=1) for j in range(2)]
        masked, ln_ready = sem("masked"), sem("ln_ready")

        def tiles(eng, tile):
            tile(0, 0, 0, 2)
            tile(1, 1, 0, 2)
            with eng.Fori(0, (NT - 5) // 2) as i:
                for j in range(2):
                    tile(i * 2 + (j + 2), j, i + 1, 2)
            for n in range(NT - 3, NT):
                tile(n, n % 2, n // 2, NT - 1 - n)

        def turn_after(j, turn):
            return turn + j

        edges = []
        whole = (NB - 1) * P * G
        for name, to, w in (("src", k.srcp, 1), ("dst", k.dstp, 1), ("edge_attr_4", k.shp, 4), ("edge_attr_8", k.attrp, 8)):
            src = t[name]
            flat = src[0:whole] if w == 1 else src[0:whole, :]
            rest = src[whole:k.E] if w == 1 else src[whole:k.E, :]
            pat = "(b p g) -> (b p) g" if w == 1 else "(b p g) f -> (b p) (g f)"
            edges.append((to[0:NB - 1].rearrange("b p f -> (b p) f"), flat.rearrange(pat, p=P, g=G)))
            pat = "(p g) -> p g" if w == 1 else "(p g) f -> p (g f)"
            edges.append((to[NB - 1, 0:ELAST, :], rest.rearrange(pat, g=G)))
        fills = []
        for tab in k.tables:
            flat = tab.rearrange("r c -> (r c)")
            total = ZR * (CNT + 1)
            chunk = P * FILL
            at = 0
            while at < total:
                n = min(chunk, total - at)
                w = n // P
                fills.append((flat[at:at + w * P].rearrange("(p w) -> p w", p=P), zer[:, 0:w]))
                at += w * P
                if n - w * P:
                    r = n - w * P
                    fills.append((flat[at:at + r].rearrange("(p w) -> p w", p=1), zer[0:1, 0:r]))
                    at += r
        LAID = len(edges) + len(fills) + 4

        with nc.Block() as block:
            @block.sync
            def _(sp):
                for i in range(NT // XT):
                    a, b = i * XT, min((i + 1) * XT, NT - 1)
                    sp.dma_start(acc[:, a:b, :], t["x"][a * P:b * P].rearrange("(t p) d -> p t d", p=P)).then_inc(x_in[i], 16)
                sp.wait_ge(x_zeroed, 1)
                sp.dma_start(acc[0:LAST, NT - 1, :], t["x"][(NT - 1) * P:N]).then_inc(x_in[-1], 16)

                def tile(n, j, turn, ahead):
                    wait(sp, xt_ready, n)
                    sp.dma_start(k.xtab[bass.ds(n, 1), :, :].rearrange("a p d -> p (a d)"),
                                 xt[:, j, :, :].rearrange("p a b -> p (a b)")).then_inc(xt_stored[j].sem, 16)
                    wait(sp, q_feat, n)
                    sp.dma_start(k.qtab[bass.ds(n, 1), :, :].rearrange("a p d -> p (a d)"), qf[:, j, :]).then_inc(stored[j].sem, 16)
                    wait(sp, y_copied, n)
                    rows = bass.ds(n * P, P)
                    sp.dma_start(k.ytab[rows, :], ysc[:, j, 0, :]).then_inc(stored[j].sem, 16)
                    sp.dma_start(k.sctab[rows, :], ysc[:, j, 1, :]).then_inc(stored[j].sem, 16)
                for x in stored + xt_stored:
                    x.credit(sp)
                tiles(sp, tile)
                for x in (stored, xt_stored):
                    wait(sp, x[0], NT // 2)
                    wait(sp, x[1], NT // 2 - 1)
                sp.wait_ge(laid, 16 * LAID)

            @block.gpsimd
            def _(pool):
                nc.gpsimd.memset(acc[:, NT - 1, :], 0.0).then_inc(x_zeroed, 1)
                nc.gpsimd.memset(wg[:, :, :, :], 0.0).then_inc(memsets, 1)
                nc.gpsimd.memset(vf[:, :, :, P:P + 1], 1.0)
                nc.gpsimd.memset(k.fc1[:, :, :], 0.0)
                nc.gpsimd.memset(k.fc2[:, :], 0.0)
                nc.gpsimd.memset(padzero[:, :], 0)
                nc.gpsimd.memset(zer[:, :], 0.0)
                nc.gpsimd.iota(padsrc[:, :], pattern=[[0, G]], base=N, channel_multiplier=1).then_inc(memsets, 1)
                pool.wait_ge(memsets, 2)
                for x in x_in[:-1]:
                    pool.wait_ge(x, 16)
                for to, of in edges:
                    pool.dma_start(to, of).then_inc(laid, 16)
                for i, (to, of) in enumerate(fills):
                    wait(pool, prod_k, i * (NT - 14) // len(fills))
                    pool.dma_start(to, of).then_inc(laid, 16)
                pool.dma_start(k.srcp[NB - 1, ELAST:P, :], padsrc[ELAST:P, :]).then_inc(laid, 16)
                pool.dma_start(k.dstp[NB - 1, ELAST:P, :], padzero[ELAST:P, :]).then_inc(laid, 16)
                pool.dma_start(k.shp[NB - 1, ELAST:P, :], zer[ELAST:P, 0:G * 4]).then_inc(laid, 16)
                pool.dma_start(k.attrp[NB - 1, ELAST:P, :], zer[ELAST:P, 0:G * 8]).then_inc(laid, 16)
                ahead_loads = load_edge_weights(k, pool, ahead_in)
                pool.wait_ge(ahead_in, 16 * ahead_loads)

            @block.vector
            def _(dve):
                for s in (xt_ready, k_low, k_feat, q_low, q_feat):
                    s.credit(dve)
                nc.vector.memset(mask[:, :], 0.0).then_inc(masked, 1)
                dve.wait_ge(masked, 1)
                for h in range(4):
                    m = nc.vector.memset(mask[32 * h:32 * h + 32, 32 * h:32 * h + 32], 1.0)
                m.then_inc(masked, 1)
                for n in range(NT):
                    if n % XT == 0:
                        dve.wait_ge(x_in[n // XT], 32 if n // XT == len(x_in) - 1 else 16)
                    nc.vector.bn_stats(stats[:, n, :], acc[:, n, :]).then_inc(statd, 1)
                dve.wait_ge(statd, NT)
                nc.vector.tensor_tensor(mv[:, :, 0], stats[:, :, 1], stats[:, :, 4], ALU.add)
                nc.vector.tensor_tensor(mv[:, :, 1], stats[:, :, 1], stats[:, :, 4], ALU.subtract)
                nc.vector.tensor_tensor(vare[:, :], stats[:, :, 2], stats[:, :, 5], ALU.add).then_inc(meant, 1)
                dve.wait_ge(meant, 1)
                nc.vector.tensor_scalar(mean[:, :], mv[:, :, 0], 0.5, None, ALU.mult)
                nc.vector.tensor_tensor(mv[:, :, 2], mv[:, :, 1], mv[:, :, 1], ALU.mult)
                nc.vector.tensor_scalar(mv[:, :, 3], vare[:, :], 1.0 / D, LN_EPS, ALU.mult, ALU.add).then_inc(meant, 1)
                dve.wait_ge(meant, 2)
                nc.vector.scalar_tensor_tensor(out=vare[:, :], in0=mv[:, :, 2], scalar=0.25, in1=mv[:, :, 3],
                                               op0=ALU.mult, op1=ALU.add).then_inc(meant, 1)
                dve.wait_ge(rooted, 1)
                nc.vector.reciprocal(rstd[:, :], root[:, :]).then_inc(meant, 1)
                dve.wait_ge(meant, 4)
                refine_rstd(nc, dve, rstd, vare, root, meant, 4)
                nc.vector.scalar_tensor_tensor(out=shift[:, :], in0=mean[:, :], scalar=-1.0, in1=rstd[:, :],
                                               op0=ALU.mult, op1=ALU.mult)
                nc.vector.tensor_scalar_add(grow[:, :], rstd[:, :], 1.0).then_inc(ln_ready, 1)
                dve.wait_ge(ln_ready, 1)

                def keep(n, j, turn):
                    wait(dve, xT_done, n)
                    dve.wait_ge(prod_y.sem, prod_y.of(n - 2))
                    dve.wait_ge(xt_stored[j].sem, xt_stored[j].of(turn - 1))
                    nc.vector.tensor_copy(xt[:, j, :, :], pT[j][:, 0:2 * P]).then_inc(xt_ready.sem, 1)

                def tile(n, j, turn, ahead):
                    wait(dve, prod_k, n)
                    dve.wait_ge(k_exp.sem, k_exp.of(n - 2))
                    nc.vector.tensor_scalar_min(low[:, j, :], pK[:, 0:D], 0.0).then_inc(k_low.sem, 1)
                    if ahead >= 1:
                        keep(n + 1, 1 - j, turn_after(j, turn))
                    wait(dve, prod_q, n)
                    dve.wait_ge(q_exp.sem, q_exp.of(n - 2))
                    nc.vector.tensor_scalar_min(qlow[:, j, :], pQ[:, 0:D], 0.0).then_inc(q_low.sem, 1)
                    wait(dve, k_exp, n)
                    dve.wait_ge(kv_added.sem, kv_added.of(n - 2))
                    nc.vector.scalar_tensor_tensor(out=kf[:, j, :], in0=pK[:, 0:D], scalar=0.0, in1=exps[:, j, :],
                                                   op0=ALU.max, op1=ALU.add).then_inc(k_feat.sem, 1)
                    wait(dve, xp_ready, n)
                    a = acc[:, bass.ds(n, 1), :].rearrange("p a d -> p (a d)")
                    nc.vector.tensor_scalar(a, a, grow[:, bass.ds(n, 1)], shift[:, bass.ds(n, 1)], ALU.mult, ALU.add)
                    wait(dve, q_exp, n)
                    dve.wait_ge(stored[j].sem, stored[j].of(turn - 1))
                    nc.vector.scalar_tensor_tensor(out=qf[:, j, :], in0=pQ[:, 0:D], scalar=0.0, in1=qexps[:, j, :],
                                                   op0=ALU.max, op1=ALU.add).then_inc(q_feat.sem, 1)
                keep(0, 0, 0)
                tiles(dve, tile)
                wait(dve, kv_added, NT - 1)
                dve.wait_ge(masked, 2)
                for ch in range(2):
                    nc.vector.tensor_tensor(k.KV[:, ch, :], pKV[:, ch * (P + 1):ch * (P + 1) + P], mask[:, :], ALU.mult)
                    nc.vector.tensor_scalar(k.KS[:, ch, :], mask[:, :], pKV[:, ch * (P + 1) + P:(ch + 1) * (P + 1)], None, ALU.mult)

            @block.scalar
            def _(act):
                for s in (xp_ready, k_exp, q_exp, v_copied, y_copied):
                    s.credit(act)
                for w, to in ((t["L0_mix_Wq"], wq), (t["L0_mix_Wk"], wk), (t["L0_mix_Wv"], wv)):
                    for chunk, p0, rows in permuted_rows(w):
                        act.dma_start(to[p0:p0 + MUL, chunk, :], rows).then_inc(w_in, 16)
                act.wait_ge(memsets, 1)
                for m, (s, v) in enumerate(((t["L0_gnn_w1_s"], t["L0_gnn_w1_v"]), (t["L0_gnn_wsc_s"], t["L0_gnn_wsc_v"]))):
                    for chunk in range(2):
                        for h in range(2):
                            w = s if (chunk, h) == (0, 0) else v
                            act.dma_start(wg[h * MUL:(h + 1) * MUL, chunk, m, h * MUL:(h + 1) * MUL], w).then_inc(w1_in, 16)
                act.wait_ge(meant, 3)
                nc.scalar.activation(root[:, :], vare[:, :], ACT.Sqrt).then_inc(rooted, 1)
                act.wait_ge(ln_ready, 1)

                def norm(n, j):
                    act.wait_ge(xT_done.sem, xT_done.of(n - 2))
                    a = acc[:, bass.ds(n, 1), :].rearrange("p a d -> p (a d)")
                    scale, bias = rstd[:, bass.ds(n, 1)], shift[:, bass.ds(n, 1)]
                    nc.scalar.activation(xp[:, j, 0:MUL], a[:, 0:MUL], ACT.Identity, scale=scale, bias=bias)
                    nc.scalar.activation(xp[:, j, MUL:D].rearrange("p (d u) -> p d u", d=3),
                                         a[:, MUL:D].rearrange("p (u d) -> p d u", d=3),
                                         ACT.Identity, scale=scale, bias=bias).then_inc(xp_ready.sem, 1)

                def tile(n, j, turn, ahead):
                    if ahead >= 2:
                        norm(n + 2, j)
                    wait(act, k_low, n)
                    act.wait_ge(k_feat.sem, k_feat.of(n - 2))
                    nc.scalar.activation(exps[:, j, :], low[:, j, :], ACT.Exp).then_inc(k_exp.sem, 1)
                    wait(act, q_low, n)
                    act.wait_ge(q_feat.sem, q_feat.of(n - 2))
                    nc.scalar.activation(qexps[:, j, :], qlow[:, j, :], ACT.Exp).then_inc(q_exp.sem, 1)
                    wait(act, prod_v, n)
                    act.wait_ge(kv_added.sem, kv_added.of(n - 2))
                    nc.scalar.copy(vf[:, j, :, 0:P], pV[:, 0:D].rearrange("p (c v) -> p c v", c=2)).then_inc(v_copied.sem, 1)
                    wait(act, prod_y, n)
                    act.wait_ge(stored[j].sem, stored[j].of(turn - 1))
                    nc.scalar.activation(ysc[:, j, :, :].rearrange("p m (c v) -> p c m v", c=2),
                                         pY[:, :].rearrange("p (c m v) -> p c m v", c=2, m=2), ACT.Copy, scale=MUL ** -0.5).then_inc(y_copied.sem, 1)
                for n in range(2):
                    norm(n, n)
                tiles(act, tile)

            @block.tensor
            def _(pe):
                for s in (xT_done, prod_k, prod_v, prod_q, prod_y, kv_added):
                    s.credit(pe)
                pe.wait_ge(memsets, 1)
                pe.wait_ge(w_in, 16 * 12)
                pe.wait_ge(w1_in, 16 * 8)
                pe.wait_ge(memsets, 2)
                nc.tensor.matmul(pKV[:, 0:2 * (P + 1)], zer[:, 0:P], zer[:, 0:2 * (P + 1)], start=True, stop=True)

                def transpose(n, j):
                    wait(pe, xp_ready, n)
                    pe.wait_ge(xt_ready.sem, xt_ready.of(n - 2))
                    for ch in range(2):
                        m = nc.tensor.transpose(pT[j][:, ch * P:(ch + 1) * P], xp[:, j, ch * P:(ch + 1) * P], ident[:, :])
                    m.then_inc(xT_done.sem, 1)

                def add_kv(n, j, rows):
                    wait(pe, k_feat, n)
                    wait(pe, v_copied, n)
                    for ch in range(2):
                        m = nc.tensor.matmul(pKV[:, ch * (P + 1):(ch + 1) * (P + 1)], kf[0:rows, j, ch * P:(ch + 1) * P],
                                             vf[0:rows, j, ch, :], start=False, stop=True, skip_group_check=True)
                    m.then_inc(kv_added.sem, 1)

                def tile(n, j, turn, ahead):
                    if ahead >= 1:
                        transpose(n + 1, 1 - j)
                    wait(pe, xt_ready, n)
                    pe.wait_ge(k_feat.sem, k_feat.of(n - 1))
                    for ch in range(2):
                        m = nc.tensor.matmul(pK[:, 0:D], xt[:, j, ch, :], wk[:, ch, :], start=ch == 0, stop=ch == 1)
                    m.then_inc(prod_k.sem, 1)
                    pe.wait_ge(q_feat.sem, q_feat.of(n - 1))
                    for m_ in range(2):
                        for ch in range(2):
                            m = nc.tensor.matmul(pQ[:, m_ * P:(m_ + 1) * P], wq[:, ch, m_ * P:(m_ + 1) * P], xt[:, j, ch, :],
                                                 start=ch == 0, stop=ch == 1)
                    m.then_inc(prod_q.sem, 1)
                    if not (isinstance(n, int) and n == 0):
                        add_kv(n - 1, 1 - j, P)
                    for ch in range(2):
                        m = nc.tensor.matmul(pV[:, 0:D], xt[:, j, ch, :], wv[:, ch, :], start=ch == 0, stop=ch == 1)
                    m.then_inc(prod_v.sem, 1)
                    pe.wait_ge(y_copied.sem, y_copied.of(n - 1))
                    for ch in range(2):
                        m = nc.tensor.matmul(pY[:, ch * D:(ch + 1) * D], xt[:, j, ch, :],
                                             wg[:, ch, :, :].rearrange("p m v -> p (m v)"), start=True, stop=True)
                    m.then_inc(prod_y.sem, 1)
                transpose(0, 0)
                tiles(pe, tile)
                add_kv(NT - 1, 0, LAST)
        clear_semaphores(k)


def stage_edges(k):
    nc, NB, N, D = k.nc, k.NB, k.N, k.D
    DUOS = G // 2
    TILES = NB * G
    AHEAD = 2
    BUFS = 4
    with ExitStack() as c:
        def sb(name, shape, dt=F32):
            return c.enter_context(nc.sbuf_tensor("e_" + name, shape, dt))

        def bank(name):
            return c.enter_context(nc.psum_tensor("e_" + name, [P, 512], F32))

        def sem(name):
            return new_sem(k, c, "e_" + name)

        srcI, dstI = sb("srcI", [P, 2, G], I32), sb("dstI", [P, 2, G], I32)
        sh, attr = sb("sh", [P, 2, G, 4]), sb("attr", [P, 2, G * 8])
        srcf, eq = sb("srcf", [P, 2, G]), sb("eq", [P, 2, G, P])
        cnt, rows = sb("cnt", [P, 2, G]), sb("rows", [P, 2, G], I32)
        flag, away = sb("flag", [P, G]), sb("away", [P, G])
        spare, spare_i = sb("spare", [P, 1]), sb("spare_i", [P, 1], I32)
        later = sb("later", [P, P])
        junk = sb("junk", [P, 4, P])
        fc1, fc2, fc3, fc3r = k.fc1, k.fc2, sb("fc3", [P, 2, D]), k.fc3r
        attrT, h1, h2 = sb("attrT", [P, P]), sb("h1", [P, DUOS * P]), sb("h2", [P, 2, DUOS * P])
        y = sb("y", [P, YSLOTS, D])
        wac = sb("wac", [P, BUFS, 2, P])
        wbd = sb("wbd", [P, BUFS, 2, P])
        te, ev = sb("te", [P, 2, 2, MUL]), sb("ev", [P, 2, 2, 3, MUL])
        ev2 = sb("ev2", [P, 2, 2, MUL])
        ev3 = sb("ev3", [P, 2, 2, MUL])
        msg = sb("msg", [P, BUFS, 2, 4, 2, MUL])
        total = sb("total", [P, OSLOTS, CNT + 1])
        pA, pH, pW, pO = bank("pA"), bank("pH"), [bank("pW0"), bank("pW1")], [bank("pO0"), bank("pO1")]

        mix = Mix(k, c)
        consts, fc_ready = sem("consts"), sem("fc_ready")
        paced = sem("paced")
        loaded = [sem("loaded0"), sem("loaded1")]
        src_float = Signal(sem("src_float"))
        attr_turned, attrT_ready = Signal(sem("attr_turned")), Signal(sem("attrT_ready"))
        up = Signal(sem("up"))
        up_silu = Signal(sem("up_silu"), lead=LEAD)
        src_rows = Signal(sem("src_rows"))
        equal = Signal(sem("equal"), lead=LEAD)
        counted, flagged, rows_ready = Signal(sem("counted"), lead=LEAD), Signal(sem("flagged")), Signal(sem("rows_ready"))
        block_done = Signal(sem("block_done"), lead=LEAD)
        w_done = Signal(sem("w_done"), lead=LEAD)
        wac_ready = Signal(sem("wac_ready"), lead=LEAD)
        y_in = [Signal(sem(f"y_in{s}"), 16) for s in range(YSLOTS)]
        ev_ready, te_ready, ev2_ready, ev3_ready = (Signal(sem(s), lead=LEAD) for s in ("ev_ready", "te_ready", "ev2_ready", "ev3_ready"))
        msg_ready = Signal(sem("msg_ready"), lead=LEAD)
        summed = Signal(sem("summed"), lead=LEAD)
        total_ready = Signal(sem("total_ready"), lead=LEAD)
        added = [Signal(sem(f"added{j}"), 16, lead=2) for j in range(TABLES)]
        ZW = 8 * -(-k.NEXP * k.CAP * D // (P * NB * 8))
        zeros, zeros_in = sb("zeros", [P, ZW]), sem("zeros_in")
        zspare = sb("zspare", [P // 2, MUL])
        DVE_STEPS = [(), (0,), (), (), (3,), (4,), (5,), (6, 7)]

        def over_blocks(eng, body):
            body(0, 0, 0, 0, True)
            with eng.Fori(0, (NB - 3) // 2) as i:
                for j in range(2):
                    body(i * 2 + (j + 1), (j + 1) % 2, i + j, i + 1, False)
            body(NB - 2, 1, (NB - 3) // 2, (NB - 1) // 2, False)
            body(NB - 1, 0, (NB - 1) // 2, None, False)

        def duo_before(b, j, d):
            return (b, j, d - 1) if d else (b - 1, 1 - j, DUOS - 1)

        def duo_ahead(b, j, d):
            return (b, j, d + AHEAD) if d + AHEAD < DUOS else (b + 1, 1 - j, d + AHEAD - DUOS)

        def duo_of(b, d):
            return b * DUOS + d

        with nc.Block() as block:
            @block.sync
            def _(sp):
                sp.wait_ge(consts, 1)
                rows = k.NEXP * k.CAP
                flat = k.buf[0:rows].rearrange("r d -> (r d)").rearrange("(p w) -> p w", p=P)

                def load(b, j):
                    sp.wait_ge(block_done.sem, block_done.of(b - 2))
                    for to, of in ((srcI, k.srcp), (dstI, k.dstp), (attr, k.attrp)):
                        sp.dma_start(to[:, j, :], of[bass.ds(b, 1)].rearrange("a p f -> p (a f)")).then_inc(loaded[j], 16)
                    sp.dma_start(sh[:, j].rearrange("p g f -> p (g f)"),
                                 k.shp[bass.ds(b, 1)].rearrange("a p f -> p (a f)")).then_inc(loaded[j], 16)
                    mix.load(sp, b, j)
                with sp.Fori(0, NB // 2) as i:
                    for j in range(2):
                        load(i * 2 + j, j)
                        sp.dma_start(flat[:, bass.ds(i * (2 * ZW) + j * ZW, ZW)], zeros[:, :]).then_inc(zeros_in, 16)
                load(NB - 1, 0)
                sp.dma_start(flat[:, (NB - 1) * ZW:], zeros[:, 0:flat.shape[1] - (NB - 1) * ZW]).then_inc(zeros_in, 16)
                sp.wait_ge(zeros_in, 16 * NB)

            @block.gpsimd
            def _(pool):
                nc.gpsimd.memset(zspare[:, :], 0.0)
                nc.gpsimd.memset(zeros[:, :], 0.0)
                nc.gpsimd.memset(fc3[:, :, :], 0.0).then_inc(consts, 1)
                nc.gpsimd.iota(spare_i[:, :], pattern=[[0, 1]], base=N, channel_multiplier=1)
                nc.gpsimd.memset(later[:, :], 1.0).then_inc(consts, 1)
                pool.wait_ge(consts, 2)
                nc.gpsimd.affine_select(out=later[:, :], in_=later[:, :], compare_op=ALU.is_ge, fill=1024.0,
                                        base=0, pattern=[[-1, P]], channel_multiplier=1).then_inc(consts, 1)

                for j in range(TABLES):
                    for h in range(2):
                        rows_ = slice(N + h * P // 2, N + (h + 1) * P // 2)
                        pool.dma_start(k.tables[j][rows_, 0:MUL], zspare[:, :]).then_inc(added[j].sem, 16)

                def gather(j, g):
                    pool.indirect_dma_start(y[:, g % YSLOTS, :], None, k.ytab,
                                            bass.IndirectOffsetOnAxis(ap=dstI[:, j, g:g + 1], axis=0)).then_inc(y_in[g % YSLOTS].sem, 16)

                def scatter(b, j, d):
                    for u in range(2):
                        g = 2 * d + u
                        tab = g % TABLES
                        before = b * (G // TABLES) + (g // TABLES - 1)
                        pool.wait_ge(added[tab].sem, added[tab].of(before))
                        wait(pool, total_ready, b * G + g)
                        pool.sem_inc(paced, 1)
                        pool.indirect_dma_start(k.tables[tab], bass.IndirectOffsetOnAxis(ap=rows[:, j, g:g + 1], axis=0),
                                                total[:, g % OSLOTS, :], None, compute_op=ALU.add).then_inc(added[tab].sem, 16)

                def body(b, j, own, turn, first):
                    for d in range(DUOS):
                        wait(pool, msg_ready, duo_of(b, d))
                        pool.sem_inc(paced, 1)
                        for u in range(2):
                            g = 2 * d + u + YSLOTS
                            if g < G:
                                gather(j, g)
                            elif turn is not None:
                                if g == G:
                                    pool.wait_ge(loaded[1 - j], turn * 64 + 64)
                                    pool.sem_inc(paced, 1)
                                gather(1 - j, g - G)
                        if not (first and d == 0):
                            scatter(*duo_before(b, j, d))

                pool.wait_ge(loaded[0], 64)
                for g in range(YSLOTS):
                    gather(0, g)
                over_blocks(pool, body)
                scatter(NB - 1, 0, DUOS - 1)
                for j in range(TABLES):
                    n = (TILES - 1 - j) // TABLES
                    pool.wait_ge(added[j].sem, added[j].of(n))

            @block.scalar
            def _(act):
                for s in (wac_ready, total_ready, up_silu):
                    s.credit(act)
                mix.credit_act(act)

                def silu(to, of, scale, n):
                    wait(act, up, n)
                    nc.scalar.activation(to, of, ACT.Silu, scale=scale).then_inc(up_silu.sem, 1)

                def prep(b, j, step):
                    if step == 0:
                        wait(act, attr_turned, b)
                        nc.scalar.copy(attrT[:, :], pA[:, 0:P]).then_inc(attrT_ready.sem, 1)
                    elif step in (1, 2):
                        h = step - 1
                        silu(h1[:, h * 512:(h + 1) * 512], pH[:, :], 8 ** -0.5, b * 4 + h)
                    elif step in (3, 4):
                        h = step - 3
                        silu(h2[:, j, h * 512:(h + 1) * 512], pH[:, :], 0.125, b * 4 + 2 + h)

                def scaled(b, j, d):
                    n = duo_of(b, d)
                    wait(act, w_done, n)
                    act.wait_ge(msg_ready.sem, msg_ready.of(n - BUFS))
                    for u in range(2):
                        nc.scalar.activation(wac[:, d % BUFS, u, :], pW[d % 2][:, u * D:u * D + P], ACT.Copy,
                                             scale=sh[:, j, 2 * d + u, 0:1])
                    nc.scalar.copy(wbd[:, d % BUFS], pW[d % 2][:, :].rearrange("p (t w) -> p t w", t=2)[:, :, P:D]).then_inc(wac_ready.sem, 1)

                def totals(b, j, d):
                    if d == 0:
                        wait(act, rows_ready, b)
                    for u in range(2):
                        g = 2 * d + u
                        n = b * G + g
                        slot = g % OSLOTS
                        a = added[g % TABLES]
                        if not (isinstance(b, int) and b == 0 and g < OSLOTS):
                            act.wait_ge(a.sem, a.of(b * (G // TABLES) + (g // TABLES - OSLOTS // TABLES)))
                        nc.scalar.copy(total[:, slot, CNT:CNT + 1], cnt[:, j, g:g + 1])
                        wait(act, summed, n)
                        nc.scalar.copy(total[:, slot, 0:CNT], pO[u][:, :]).then_inc(total_ready.sem, 1)

                def body(b, j, own, turn, first):
                    for d in range(DUOS):
                        if turn is not None or d + AHEAD < DUOS:
                            scaled(*duo_ahead(b, j, d))
                        mix.act(act, b, j, d, first)
                        if turn is not None and 1 <= d < 6:
                            prep(b + 1, 1 - j, d - 1)
                        if not (first and d == 0):
                            totals(*duo_before(b, j, d))
                act.wait_ge(fc_ready, 1)
                for s in range(5):
                    prep(0, 0, s)
                for d in range(AHEAD):
                    scaled(0, 0, d)
                over_blocks(act, body)
                totals(NB - 1, 0, DUOS - 1)
                for d in range(DUOS):
                    mix.act(act, NB, 1, d, last=True)

            @block.vector
            def _(dve):
                for s in (block_done, equal, counted, ev_ready, te_ready, ev2_ready, ev3_ready, msg_ready):
                    s.credit(dve)
                dve.wait_ge(consts, 3)
                for h in range(2):
                    s = slice(h * MUL, (h + 1) * MUL)
                    for to, of, by in ((0, 0, 0.125), (1, 2, 0.125), (2, 1, 0.125), (3, 3, 0.125 * 3 ** -0.5)):
                        m = nc.vector.tensor_scalar(fc3[s, h, to * MUL:(to + 1) * MUL], fc3r[s, of * MUL:(of + 1) * MUL], by, None, ALU.mult)
                nc.vector.tensor_copy(spare[:, :], spare_i[:, :]).then_inc(fc_ready, 1)
                dve.wait_ge(fc_ready, 1)

                def prep(b, j, step, turn):
                    if step == 0:
                        dve.wait_ge(loaded[j], turn * 64 + 64)
                        nc.vector.tensor_copy(srcf[:, j, :], srcI[:, j, :]).then_inc(src_float.sem, 1)
                    elif step in (3, 4, 5, 6):
                        q = step - 3
                        n = b * 4 + q
                        wait(dve, src_rows, n)
                        g = slice(4 * q, 4 * q + 4)
                        nc.vector.tensor_tensor(eq[:, j, g, :], pA[:, :].rearrange("p (g i) -> p g i", g=4),
                                                srcf[:, j, g].unsqueeze(2).to_broadcast([P, 4, P]), ALU.is_equal).then_inc(equal.sem, 1)
                        wait(dve, equal, n)
                        dve.wait_ge(counted.sem, counted.of(n - 1))
                        for u in range(4):
                            m = nc.vector.tensor_tensor_reduce(out=junk[:, u, :], in0=eq[:, j, 4 * q + u, :], in1=later[:, :],
                                                               scale=1.0, scalar=0.0, op0=ALU.mult, op1=ALU.add,
                                                               accum_out=cnt[:, j, 4 * q + u:4 * q + u + 1])
                        m.then_inc(counted.sem, 1)
                    elif step == 7:
                        wait(dve, counted, b * 4 + 3)
                        nc.vector.tensor_scalar(flag[:, :], cnt[:, j, :], 1000.0, None, ALU.is_ge)
                        nc.vector.tensor_tensor(away[:, :], spare[:, :].to_broadcast([P, G]), srcf[:, j, :], ALU.subtract).then_inc(flagged.sem, 1)
                        dve.wait_ge(flagged.sem, flagged.of(b * 2))
                        nc.vector.tensor_tensor(away[:, :], away[:, :], flag[:, :], ALU.mult).then_inc(flagged.sem, 1)
                        dve.wait_ge(flagged.sem, flagged.of(b * 2 + 1))
                        nc.vector.tensor_tensor(rows[:, j, :], srcf[:, j, :], away[:, :], ALU.add).then_inc(rows_ready.sem, 1)

                def messages(b, j, d):
                    n, par = duo_of(b, d), d % 2
                    s0 = (2 * d) % YSLOTS
                    for u in range(2):
                        dve.wait_ge(y_in[s0 + u].sem, y_in[s0 + u].of(b * (G // YSLOTS) + (2 * d) // YSLOTS))
                    yd = y[:, s0:s0 + 2, :]
                    es = yd[:, :, 0:MUL]
                    evd = yd[:, :, MUL:D].rearrange("p t (d u) -> p t d u", d=3)
                    shd = sh[:, j, 2 * d:2 * d + 2, 1:4].unsqueeze(3).to_broadcast([P, 2, 3, MUL])
                    ac, bd, m_ = wac[:, d % BUFS], wbd[:, d % BUFS], msg[:, d % BUFS]
                    dve.wait_ge(ev3_ready.sem, ev3_ready.of(n - 2))
                    nc.vector.tensor_tensor(ev[:, par], evd, shd, ALU.mult).then_inc(ev_ready.sem, 1)
                    wait(dve, wac_ready, n)
                    if not (isinstance(b, int) and b == 0 and d < BUFS):
                        dve.wait_ge(summed.sem, summed.of((n - BUFS) * 2 + 1))
                    nc.vector.tensor_tensor(te[:, par], bd[:, :, 0:MUL], es, ALU.mult).then_inc(te_ready.sem, 1)
                    wait(dve, ev_ready, n)
                    nc.vector.tensor_tensor(ev2[:, par], ev[:, par, :, 0, :], ev[:, par, :, 1, :], ALU.add).then_inc(ev2_ready.sem, 1)
                    nc.vector.tensor_tensor(m_[:, :, 0, 0, :], ac[:, :, 0:MUL], es, ALU.mult)
                    wait(dve, ev2_ready, n)
                    nc.vector.tensor_tensor(ev3[:, par], ev2[:, par], ev[:, par, :, 2, :], ALU.add).then_inc(ev3_ready.sem, 1)
                    nc.vector.tensor_tensor(m_[:, :, 1:4, 1, :], evd, ac[:, :, MUL:P].unsqueeze(2).to_broadcast([P, 2, 3, MUL]), ALU.mult)
                    wait(dve, te_ready, n)
                    nc.vector.tensor_tensor(m_[:, :, 1:4, 0, :], te[:, par].unsqueeze(2).to_broadcast([P, 2, 3, MUL]), shd, ALU.mult)
                    wait(dve, ev3_ready, n)
                    nc.vector.tensor_tensor(m_[:, :, 0, 1, :], bd[:, :, MUL:P], ev3[:, par], ALU.mult).then_inc(msg_ready.sem, 1)

                mix.credit_dve(dve)
                for s in range(8):
                    prep(0, 0, s, 0)
                def body(b, j, own, turn, first):
                    for d in range(DUOS):
                        messages(b, j, d)
                        if turn is not None:
                            for step in DVE_STEPS[d]:
                                prep(b + 1, 1 - j, step, turn)
                        mix.dve(dve, b, j, d, first)
                    wait(dve, msg_ready, duo_of(b, DUOS - 1))
                    dve.sem_inc(block_done.sem, 1)
                over_blocks(dve, body)
                for d in range(DUOS):
                    mix.dve(dve, NB, 1, d, last=True)

            @block.tensor
            def _(pe):
                for s in (w_done, summed):
                    s.credit(pe)
                mix.credit_pe(pe)
                pe.wait_ge(fc_ready, 1)

                def prep(b, j, step, turn):
                    if step == 0:
                        pe.wait_ge(loaded[j], turn * 64 + 64)
                        pe.wait_ge(equal.sem, equal.of(b * 4 - 1))
                        nc.tensor.transpose(pA[:, 0:P], attr[:, j, :], k.ident[:, :]).then_inc(attr_turned.sem, 1)
                    elif step in (1, 2):
                        h = step - 1
                        if h == 0:
                            wait(pe, attrT_ready, b)
                        pe.wait_ge(up_silu.sem, up_silu.of(b * 4 + h - 1))
                        for q in range(4):
                            m = nc.tensor.matmul(pH[:, q * P:(q + 1) * P], fc1[:, 4 * h + q, :], attrT[:, :], start=True, stop=True)
                        m.then_inc(up.sem, 1)
                    elif step in (3, 4):
                        h = step - 3
                        wait(pe, up_silu, b * 4 + h + 1)
                        nc.tensor.matmul(pH[:, :], fc2[:, :], h1[:, h * 512:(h + 1) * 512], start=True, stop=True).then_inc(up.sem, 1)
                    if step in (2, 3, 4, 5):
                        q = step - 2
                        if q == 0:
                            wait(pe, src_float, b)
                            wait(pe, attrT_ready, b)
                        else:
                            wait(pe, equal, b * 4 + q - 1)
                        for u in range(4):
                            m = nc.tensor.transpose(pA[:, u * P:(u + 1) * P],
                                                    srcf[:, j, 4 * q + u:4 * q + u + 1].to_broadcast([P, P]), k.ident[:, :])
                        m.then_inc(src_rows.sem, 1)

                def weights(b, j, d):
                    n = duo_of(b, d)
                    if d == 0 or d == 4:
                        wait(pe, up_silu, b * 4 + 2 + d // 4)
                    pe.wait_ge(wac_ready.sem, wac_ready.of(n - 2))
                    for u in range(2):
                        m = nc.tensor.matmul(pW[d % 2][:, u * D:(u + 1) * D], h2[:, j, d * P:(d + 1) * P], fc3[:, u, :], start=True, stop=True)
                    m.then_inc(w_done.sem, 1)

                def sums(b, j, d):
                    n = duo_of(b, d)
                    wait(pe, msg_ready, n)
                    for u in range(2):
                        tile = b * G + 2 * d + u
                        pe.wait_ge(total_ready.sem, total_ready.of(tile - 2))
                        nc.tensor.matmul(pO[u][:, :], eq[:, j, 2 * d + u, :],
                                         msg[:, d % BUFS, u].rearrange("p a b c -> p (a b c)"), start=True, stop=True).then_inc(summed.sem, 1)

                def body(b, j, own, turn, first):
                    for d in range(DUOS):
                        if turn is not None or d + AHEAD < DUOS:
                            weights(*duo_ahead(b, j, d))
                        if turn is not None and d:
                            prep(b + 1, 1 - j, d - 1, turn)
                        if not (first and d == 0):
                            sums(*duo_before(b, j, d))
                        mix.pe(pe, b, j, d, own, first)

                for s in range(8):
                    prep(0, 0, s, 0)
                for d in range(AHEAD):
                    weights(0, 0, d)
                over_blocks(pe, body)
                sums(NB - 1, 0, DUOS - 1)
                for d in range(2):
                    mix.pe(pe, NB, 1, d, 0, last=True)
        clear_semaphores(k)


class Mix:

    def __init__(self, k, c):
        self.k, nc, D = k, k.nc, k.D

        def sb(name, shape, dt=F32):
            return c.enter_context(nc.sbuf_tensor("m_" + name, shape, dt))

        def sem(name):
            return new_sem(k, c, "m_" + name)

        self.wm, self.w1, self.w2, self.g1, self.b1, self.g2, self.b2 = k.wm, k.w1, k.w2, k.g1, k.b1, k.g2, k.b2
        self.q, self.x = sb("q", [P, D]), sb("x", [P, 2, 2, P])
        self.den, self.rden, self.msgT = sb("den", [P, D]), sb("rden", [P, D]), sb("msgT", [P, 2, P])
        self.st, self.mv = sb("st", [P, 2, 6]), sb("mv", [P, 2, 2])
        self.ve, self.sd, self.rs, self.nb = sb("ve", [P, 2]), sb("sd", [P, 2]), sb("rs", [P, 2]), sb("nb", [P, 2])
        self.mlp = sb("mlp", [P, D])
        self.mn, self.mT, self.hid = sb("mn", [P, D]), sb("mT", [P, 2, P]), sb("hid", [P, 4, P])
        self.o1, self.o2 = sb("o1", [P, D]), self.den
        self.pM = [c.enter_context(nc.psum_tensor(f"m_pM{i}", [P, 512], F32)) for i in range(2)]
        self.q_in = Signal(sem("q_in"), 16)
        self.x_in = [sem("x_in0"), sem("x_in1")]
        s = lambda name, lead=0: Signal(sem(name), lead=lead)
        self.attended = s("attended", LEAD)
        self.den_eps, self.den_inv, self.msg_T = s("den_eps"), s("den_inv"), s("msg_T")
        self.projected, self.stat, self.aggr, self.var_eps = s("projected"), s("stat"), s("aggr"), s("var_eps")
        self.sqrt, self.rstd, self.shift = s("sqrt"), s("rstd"), s("shift")
        self.normed, self.turned, self.turned_ready = s("normed"), s("turned"), s("turned_ready")
        self.hidden, self.hid_ready, self.mlp_out = s("hidden", LEAD), s("hid_ready", LEAD), s("mlp_out")
        self.mlp_kept = s("mlp_kept", LEAD)
        self.out_normed, self.gained, self.acc_msg = s("out_normed", LEAD), s("gained"), s("acc_msg")
        self.acc_done = s("acc_done", LEAD)
        self.aggregates = sem("aggregates")

    def load(self, sp, n, j):
        sp.wait_ge(self.attended.sem, self.attended.of(n - 1))
        sp.dma_start(self.q[:, :], self.k.qtab[bass.ds(n, 1)].rearrange("a p d -> p (a d)")).then_inc(self.q_in.sem, 16)
        sp.wait_ge(self.hidden.sem, self.hidden.of(n * 2 - 3))
        sp.dma_start(self.x[:, j, :, :].rearrange("p a b -> p (a b)"),
                     self.k.xtab[bass.ds(n, 1)].rearrange("a p d -> p (a d)")).then_inc(self.x_in[j], 16)

    def credit_pe(self, pe):
        self.attended.credit(pe)
        self.hidden.credit(pe)

    def bank(self, j):
        return self.pM[j]

    def pe(self, pe, n, j, d, x_turn, first=False, last=False):
        nc, k, D = self.k.nc, self.k, self.k.D

        def hidden(n, j, half):
            for m_ in (2 * half, 2 * half + 1):
                for ch in range(4):
                    x = self.x[:, j, ch, :] if ch < 2 else self.mT[:, ch - 2, :]
                    m = nc.tensor.matmul(self.bank(j)[:, m_ * P:(m_ + 1) * P], self.w1[:, ch, m_ * P:(m_ + 1) * P], x,
                                         start=ch == 0, stop=ch == 3)
            m.then_inc(self.hidden.sem, 1)
        if d == 0:
            if not first:
                wait(pe, self.hid_ready, (n - 1) * 2)
                hidden(n - 1, 1 - j, 1)
                wait(pe, self.turned_ready, n - 1)
            if not last:
                wait(pe, self.q_in, n)
                for w, at in ((k.KS, 0), (k.KV, D)):
                    for ch in range(2):
                        m = nc.tensor.matmul(self.bank(j)[:, at + ch * P:at + (ch + 1) * P], w[:, ch, :], self.q[:, ch * P:(ch + 1) * P],
                                             start=True, stop=True)
                m.then_inc(self.attended.sem, 1)
        elif d == 1 and not first:
            wait(pe, self.hid_ready, (n - 1) * 2 + 1)
            for ch in range(4):
                m = nc.tensor.matmul(self.bank(1 - j)[:, 0:D], self.hid[:, ch, :], self.w2[:, ch, :], start=ch == 0, stop=ch == 3)
            m.then_inc(self.mlp_out.sem, 1)
        elif d == 2 and not last:
            wait(pe, self.msg_T, n)
            for ch in range(2):
                m = nc.tensor.matmul(self.bank(j)[:, 0:D], self.msgT[:, ch, :], self.wm[:, ch, :], start=ch == 0, stop=ch == 1)
            m.then_inc(self.projected.sem, 1)
        elif d == 6:
            wait(pe, self.normed, n)
            pe.wait_ge(self.mlp_kept.sem, self.mlp_kept.of(n - 1))
            for ch in range(2):
                m = nc.tensor.transpose(self.bank(1 - j)[:, ch * P:(ch + 1) * P], self.mn[:, ch * P:(ch + 1) * P], k.ident[:, :])
            m.then_inc(self.turned.sem, 1)
        elif d == 7:
            wait(pe, self.turned_ready, n)
            pe.wait_ge(self.x_in[j], x_turn * 16 + 16)
            hidden(n, j, 0)

    def credit_dve(self, dve):
        self.acc_done.credit(dve)

    def dve(self, dve, n, j, d, first=False, last=False):
        nc, k, D = self.k.nc, self.k, self.k.D
        which = slice(1 if last else 0, 1 if first else 2)
        if d == 1 and not last:
            pM = self.bank(j)
            wait(dve, self.attended, n)
            dve.wait_ge(self.acc_done.sem, self.acc_done.of(n - 2))
            nc.vector.tensor_scalar_add(self.den[:, :], pM[:, 0:D], ATT_EPS).then_inc(self.den_eps.sem, 1)
            wait(dve, self.den_eps, n)
            nc.vector.reciprocal(self.rden[:, :], self.den[:, :]).then_inc(self.den_inv.sem, 1)
            wait(dve, self.den_inv, n)
            nc.vector.tensor_tensor(self.msgT[:, :, :].rearrange("p a b -> p (a b)"), pM[:, D:2 * D], self.rden[:, :], ALU.mult).then_inc(self.msg_T.sem, 1)
        elif d == 3:
            if not last:
                wait(dve, self.projected, n)
                m = nc.vector.bn_stats(self.st[:, 0, :], self.bank(j)[:, 0:D])
            if not first:
                wait(dve, self.mlp_kept, n - 1)
                m = nc.vector.bn_stats(self.st[:, 1, :], self.mlp[:, :])
            m.then_inc(self.stat.sem, 1)
            wait(dve, self.stat, n)
            dve.sem_inc(self.aggregates, 1)
            for h in range(which.start, which.stop):
                m = nc.vector.bn_aggr(self.mv[:, h, :], self.st[:, h, :])
            m.then_inc(self.aggr.sem, 1)
            wait(dve, self.aggr, n)
            nc.vector.tensor_scalar_add(self.ve[:, which], self.mv[:, which, 1], LN_EPS).then_inc(self.var_eps.sem, 1)
        elif d == 5:
            wait(dve, self.sqrt, n)
            nc.vector.reciprocal(self.rs[:, which], self.sd[:, which]).then_inc(self.rstd.sem, 1)
            wait(dve, self.rstd, n)
            nc.vector.scalar_tensor_tensor(out=self.nb[:, which], in0=self.mv[:, which, 0], scalar=-1.0, in1=self.rs[:, which],
                                           op0=ALU.mult, op1=ALU.mult).then_inc(self.shift.sem, 1)
        elif d == 7 and not first:
            a = k.acc[:, bass.ds(n - 1, 1), :].rearrange("p a d -> p (a d)")
            wait(dve, self.out_normed, n - 1)
            nc.vector.tensor_tensor(a, a, self.b2[:, :], ALU.add).then_inc(self.gained.sem, 1)
            nc.vector.tensor_tensor(self.o2[:, :], self.o1[:, :], self.g2[:, :], ALU.mult).then_inc(self.acc_msg.sem, 1)
            wait(dve, self.gained, n - 1)
            wait(dve, self.acc_msg, n - 1)
            nc.vector.tensor_tensor(a, a, self.o2[:, :], ALU.add).then_inc(self.acc_done.sem, 1)

    def credit_act(self, act):
        for s in (self.out_normed, self.hid_ready, self.mlp_kept):
            s.credit(act)

    def act(self, act, n, j, d, first=False, last=False):
        nc, D = self.k.nc, self.k.D
        which = slice(1 if last else 0, 1 if first else 2)
        if d in (0, 1) and not first:
            wait(act, self.hidden, (n - 1) * 2 + d)
            nc.scalar.activation(self.hid[:, 2 * d:2 * d + 2, :].rearrange("p a b -> p (a b)"),
                                 self.bank(1 - j)[:, 256 * d:256 * d + 256], ACT.Relu).then_inc(self.hid_ready.sem, 1)
        elif d == 2 and not first:
            wait(act, self.mlp_out, n - 1)
            act.wait_ge(self.out_normed.sem, self.out_normed.of(n - 2))
            nc.scalar.copy(self.mlp[:, :], self.bank(1 - j)[:, 0:D]).then_inc(self.mlp_kept.sem, 1)
        elif d == 4:
            wait(act, self.var_eps, n)
            nc.scalar.activation(self.sd[:, which], self.ve[:, which], ACT.Sqrt).then_inc(self.sqrt.sem, 1)
        elif d == 6:
            wait(act, self.shift, n)
            if not last:
                nc.scalar.activation(self.mn[:, :], self.bank(j)[:, 0:D], ACT.Identity, scale=self.rs[:, 0:1], bias=self.nb[:, 0:1])\
                    .then_inc(self.normed.sem, 1)
            if not first:
                act.wait_ge(self.acc_done.sem, self.acc_done.of(n - 2))
                nc.scalar.activation(self.o1[:, :], self.mlp[:, :], ACT.Identity, scale=self.rs[:, 1:2], bias=self.nb[:, 1:2])\
                    .then_inc(self.out_normed.sem, 1)
        elif d == 7 and not last:
            wait(act, self.turned, n)
            for ch in range(2):
                m = nc.scalar.activation(self.mT[:, ch, :], self.bank(1 - j)[:, ch * P:(ch + 1) * P], ACT.Identity,
                                         scale=self.g1[:, ch:ch + 1], bias=self.b1[:, ch:ch + 1])
            m.then_inc(self.turned_ready.sem, 1)


def stage_gnn(k):
    nc, t, NT, D, N = k.nc, k.t, k.NT, k.D, k.N
    T = 7
    NG = NT // T
    assert NG * T == NT and NG % 2 == 1 and T % 2 == 1 and NT * P <= N + P
    with ExitStack() as c:
        def sb(name, shape, dt=F32):
            return c.enter_context(nc.sbuf_tensor("g_" + name, shape, dt))

        def bank(name):
            return c.enter_context(nc.psum_tensor("g_" + name, [P, 512], F32))

        def sem(name):
            return new_sem(k, c, "g_" + name)

        parts, sc = sb("parts", [P, 2, TABLES, T, CNT + 1]), sb("sc", [P, 2, T, D])
        count, deg, root, dn = sb("count", [P, T]), sb("deg", [P, T]), sb("root", [P, T]), sb("dn", [P, T])
        nT = sb("nT", [P, 2, 4, P])
        w2r, w2 = sb("w2r", [P, 2, MUL]), sb("w2", [P, 2, MUL])
        gain = sb("gain", [P, D])
        gv = sb("gv", [P, MUL])
        o, o2, junk = sb("o", [P, 2, T, D]), sb("o2", [P, T, D]), sb("junk", [P, T, D])
        ms, mse, rms, inv = sb("ms", [P, 2, T]), sb("mse", [P, 2, T]), sb("rms", [P, 2, T]), sb("inv", [P, 2, T])
        pT, pG = [bank("pT0"), bank("pT1")], [bank("pG0"), bank("pG1")]
        w_in, loaded, ready = sem("w_in"), [sem("loaded0"), sem("loaded1")], sem("ready")
        last_added = sem("last_added")
        sc_in = [sem("sc_in0"), sem("sc_in1")]
        s = lambda name: Signal(sem(name), lead=T + 1)
        summed, turned, turned_ready, through, with_sc = (s(x) for x in (
            "summed", "turned", "turned_ready", "through", "with_sc"))
        s = lambda name: Signal(sem(name), lead=LEAD)
        counted, degree, rooted, dn_ready, squares, eps_in, rms_ready, inv_ready, gained, added = (s(x) for x in (
            "counted", "degree", "rooted", "dn_ready", "squares", "eps_in", "rms_ready", "inv_ready", "gained", "added"))

        def groups(eng, body):
            with eng.Fori(0, NG // 2) as i:
                for j in range(2):
                    body(i * 2 + j, j, i)
            body(NG - 1, 0, NG // 2)

        with nc.Block() as block:
            @block.sync
            def _(sp):
                def load(q, j, turn):
                    sp.wait_ge(turned.sem, turned.of(q * T - (T + 1)))
                    for tab in range(TABLES):
                        sp.dma_start(parts[:, j, tab], k.tables[tab][bass.ds(q * (T * P), T * P), :]
                                     .rearrange("(t p) c -> p t c", p=P)).then_inc(loaded[j], 16)
                    sp.wait_ge(squares.sem, squares.of(q - 2))
                    sp.dma_start(sc[:, j], k.sctab[bass.ds(q * (T * P), T * P), :].rearrange("(t p) c -> p t c", p=P)).then_inc(sc_in[j], 16)
                for to, of in ((0, "L0_gnn_w2_s"), (1, "L0_gnn_w2_v")):
                    sp.dma_start(w2r[:, to, :], t[of]).then_inc(w_in, 16)
                sp.dma_start(gain[:, 0:MUL], t["L0_gnn_g_s"].partition_broadcast(P)).then_inc(w_in, 16)
                sp.dma_start(gv[:, :], t["L0_gnn_g_v"].partition_broadcast(P)).then_inc(w_in, 16)
                groups(sp, load)

            @block.gpsimd
            def _(pool):
                for x in (summed, added):
                    x.credit(pool)

                def sum_parts(q, j, turn):
                    pool.wait_ge(loaded[j], (turn + 1) * 16 * TABLES)
                    for u in range(T):
                        a = parts[:, j, 0, u, 0:CNT]
                        nc.gpsimd.tensor_tensor(a, a, parts[:, j, 1, u, 0:CNT], ALU.add).then_inc(summed.sem, 1)

                def add_acc(q):
                    wait(pool, gained, q)
                    r = k.acc[:, bass.ds(q * T, T), :]
                    nc.gpsimd.tensor_tensor(r[:, :, 0:MUL], r[:, :, 0:MUL], o2[:, :, 0:MUL], ALU.add)
                    for d in range(3):
                        v = r[:, :, MUL + d::3]
                        m = nc.gpsimd.tensor_tensor(v, v, o2[:, :, (d + 1) * MUL:(d + 2) * MUL], ALU.add)
                    m.then_inc(added.sem, 1)
                sum_parts(0, 0, 0)
                sum_parts(1, 1, 0)
                with pool.Fori(0, NG // 2 - 1) as i:
                    for j in range(2):
                        sum_parts(i * 2 + (j + 2), j, i + 1)
                        add_acc(i * 2 + j)
                sum_parts(NG - 1, 0, NG // 2)
                for q in range(NG - 3, NG - 1):
                    add_acc(q)

            @block.vector
            def _(dve):
                for x in (counted, degree, dn_ready, with_sc, squares, eps_in, inv_ready, gained):
                    x.credit(dve)
                dve.wait_ge(w_in, 64)
                nc.vector.tensor_scalar(w2[:, :, :], w2r[:, :, :], (2.0 * MUL) ** -0.5, None, ALU.mult)
                nc.vector.tensor_copy(gain[:, MUL:D].rearrange("p (d u) -> p d u", d=3),
                                      gv[:, :].unsqueeze(1).to_broadcast([P, 3, MUL])).then_inc(ready, 1)
                dve.wait_ge(ready, 1)

                def degrees(q, j, turn):
                    dve.wait_ge(loaded[j], (turn + 1) * 16 * TABLES)
                    nc.vector.tensor_tensor(count[:, :], parts[:, j, 0, :, CNT], parts[:, j, 1, :, CNT], ALU.add).then_inc(counted.sem, 1)
                    wait(dve, counted, q)
                    nc.vector.tensor_scalar_max(deg[:, :], count[:, :], 1.0).then_inc(degree.sem, 1)

                def gain_of(q, j, u, to=o2):
                    if u == 0 and to is o2:
                        dve.wait_ge(added.sem, added.of(q - 1))
                    for h, (a, b) in enumerate(((0, MUL), (MUL, D))):
                        m = nc.vector.scalar_tensor_tensor(out=to[:, u, a:b], in0=o[:, j, u, a:b], scalar=inv[:, h, u:u + 1],
                                                           in1=gain[:, a:b], op0=ALU.mult, op1=ALU.mult)
                    if u == T - 1:
                        m.then_inc(gained.sem, 1)

                def statistics(q, u):
                    if u == 0 and not (isinstance(q, int) and q == NG - 1):
                        wait(dve, added, q)
                    n = q * T + u
                    nc.vector.bn_stats(k.stats[:, bass.ds(n, 1), :].rearrange("p a d -> p (a d)"),
                                       k.acc[:, bass.ds(n, 1), :].rearrange("p a d -> p (a d)"))

                def inverses(q):
                    wait(dve, rms_ready, q)
                    nc.vector.reciprocal(inv[:, :, :], rms[:, :, :]).then_inc(inv_ready.sem, 1)
                    wait(dve, inv_ready, q)

                def body(q, j, turn, behind, ahead):
                    wait(dve, rooted, q)
                    nc.vector.reciprocal(dn[:, :], root[:, :]).then_inc(dn_ready.sem, 1)
                    wait(dve, dn_ready, q)
                    dve.wait_ge(sc_in[j], (turn + 1) * 16)
                    for u in range(T + 2):
                        if u < T:
                            wait(dve, through, q * T + u)
                            nc.vector.scalar_tensor_tensor(out=o[:, j, u, :], in0=pG[(u + j) % 2][:, 0:D], scalar=dn[:, u:u + 1], in1=sc[:, j, u, :],
                                                           op0=ALU.mult, op1=ALU.add).then_inc(with_sc.sem, 1)
                        if 0 < u <= T:
                            v = u - 1
                            wait(dve, with_sc, q * T + v)
                            for h, (a, b) in enumerate(((0, MUL), (MUL, D))):
                                m = nc.vector.tensor_tensor_reduce(out=junk[:, v, a:b], in0=o[:, j, v, a:b], in1=o[:, j, v, a:b], scale=1.0 / (b - a),
                                                                   scalar=0.0, op0=ALU.mult, op1=ALU.add, accum_out=ms[:, h, v:v + 1])
                            if u == T:
                                m.then_inc(squares.sem, 1)
                        if behind >= 1 and u == 2:
                            inverses(q - 1)
                        if behind >= 1 and u >= 2:
                            gain_of(q - 1, 1 - j, u - 2)
                        if behind >= 2 and u >= 2:
                            statistics(q - 2, u - 2)
                        if ahead and u == T - 2:
                            degrees(q + 1, 1 - j, turn + j)
                    wait(dve, squares, q)
                    nc.vector.tensor_scalar_add(mse[:, :, :], ms[:, :, :], LN_EPS).then_inc(eps_in.sem, 1)

                degrees(0, 0, 0)
                body(0, 0, 0, 0, True)
                body(1, 1, 0, 1, True)
                with dve.Fori(0, NG // 2 - 1) as i:
                    for j in range(2):
                        body(i * 2 + (2 + j), j, i + 1, 2, True)
                body(NG - 1, 0, NG // 2, 2, False)
                inverses(NG - 1)
                q = NG - 1
                for u in range(T):
                    gain_of(q, 0, u, junk)
                wait(dve, gained, q)
                r = k.acc[:, q * T:(q + 1) * T, :]
                nc.vector.tensor_tensor(r[:, :, 0:MUL], r[:, :, 0:MUL], junk[:, :, 0:MUL], ALU.add)
                for d in range(3):
                    v = r[:, :, MUL + d::3]
                    m = nc.vector.tensor_tensor(v, v, junk[:, :, (d + 1) * MUL:(d + 2) * MUL], ALU.add)
                m.then_inc(last_added, 1)
                for u in range(T):
                    statistics(q - 1, u)
                dve.wait_ge(last_added, 1)
                for u in range(T):
                    statistics(q, u)

            @block.scalar
            def _(act):
                for x in (rooted, turned_ready, rms_ready):
                    x.credit(act)

                def root_degrees(q):
                    wait(act, degree, q)
                    act.wait_ge(dn_ready.sem, dn_ready.of(q - 1))
                    nc.scalar.activation(root[:, :], deg[:, :], ACT.Sqrt).then_inc(rooted.sem, 1)

                def root_squares(q):
                    wait(act, eps_in, q)
                    nc.scalar.activation(rms[:, :, :], mse[:, :, :], ACT.Sqrt).then_inc(rms_ready.sem, 1)

                def body(q, j, turn):
                    for u in range(T):
                        n, p = q * T + u, (u + j) % 2
                        wait(act, turned, n)
                        act.wait_ge(through.sem, through.of(n - 2))
                        nc.scalar.copy(nT[:, p].rearrange("p a b -> p (a b)"), pT[p][:, :]).then_inc(turned_ready.sem, 1)
                        if u == 2 and not (isinstance(q, int) and q == 0):
                            root_squares(q - 1)
                        if u == T - 1 and not (isinstance(q, int) and q == NG - 1):
                            root_degrees(q + 1)
                root_degrees(0)
                body(0, 0, 0)
                body(1, 1, 0)
                with act.Fori(0, NG // 2 - 1) as i:
                    for j in range(2):
                        body(i * 2 + (2 + j), j, 0)
                body(NG - 1, 0, 0)
                root_squares(NG - 1)

            @block.tensor
            def _(pe):
                for x in (turned, through):
                    x.credit(pe)
                pe.wait_ge(ready, 1)

                def turn_(q, j, u):
                    n, p = q * T + u, (u + j) % 2
                    wait(pe, summed, n)
                    pe.wait_ge(turned_ready.sem, turned_ready.of(n - 2))
                    for ch in range(4):
                        m = nc.tensor.transpose(pT[p][:, ch * P:(ch + 1) * P], parts[:, j, 0, u, ch * P:(ch + 1) * P], k.ident[:, :])
                    m.then_inc(turned.sem, 1)

                def product(q, j, u):
                    n, p = q * T + u, (u + j) % 2
                    wait(pe, turned_ready, n)
                    pe.wait_ge(with_sc.sem, with_sc.of(n - 2))
                    for ch in range(4):
                        m = nc.tensor.matmul(pG[p][:, ch * MUL:(ch + 1) * MUL], nT[:, p, ch, :], w2[:, min(ch, 1), :], start=True, stop=True)
                    m.then_inc(through.sem, 1)

                def body(q, j, turn):
                    for u in range(T + 1):
                        if u < T:
                            turn_(q, j, u)
                        if u > 0:
                            product(q, j, u - 1)
                groups(pe, body)
        clear_semaphores(k)


def stage_route(k):
    nc, t, NT, D, N = k.nc, k.t, k.NT, k.D, k.N
    X, CAP = k.NEXP, k.CAP
    T = 7
    NG = NT // T
    LINKS = 16
    assert NG * T == NT and NG % 2 == 1 and T % 2 == 1
    with ExitStack() as c:
        def sb(name, shape, dt=F32):
            return c.enter_context(nc.sbuf_tensor("r_" + name, shape, dt))

        def bank(name):
            return c.enter_context(nc.psum_tensor("r_" + name, [P, 512], F32))

        def sem(name):
            return new_sem(k, c, "r_" + name)

        stats = k.stats
        mean, diff, vare, root = sb("mean", [P, NT]), sb("diff", [P, NT]), sb("vare", [P, NT]), sb("root", [P, NT])
        msum, vs, dsq = sb("msum", [P, NT]), sb("vs", [P, NT]), sb("dsq", [P, NT])
        rstd, shift = sb("rstd", [P, NT]), sb("shift", [P, NT])
        tn, ts, tT = sb("tn", [P, NT, D]), sb("ts", [P, 2, T, D]), sb("tT", [P, 2, 2, P])
        gw, gb = sb("gw", [P, 2, X]), sb("gb", [P, X])
        logits, ex, onehot = sb("logits", [P, T, X]), sb("ex", [P, T, X]), sb("onehot", [P, T, X])
        score, pos, tmp = sb("score", [P, T, X]), sb("pos", [P, T, X]), sb("tmp", [P, T, X])
        cum, tot, base = sb("cum", [P, T, X]), sb("tot", [P, T, X]), sb("base", [P, X])
        top, total, best, place = sb("top", [P, T]), sb("total", [P, T]), sb("best", [P, T]), sb("place", [P, T])
        slot, kept, over, onest = sb("slot", [P, T]), sb("kept", [P, T]), sb("over", [P, T]), sb("onest", [P, T])
        spare, valid = sb("spare", [P, NT]), sb("valid", [P, NT])
        first, start = sb("first", [P, X]), sb("start", [P, X])
        first_i, start_i, spare_i = sb("first_i", [P, X], I32), sb("start_i", [P, X], I32), sb("spare_i", [P, NT], I32)
        rows = sb("rows", [P, NT], I32)
        before = sb("before", [P, P])
        pT, pL = [bank("pT0"), bank("pT1")], [bank("pL0"), bank("pL1")]
        pC, pS = bank("pC"), bank("pS")
        w_in, set_up, masks, ln_steps, linked, rooted, ln_ready = (sem(x) for x in (
            "w_in", "set_up", "masks", "ln_steps", "linked", "rooted", "ln_ready"))
        scattered, ahead_in = sem("scattered"), sem("ahead_in")
        s = lambda name: Signal(sem(name), lead=2 * T)
        ts_ready, turned, turned_ready, gated = (s(x) for x in ("ts_ready", "turned", "turned_ready", "gated"))
        s = lambda name: Signal(sem(name), lead=LEAD)
        tn_kept, logit, centred, expd, chosen, counted, rows_ready = (s(x) for x in (
            "tn_kept", "logit", "centred", "expd", "chosen", "counted", "rows_ready"))

        def groups(eng, body):
            with eng.Fori(0, NG // 2) as i:
                for j in range(2):
                    body(i * 2 + j, j, False)
            body(NG - 1, 0, True)

        with nc.Block() as block:
            @block.sync
            def _(sp):
                for ch in range(2):
                    sp.dma_start(gw[:, ch, :], t["L0_ffn_gate_w"][ch * P:(ch + 1) * P, :]).then_inc(w_in, 16)
                sp.dma_start(gb[:, :], t["L0_ffn_gate_b"].partition_broadcast(P)).then_inc(w_in, 16)
                n = sum(load_expert_weights(k, sp, e, e, ahead_in) for e in range(2))
                sp.wait_ge(ahead_in, 16 * n)

            @block.gpsimd
            def _(pool):
                nc.gpsimd.memset(onest[:, :], 1.0)
                nc.gpsimd.memset(valid[:, :], 1.0)
                nc.gpsimd.memset(base[:, :], 0.0)
                nc.gpsimd.memset(before[:, :], 1.0)
                nc.gpsimd.iota(first_i[:, :], pattern=[[-1, X]], base=X, channel_multiplier=0)
                nc.gpsimd.iota(start_i[:, :], pattern=[[CAP, X]], base=0, channel_multiplier=0)
                nc.gpsimd.iota(spare_i[:, :], pattern=[[P, NT]], base=X * CAP, channel_multiplier=1).then_inc(set_up, 1)
                pool.wait_ge(set_up, 1)
                nc.gpsimd.affine_select(out=valid[:, :], in_=valid[:, :], compare_op=ALU.is_ge, fill=0.0,
                                        base=N - 1, pattern=[[-P, NT]], channel_multiplier=-1)
                nc.gpsimd.affine_select(out=before[:, :], in_=before[:, :], compare_op=ALU.is_ge, fill=0.0,
                                        base=-1, pattern=[[1, P]], channel_multiplier=-1).then_inc(masks, 1)
                for n in range(NT):
                    if n % T == 0:
                        wait(pool, rows_ready, n // T)
                    pool.indirect_dma_start(k.buf, bass.IndirectOffsetOnAxis(ap=rows[:, n:n + 1], axis=0), tn[:, n, :], None)\
                        .then_inc(scattered, 16)
                pool.wait_ge(scattered, 16 * NT)

            @block.vector
            def _(dve):
                n_ = [0]

                def ln_link(m):
                    n_[0] += 1
                    m.then_inc(ln_steps, 1)
                    dve.wait_ge(ln_steps, n_[0])
                for x in (tn_kept, logit, centred, chosen, rows_ready):
                    x.credit(dve)
                nc.vector.tensor_tensor(msum[:, :], stats[:, :, 1], stats[:, :, 4], ALU.add)
                nc.vector.tensor_tensor(diff[:, :], stats[:, :, 1], stats[:, :, 4], ALU.subtract)
                ln_link(nc.vector.tensor_tensor(vare[:, :], stats[:, :, 2], stats[:, :, 5], ALU.add))
                nc.vector.tensor_scalar(mean[:, :], msum[:, :], 0.5, None, ALU.mult)
                nc.vector.tensor_tensor(dsq[:, :], diff[:, :], diff[:, :], ALU.mult)
                ln_link(nc.vector.tensor_scalar(vs[:, :], vare[:, :], 1.0 / D, LN_EPS, ALU.mult, ALU.add))
                ln_link(nc.vector.scalar_tensor_tensor(out=vare[:, :], in0=dsq[:, :], scalar=0.25, in1=vs[:, :], op0=ALU.mult, op1=ALU.add))
                dve.wait_ge(rooted, 1)
                ln_link(nc.vector.reciprocal(rstd[:, :], root[:, :]))
                refine_rstd(nc, dve, rstd, vare, root, ln_steps, n_[0])
                nc.vector.scalar_tensor_tensor(out=shift[:, :], in0=mean[:, :], scalar=-1.0, in1=rstd[:, :],
                                               op0=ALU.mult, op1=ALU.mult).then_inc(ln_ready, 1)
                dve.wait_ge(set_up, 1)
                nc.vector.tensor_copy(first[:, :], first_i[:, :])
                nc.vector.tensor_copy(start[:, :], start_i[:, :])
                nc.vector.tensor_copy(spare[:, :], spare_i[:, :]).then_inc(ln_ready, 1)
                dve.wait_ge(ln_ready, 2)
                dve.wait_ge(w_in, 48)
                dve.wait_ge(masks, 1)

                def wide(a):
                    return a.unsqueeze(2).to_broadcast([P, T, X])

                def over_tiles(a):
                    return a[:, :].unsqueeze(1).to_broadcast([P, T, X])

                def flat(a):
                    return a[:, :, :].rearrange("p a b -> p (a b)")

                def body(q, j, last):
                    done = [0]

                    def link(m):
                        done[0] += 1
                        m.then_inc(linked, 1)
                        dve.wait_ge(linked, q * LINKS + done[0])
                    tiles = bass.ds(q * T, T)
                    wait(dve, ts_ready, q * T + (T - 1))
                    nc.vector.tensor_copy(tn[:, tiles, :], ts[:, j, :, :]).then_inc(tn_kept.sem, 1)
                    wait(dve, gated, q * T + (T - 1))
                    nc.vector.tensor_tensor(logits[:, :, :], pL[j][:, 0:T * X].rearrange("p (a b) -> p a b", a=T), over_tiles(gb),
                                            ALU.add).then_inc(logit.sem, 1)
                    wait(dve, logit, q)
                    link(nc.vector.tensor_reduce(out=top[:, :], in_=logits[:, :, :], op=ALU.max, axis=AX))
                    nc.vector.tensor_tensor(tmp[:, :, :], logits[:, :, :], wide(top[:, :]), ALU.subtract).then_inc(centred.sem, 1)
                    wait(dve, expd, q)
                    nc.vector.tensor_reduce(out=total[:, :], in_=ex[:, :, :], op=ALU.add, axis=AX)
                    link(nc.vector.tensor_reduce(out=top[:, :], in_=ex[:, :, :], op=ALU.max, axis=AX))
                    nc.vector.reciprocal(best[:, :], total[:, :])
                    link(nc.vector.tensor_tensor(onehot[:, :, :], ex[:, :, :], wide(top[:, :]), ALU.is_equal))
                    link(nc.vector.tensor_tensor(score[:, :, :], onehot[:, :, :], over_tiles(first), ALU.mult))
                    link(nc.vector.tensor_reduce(out=place[:, :], in_=score[:, :, :], op=ALU.max, axis=AX))
                    link(nc.vector.tensor_tensor(onehot[:, :, :], score[:, :, :], wide(place[:, :]), ALU.is_equal))
                    nc.vector.tensor_tensor(best[:, :], best[:, :], top[:, :], ALU.mult)
                    nc.vector.tensor_tensor(onehot[:, :, :], onehot[:, :, :], wide(valid[:, tiles]), ALU.mult).then_inc(chosen.sem, 1)
                    wait(dve, counted, q)
                    link(nc.vector.tensor_copy(flat(tot), pS[:, 0:T * X]))
                    for e in range(X):
                        m = nc.vector.tensor_tensor_scan(cum[:, :, e], onest[:, :], tot[:, :, e], 0.0, ALU.mult, ALU.add)
                    link(m)
                    link(nc.vector.tensor_tensor(pos[:, :, :], cum[:, :, :], tot[:, :, :], ALU.subtract))
                    link(nc.vector.tensor_tensor(flat(pos), flat(pos), pC[:, 0:T * X], ALU.add))
                    link(nc.vector.tensor_tensor(pos[:, :, :], pos[:, :, :], over_tiles(base), ALU.add))
                    nc.vector.tensor_tensor(base[:, :], base[:, :], cum[:, T - 1, :], ALU.add)
                    nc.vector.tensor_tensor(score[:, :, :], pos[:, :, :], over_tiles(start), ALU.add)
                    link(nc.vector.tensor_tensor(tmp[:, :, :], pos[:, :, :], onehot[:, :, :], ALU.mult))
                    nc.vector.tensor_reduce(out=place[:, :], in_=tmp[:, :, :], op=ALU.add, axis=AX)
                    link(nc.vector.tensor_tensor(score[:, :, :], score[:, :, :], onehot[:, :, :], ALU.mult))
                    nc.vector.tensor_reduce(out=slot[:, :], in_=score[:, :, :], op=ALU.add, axis=AX)
                    link(nc.vector.tensor_scalar(kept[:, :], place[:, :], float(CAP), None, ALU.is_lt))
                    nc.vector.tensor_scalar(over[:, :], place[:, :], float(1 - CAP), 0.0, ALU.add, ALU.max)
                    nc.vector.tensor_tensor(total[:, :], slot[:, :], spare[:, tiles], ALU.subtract)
                    link(nc.vector.tensor_tensor(kept[:, :], kept[:, :], valid[:, tiles], ALU.mult))
                    link(nc.vector.tensor_tensor(total[:, :], total[:, :], kept[:, :], ALU.mult))
                    nc.vector.tensor_tensor(k.weight[:, tiles], best[:, :], kept[:, :], ALU.mult)
                    nc.vector.tensor_tensor(k.back[:, tiles], slot[:, :], over[:, :], ALU.subtract)
                    nc.vector.tensor_tensor(rows[:, tiles], total[:, :], spare[:, tiles], ALU.add).then_inc(rows_ready.sem, 1)
                    assert done[0] == LINKS, done
                groups(dve, body)

            @block.scalar
            def _(act):
                for x in (ts_ready, turned_ready, expd):
                    x.credit(act)
                act.wait_ge(ln_steps, 3)
                nc.scalar.activation(root[:, :], vare[:, :], ACT.Sqrt).then_inc(rooted, 1)
                act.wait_ge(ln_ready, 1)

                def norm(q, j, u):
                    n = q * T + u
                    act.wait_ge(tn_kept.sem, tn_kept.of(q - 2))
                    act.wait_ge(turned.sem, turned.of(n - 2 * T))
                    nc.scalar.activation(ts[:, j, u, :], k.acc[:, bass.ds(n, 1), :].rearrange("p a d -> p (a d)"), ACT.Identity,
                                         scale=rstd[:, bass.ds(n, 1)], bias=shift[:, bass.ds(n, 1)]).then_inc(ts_ready.sem, 1)

                def exp(q):
                    wait(act, centred, q)
                    nc.scalar.activation(ex[:, :, :], tmp[:, :, :], ACT.Exp).then_inc(expd.sem, 1)

                def body(q, j, last):
                    for u in range(T):
                        n, p = q * T + u, (u + j) % 2
                        if u + 2 < T:
                            norm(q, j, u + 2)
                        elif not last:
                            norm(q + 1, 1 - j, u + 2 - T)
                        wait(act, turned, n)
                        act.wait_ge(gated.sem, gated.of(n - 2))
                        nc.scalar.copy(tT[:, p].rearrange("p a b -> p (a b)"), pT[p][:, 0:D]).then_inc(turned_ready.sem, 1)
                        if u == 2 and not (isinstance(q, int) and q == 0):
                            exp(q - 1)
                for u in range(2):
                    norm(0, 0, u)
                body(0, 0, False)
                body(1, 1, False)
                with act.Fori(0, NG // 2 - 1) as i:
                    for j in range(2):
                        body(i * 2 + (2 + j), j, False)
                body(NG - 1, 0, True)
                exp(NG - 1)

            @block.tensor
            def _(pe):
                for x in (turned, gated, counted):
                    x.credit(pe)
                pe.wait_ge(w_in, 48)
                pe.wait_ge(masks, 1)

                def counts(q):
                    wait(pe, chosen, q)
                    pe.wait_ge(rows_ready.sem, rows_ready.of(q - 1))
                    oh = onehot[:, :, :].rearrange("p a b -> p (a b)")
                    nc.tensor.matmul(pC[:, 0:T * X], before[:, :], oh, start=True, stop=True)
                    nc.tensor.matmul(pS[:, 0:T * X], k.ones[:, :], oh, start=True, stop=True).then_inc(counted.sem, 1)

                def turn(q, j, u):
                    n, p = q * T + u, (u + j) % 2
                    wait(pe, ts_ready, n)
                    pe.wait_ge(turned_ready.sem, turned_ready.of(n - 2))
                    for ch in range(2):
                        m = nc.tensor.transpose(pT[p][:, ch * P:(ch + 1) * P], ts[:, j, u, ch * P:(ch + 1) * P], k.ident[:, :])
                    m.then_inc(turned.sem, 1)

                def gate(q, j, u):
                    n, p = q * T + u, (u + j) % 2
                    wait(pe, turned_ready, n)
                    for ch in range(2):
                        m = nc.tensor.matmul(pL[j][:, u * X:(u + 1) * X], tT[:, p, ch, :], gw[:, ch, :], start=ch == 0, stop=ch == 1)
                    m.then_inc(gated.sem, 1)

                def body(q, j, last):
                    for u in range(T):
                        if u + 1 < T:
                            turn(q, j, u + 1)
                        elif not last:
                            turn(q + 1, 1 - j, 0)
                        if u == 0:
                            pe.wait_ge(logit.sem, logit.of(q - 2))
                        gate(q, j, u)
                        if u == 5 and not (isinstance(q, int) and q == 0):
                            counts(q - 1)
                turn(0, 0, 0)
                body(0, 0, False)
                body(1, 1, False)
                with pe.Fori(0, NG // 2 - 1) as i:
                    for j in range(2):
                        body(i * 2 + (2 + j), j, False)
                body(NG - 1, 0, True)
                counts(NG - 1)
        clear_semaphores(k)


def stage_experts(k):
    nc, D, FF, CAP = k.nc, k.D, k.FF, k.CAP
    M = FF // P
    R = (CAP + P - 1) // P
    RL = CAP - (R - 1) * P
    SPLIT = (CAP + 1) // 2
    halves = ((0, SPLIT), (SPLIT, CAP))
    assert R == 8 and SPLIT <= 512
    with ExitStack() as c:
        def sb(name, shape, dt=F32):
            return c.enter_context(nc.sbuf_tensor("x_" + name, shape, dt))

        def bank(name):
            return c.enter_context(nc.psum_tensor("x_" + name, [P, 512], F32))

        def sem(name):
            return new_sem(k, c, "x_" + name)

        w1, w2, b1, b2 = k.xw1, k.xw2, k.xb1, k.xb2
        xb, xT = sb("xb", [P, 2, R, D]), sb("xT", [P, 2, 2, R * P])
        hid, yo = sb("hid", [P, M, CAP]), sb("yo", [P, R, D])
        pT, pH, pY = [bank("pT0"), bank("pT1")], [bank("pH0"), bank("pH1")], [bank("pY0"), bank("pY1")]
        loaded, zeroed = [sem("loaded0"), sem("loaded1")], sem("zeroed")
        s = lambda name, unit=1: Signal(sem(name), unit, lead=LEAD)
        turned, turned_ready = s("turned"), s("turned_ready")
        hidden, hid_ready = s("hidden"), s("hid_ready")
        out, row_tile = s("out"), s("row_tile")
        out_ready = s("out_ready")
        stores = sem("stores")
        stored = s("stored")
        FIRST, LOADS = 2, 2 + 2 + 1 + M + 1
        QT = R // 2

        def experts(eng, *steps):
            with eng.Fori(0, k.NEXP // 2) as i:
                for j in range(2):
                    for step in steps:
                        step(i * 2 + j, j, i)

        with nc.Block() as block:
            @block.sync
            def _(sp):
                sp.wait_ge(zeroed, 1)

                def load_rows(e, j):
                    sp.dma_start(xb[:, j, 0:R - 1, :], k.buf[bass.ds(e * CAP, (R - 1) * P), :].rearrange("(r p) d -> p r d", p=P)).then_inc(loaded[j], 16)
                    sp.dma_start(xb[0:RL, j, R - 1, :], k.buf[bass.ds(e * CAP + (R - 1) * P, RL), :]).then_inc(loaded[j], 16)
                load_rows(0, 0)
                load_rows(1, 1)
                with sp.Fori(0, k.NEXP // 2 - 1) as i:
                    for j in range(2):
                        e = i * 2 + (j + 2)
                        sp.wait_ge(out_ready.sem, out_ready.of(e - 2))
                        load_rows(e, j)
                        load_expert_weights(k, sp, e, j, loaded[j])

            @block.gpsimd
            def _(pool):
                nc.gpsimd.memset(xb[:, :, R - 1, :], 0.0).then_inc(zeroed, 1)
                stored.credit(pool)

                def store(e, j, turn):
                    wait(pool, out_ready, e)
                    pool.dma_start(k.ybuf[bass.ds(e * CAP, (R - 1) * P), :].rearrange("(r p) d -> p r d", p=P), yo[:, 0:R - 1, :]).then_inc(stores, 16)
                    pool.dma_start(k.ybuf[bass.ds(e * CAP + (R - 1) * P, RL), :], yo[0:RL, R - 1, :]).then_inc(stores, 16)
                    pool.wait_ge(stores, (e + 1) * 32)
                    pool.sem_inc(stored.sem, 1)
                experts(pool, store)

            @block.scalar
            def _(act):
                hid_ready.credit(act)

                def hide(e, j, turn):
                    for m in range(M):
                        for h, (a, b) in enumerate(halves):
                            wait(act, hidden, e * 2 * M + 2 * m + h)
                            nc.scalar.activation(hid[:, m, a:b], pH[h][:, 0:b - a], ACT.Relu, bias=b1[:, j, m:m + 1]).then_inc(hid_ready.sem, 1)
                experts(act, hide)

            @block.vector
            def _(dve):
                for x in (turned_ready, row_tile, out_ready):
                    x.credit(dve)

                def turn(e, j, turn_):
                    for q in range(QT):
                        wait(dve, turned, e * QT + q)
                        nc.vector.tensor_copy(xT[:, j, :, 2 * q * P:(2 * q + 2) * P], pT[q % 2][:, :].rearrange("p (c r) -> p c r", c=2)).then_inc(turned_ready.sem, 1)

                def add_b2(e, j, turn_):
                    dve.wait_ge(stored.sem, stored.of(e - 1))
                    for r in range(R):
                        wait(dve, out, e * R + r)
                        nc.vector.tensor_tensor(yo[:, r, :], pY[r % 2][:, 0:D], b2[:, j, :], ALU.add).then_inc(row_tile.sem, 1)
                    wait(dve, row_tile, e * R + R - 1)
                    dve.sem_inc(out_ready.sem, 1)
                turn(0, 0, 0)
                with dve.Fori(0, k.NEXP // 2 - 1) as i:
                    for j in range(2):
                        turn(i * 2 + j + 1, 1 - j, i)
                        add_b2(i * 2 + j, j, i)
                turn(k.NEXP - 1, 1, 0)
                add_b2(k.NEXP - 2, 0, 0)
                add_b2(k.NEXP - 1, 1, 0)

            @block.tensor
            def _(pe):
                for x in (turned, hidden, out):
                    x.credit(pe)

                def turn(e, j, e_turn):
                    pe.wait_ge(loaded[j], e_turn * (16 * LOADS) + 16 * FIRST)
                    for q in range(QT):
                        pe.wait_ge(turned_ready.sem, turned_ready.of(e * QT + q - 2))
                        for ch in range(2):
                            for r in range(2):
                                m = nc.tensor.transpose(pT[q % 2][:, (2 * ch + r) * P:(2 * ch + r + 1) * P],
                                                        xb[:, j, 2 * q + r, ch * P:(ch + 1) * P], k.ident[:, :])
                        m.then_inc(turned.sem, 1)

                def up(e, j):
                    wait(pe, turned_ready, e * QT + QT - 1)
                    for m_ in range(M):
                        for h, (a, b) in enumerate(halves):
                            pe.wait_ge(hid_ready.sem, hid_ready.of(e * 2 * M + 2 * m_ + h - 2))
                            for ch in range(2):
                                m = nc.tensor.matmul(pH[h][:, 0:b - a], w1[:, j, ch, m_ * P:(m_ + 1) * P], xT[:, j, ch, a:b], start=ch == 0, stop=ch == 1)
                            m.then_inc(hidden.sem, 1)

                def down(e, j):
                    wait(pe, hid_ready, e * 2 * M + 2 * M - 1)
                    for r in range(R):
                        n = P if r < R - 1 else RL
                        pe.wait_ge(row_tile.sem, row_tile.of(e * R + r - 2))
                        for m_ in range(M):
                            m = nc.tensor.matmul(pY[r % 2][0:n, 0:D], hid[:, m_, r * P:r * P + n], w2[:, j, m_, :], start=m_ == 0, stop=m_ == M - 1)
                        m.then_inc(out.sem, 1)
                turn(0, 0, 0)
                with pe.Fori(0, k.NEXP // 2 - 1) as i:
                    for j in range(2):
                        up(i * 2 + j, j)
                        turn(i * 2 + j + 1, 1 - j, i + j)
                        down(i * 2 + j, j)
                up(k.NEXP - 2, 0)
                turn(k.NEXP - 1, 1, k.NEXP // 2 - 1)
                down(k.NEXP - 2, 0)
                up(k.NEXP - 1, 1)
                down(k.NEXP - 1, 1)
        clear_semaphores(k)


def stage_combine(k):
    nc, NT, D, N, LAST = k.nc, k.NT, k.D, k.N, k.LAST
    T = 7
    NG = NT // T
    FMAX = 3.4028234e38
    BY_POOL = 4
    with ExitStack() as c:
        def sb(name, shape, dt=F32):
            return c.enter_context(nc.sbuf_tensor("o_" + name, shape, dt))

        def sem(name):
            return new_sem(k, c, "o_" + name)

        y = sb("y", [P, NT, D])
        odd, high = sb("odd", [P, 2, T * D], I32), sb("high", [P, 2, T * D])
        sign, value = sb("sign", [P, 2, T * D]), sb("value", [P, 2, T * D])
        rows = sb("rows", [P, NT], I32)
        rows_ready = sem("rows_ready")
        got = [sem(f"got{q}") for q in range(NG)]
        s = lambda name: Signal(sem(name))
        scaled, flagged, signed, valued, finite, added_pool, added_dve = (s(x) for x in (
            "scaled", "flagged", "signed", "valued", "finite", "added_pool", "added_dve"))
        stored = sem("stored")

        def group(a, q):
            return a[:, q * T:(q + 1) * T, :].rearrange("p t d -> p (t d)")

        with nc.Block() as block:
            @block.sync
            def _(sp):
                for q in range(NG):
                    if q < BY_POOL:
                        wait(sp, added_pool, q)
                    else:
                        wait(sp, added_dve, q - BY_POOL)
                    a, b = q * T, min((q + 1) * T, NT - 1)
                    sp.dma_start(k.out[a * P:b * P, :].rearrange("(t p) d -> p t d", p=P), k.acc[:, a:b, :]).then_inc(stored, 16)
                sp.dma_start(k.out[(NT - 1) * P:N, :], k.acc[0:LAST, NT - 1, :]).then_inc(stored, 16)
                sp.wait_ge(stored, 16 * (NG + 1))

            @block.gpsimd
            def _(pool):
                pool.wait_ge(rows_ready, 1)
                for n in range(NT):
                    pool.indirect_dma_start(y[:, n, :], None, k.ybuf, bass.IndirectOffsetOnAxis(ap=rows[:, n:n + 1], axis=0)).then_inc(got[n // T], 16)
                for q in range(BY_POOL):
                    wait(pool, finite, q)
                    a = group(k.acc, q)
                    nc.gpsimd.tensor_tensor(a, a, group(y, q), ALU.add).then_inc(added_pool.sem, 1)

            @block.scalar
            def _(act):
                def give_value(q):
                    wait(act, signed, q)
                    if q >= 2:
                        wait(act, finite, q - 2)
                    nc.scalar.activation(value[:, q % 2, :], sign[:, q % 2, :], ACT.Copy, scale=-1e4).then_inc(valued.sem, 1)
                for q in range(NG):
                    act.wait_ge(got[q], 16 * T)
                    for n in range(q * T, (q + 1) * T):
                        m = nc.scalar.activation(y[:, n, :], y[:, n, :], ACT.Copy, scale=k.weight[:, n:n + 1])
                    m.then_inc(scaled.sem, 1)
                    if q:
                        give_value(q - 1)
                give_value(NG - 1)

            @block.vector
            def _(dve):
                nc.vector.tensor_copy(rows[:, :], k.back[:, :]).then_inc(rows_ready, 1)

                def flag(q):
                    v, j = group(y, q), q % 2
                    wait(dve, scaled, q)
                    if q >= 2:
                        wait(dve, valued, q - 2)
                        wait(dve, finite, q - 2)
                    nc.vector.tensor_scalar(odd[:, j, :], v, 0.0, 0.0, ALU.mult, ALU.not_equal)
                    nc.vector.tensor_scalar(high[:, j, :], v, FMAX, None, ALU.is_gt).then_inc(flagged.sem, 1)
                    wait(dve, flagged, q)
                    nc.vector.scalar_tensor_tensor(out=sign[:, j, :], in0=v, scalar=-FMAX, in1=high[:, j, :],
                                                   op0=ALU.is_lt, op1=ALU.subtract).then_inc(signed.sem, 1)

                def replace(q):
                    v, j = group(y, q), q % 2
                    wait(dve, valued, q)
                    nc.vector.copy_predicated(v, odd[:, j, :], value[:, j, :]).then_inc(finite.sem, 1)
                    if q >= BY_POOL:
                        wait(dve, finite, q)
                        a = group(k.acc, q)
                        nc.vector.tensor_tensor(a, a, v, ALU.add).then_inc(added_dve.sem, 1)
                for q in range(NG):
                    flag(q)
                    if q:
                        replace(q - 1)
                replace(NG - 1)


_INS = ['x', 'src', 'dst', 'edge_attr_4', 'edge_attr_8', 'L0_gnn_w1_s', 'L0_gnn_w1_v', 'L0_gnn_wsc_s', 'L0_gnn_wsc_v',
        'L0_gnn_w2_s', 'L0_gnn_w2_v', 'L0_gnn_fc_w1', 'L0_gnn_fc_w2', 'L0_gnn_fc_w3', 'L0_gnn_g_s', 'L0_gnn_g_v',
        'L0_mix_Wq', 'L0_mix_Wk', 'L0_mix_Wv', 'L0_mix_Wm', 'L0_mix_W1', 'L0_mix_W2', 'L0_mix_g1', 'L0_mix_b1',
        'L0_mix_g2', 'L0_mix_b2', 'L0_ffn_gate_w', 'L0_ffn_gate_b', 'L0_ffn_w1', 'L0_ffn_b1', 'L0_ffn_w2', 'L0_ffn_b2']


def kernel(**inputs):
    import numpy as _np
    import concourse.bacc as _bacc
    from concourse import mybir as _mybir
    from concourse.bass_utils import run_bass_kernel_spmd as _run

    nc = _bacc.Bacc("TRN2", target_bir_lowering=False, num_devices=1)
    arrays, aps = {}, {}
    for name in _INS:
        a = _np.ascontiguousarray(inputs[name])
        arrays[f"in_{name}"] = a
        aps[name] = nc.dram_tensor(f"in_{name}", a.shape, _mybir.dt.from_np(a.dtype), kind="ExternalInput").ap()
    out = nc.dram_tensor("out_0", inputs["x"].shape, _mybir.dt.float32, kind="ExternalOutput").ap()
    program(nc, aps, out)
    r = _run(nc, [arrays], core_ids=[0])
    return r.results[0]["out_0"]
```
